# Optimizing a Trainium2 kernel written in Bass

```python
import numpy as np
import jax
import jax.numpy as jnp

def _softmax(x, axis=-1):
    return jax.nn.softmax(x, axis=axis)

def _gelu(x):
    return jax.nn.gelu(x, approximate=True)

def _silu(x):
    return jax.nn.silu(x)

def _sigmoid(x):
    return jax.nn.sigmoid(x)

def _layernorm(x, axis=-1, eps=1e-05):
    m = jnp.mean(x, axis=axis, keepdims=True)
    v = jnp.var(x, axis=axis, keepdims=True)
    return (x - m) / jnp.sqrt(v + eps)

def _scatter_add(tgt, idx, src, axis=0):
    return tgt.at[idx].add(src)

def _segment_sum(src, seg, n):
    return jax.ops.segment_sum(src, seg, n)
kernel_name = 'mk_lm_tower_d1_tok_ids768_r4_34b917'

def setup_inputs(seed: int=0):
    np.random.seed(seed)
    _w = jnp.asarray

    def _rec_inputs():
        import jax
        import jax.numpy as jnp
        _rk = jax.random.key(seed)
        x = jax.random.randint(jax.random.fold_in(_rk, 1), (8, 1024), 0, 12564, jnp.int32)
        return x
    x = _rec_inputs()

    def _L0_tok_setup():
        import jax, jax.numpy as jnp
        import numpy as np
        BASE = 16

        def _digits(T):
            temp = np.arange(T, dtype=np.int64)
            digits = []
            while True:
                digits.append(temp % BASE)
                temp = temp // BASE
                if temp.max() == 0:
                    break
            return digits[::-1]
        key = jax.random.key(seed)
        k1, k2, k3, k4 = jax.random.split(key, 4)
        B, T, V, C = (8, 1024, 50257, 192)
        idx = jax.random.randint(k1, (B, T), 0, V, dtype=jnp.int64)
        tok_table = jax.random.normal(k2, (V, C), dtype=jnp.float32) * 0.02
        pos_table = jax.random.normal(k3, (BASE, C), dtype=jnp.float32) * 0.02
        carry_W = jax.random.normal(k4, (C, C), dtype=jnp.float32) * 0.02
        return {'idx': idx, 'tok_table': tok_table, 'pos_table': pos_table, 'carry_W': carry_W}
    _L0_tok_all = _L0_tok_setup()
    _L0_tok_in = {k: v for k, v in _L0_tok_all.items() if k in ('tok_table', 'pos_table', 'carry_W')}
    del _L0_tok_all

    def _L0_attn_setup():
        import jax, jax.numpy as jnp
        import numpy as np
        DILATIONS = [(1, 2, 4), (1, 1, 1), (4, 8, 16), (8, 16, 32), (32, 64, 128), (64, 128, 64), (64, 128, 256), (1, 100, 200), (1, 125, 250), (1, 256, 512), (3, 9, 27), (5, 25, 125)]
        MEM_HEADS = (6, 7, 8, 9)
        NUM_HEADS = 12
        HIDDEN = 192
        HEAD_DIM = HIDDEN // NUM_HEADS
        KSZ = 4
        MEM_DIM = 128
        STRIDE = 64

        def causal_dconv(h, w, b, dilation):
            pad = (KSZ - 1) * dilation
            hp = jnp.pad(h, ((0, 0), (0, 0), (pad, 0)))
            out = jax.lax.conv_general_dilated(hp, w[:, None, :], window_strides=(1,), padding='VALID', rhs_dilation=(dilation,), dimension_numbers=('NCH', 'OIH', 'NCH'), feature_group_count=h.shape[1])
            return out + b[None, :, None]

        def neural_memory(x, Wq, Wk, Wv, Wg_w, Wg_b, Wout):
            B, S, D = x.shape
            q = x @ Wq.T
            k = x @ Wk.T
            v = x @ Wv.T
            g = jax.nn.sigmoid(x @ Wg_w.T + Wg_b)
            nC = S // STRIDE
            qc = q.reshape(B, nC, STRIDE, D).transpose(1, 0, 2, 3)
            kc = k.reshape(B, nC, STRIDE, D).transpose(1, 0, 2, 3)
            vc = v.reshape(B, nC, STRIDE, MEM_DIM).transpose(1, 0, 2, 3)
            gc = g.reshape(B, nC, STRIDE, 1).transpose(1, 0, 2, 3)

            def step(M, inp):
                qi, ki, vi, gi = inp
                reads = jnp.einsum('bsd,bdm->bsm', qi, M)
                write = jnp.einsum('bsd,bsm->bdm', ki * gi, vi)
                avg_gate = gi.mean(axis=1, keepdims=True)
                return ((1.0 - avg_gate) * M + write, reads)
            M0 = jnp.zeros((B, D, MEM_DIM), x.dtype)
            _, reads = jax.lax.scan(step, M0, (qc, kc, vc, gc))
            reads = reads.transpose(1, 0, 2, 3).reshape(B, S, MEM_DIM)
            return reads @ Wout.T
        key = jax.random.key(seed)
        ks = jax.random.split(key, 17)
        B, S = (4, 1024)
        s = 0.01
        return {'x': jax.random.normal(ks[0], (B, S, HIDDEN), jnp.float32), 'conv_w': jax.random.normal(ks[1], (NUM_HEADS, 3, HEAD_DIM, KSZ), jnp.float32) * 0.1, 'conv_b': jax.random.normal(ks[2], (NUM_HEADS, 3, HEAD_DIM), jnp.float32) * 0.01, 'mem_Wq': jax.random.normal(ks[3], (4, HEAD_DIM, HEAD_DIM), jnp.float32) * s, 'mem_Wk': jax.random.normal(ks[4], (4, HEAD_DIM, HEAD_DIM), jnp.float32) * s, 'mem_Wv': jax.random.normal(ks[5], (4, MEM_DIM, HEAD_DIM), jnp.float32) * s, 'mem_Wg_w': jax.random.normal(ks[6], (4, 1, HEAD_DIM), jnp.float32) * 0.02, 'mem_Wg_b': jnp.full((4, 1), -2.0, jnp.float32), 'mem_Wout': jax.random.normal(ks[7], (4, HEAD_DIM, MEM_DIM), jnp.float32) * s, 'gate_w': jax.random.normal(ks[8], (2 * HIDDEN, HIDDEN), jnp.float32) * 0.02, 'router_w': jax.random.normal(ks[9], (NUM_HEADS, HIDDEN), jnp.float32) * 0.02, 'router_b': jnp.zeros((NUM_HEADS,), jnp.float32), 'mixg_w': jax.random.normal(ks[10], (HIDDEN, HIDDEN), jnp.float32) * 0.02, 'mixg_b': jnp.full((HIDDEN,), 2.0, jnp.float32), 'mix_w': jax.random.normal(ks[11], (HIDDEN, HIDDEN), jnp.float32) * 0.02, 'mix_b': jnp.zeros((HIDDEN,), jnp.float32)}
    _L0_attn_all = _L0_attn_setup()
    _L0_attn_in = {k: v for k, v in _L0_attn_all.items() if k in ('conv_w', 'conv_b', 'mem_Wq', 'mem_Wk', 'mem_Wv', 'mem_Wg_w', 'mem_Wg_b', 'mem_Wout', 'gate_w', 'router_w', 'router_b', 'mixg_w', 'mixg_b', 'mix_w', 'mix_b')}
    del _L0_attn_all

    def _L0_ffn_setup():
        import jax, jax.numpy as jnp
        import numpy as np
        B, S, D_IN, D_HID, D_OUT = (32, 128, 192, 768, 192)
        key = jax.random.key(seed)
        k1, k2, k3, k4 = jax.random.split(key, 4)
        init_k = float(np.sqrt(1.0 / D_IN))
        init_k2 = float(np.sqrt(1.0 / D_HID))
        x = jax.random.normal(k1, (B, S, D_IN), dtype=jnp.float32)
        in_weight = jax.random.uniform(k2, (D_HID, D_IN), dtype=jnp.float32, minval=-init_k, maxval=init_k)
        in_bias = jax.random.uniform(k3, (D_HID,), dtype=jnp.float32, minval=-init_k, maxval=init_k)
        out_weight = jax.random.uniform(k4, (D_HID, D_OUT), dtype=jnp.float32, minval=-init_k2, maxval=init_k2)
        return {'x': x, 'in_weight': in_weight, 'in_bias': in_bias, 'out_weight': out_weight}
    _L0_ffn_all = _L0_ffn_setup()
    _L0_ffn_in = {k: v for k, v in _L0_ffn_all.items() if k in ('in_weight', 'in_bias', 'out_weight')}
    del _L0_ffn_all
    return {'x': x, 'L0_tok_tok_table': _L0_tok_in['tok_table'], 'L0_tok_pos_table': _L0_tok_in['pos_table'], 'L0_tok_carry_W': _L0_tok_in['carry_W'], 'L0_attn_conv_w': _L0_attn_in['conv_w'], 'L0_attn_conv_b': _L0_attn_in['conv_b'], 'L0_attn_mem_Wq': _L0_attn_in['mem_Wq'], 'L0_attn_mem_Wk': _L0_attn_in['mem_Wk'], 'L0_attn_mem_Wv': _L0_attn_in['mem_Wv'], 'L0_attn_mem_Wg_w': _L0_attn_in['mem_Wg_w'], 'L0_attn_mem_Wg_b': _L0_attn_in['mem_Wg_b'], 'L0_attn_mem_Wout': _L0_attn_in['mem_Wout'], 'L0_attn_gate_w': _L0_attn_in['gate_w'], 'L0_attn_router_w': _L0_attn_in['router_w'], 'L0_attn_router_b': _L0_attn_in['router_b'], 'L0_attn_mixg_w': _L0_attn_in['mixg_w'], 'L0_attn_mixg_b': _L0_attn_in['mixg_b'], 'L0_attn_mix_w': _L0_attn_in['mix_w'], 'L0_attn_mix_b': _L0_attn_in['mix_b'], 'L0_ffn_in_weight': _L0_ffn_in['in_weight'], 'L0_ffn_in_bias': _L0_ffn_in['in_bias'], 'L0_ffn_out_weight': _L0_ffn_in['out_weight']}

def reference(x, L0_tok_tok_table, L0_tok_pos_table, L0_tok_carry_W, L0_attn_conv_w, L0_attn_conv_b, L0_attn_mem_Wq, L0_attn_mem_Wk, L0_attn_mem_Wv, L0_attn_mem_Wg_w, L0_attn_mem_Wg_b, L0_attn_mem_Wout, L0_attn_gate_w, L0_attn_router_w, L0_attn_router_b, L0_attn_mixg_w, L0_attn_mixg_b, L0_attn_mix_w, L0_attn_mix_b, L0_ffn_in_weight, L0_ffn_in_bias, L0_ffn_out_weight):
    import jax
    import jax.numpy as jnp

    def _L0_tok_ref(idx, tok_table, pos_table, carry_W):
        import jax, jax.numpy as jnp
        import numpy as np
        BASE = 16

        def _digits(T):
            temp = np.arange(T, dtype=np.int64)
            digits = []
            while True:
                digits.append(temp % BASE)
                temp = temp // BASE
                if temp.max() == 0:
                    break
            return digits[::-1]
        B, T = idx.shape
        C = tok_table.shape[1]
        tok_emb = tok_table[idx]
        state = jnp.zeros((T, C), dtype=tok_table.dtype)
        for d in _digits(T):
            state = state @ carry_W.T + pos_table[jnp.asarray(d)]
        pos_emb = state[::-1]
        return tok_emb + pos_emb[None, :, :]

    def _L0_attn_ref(x, conv_w, conv_b, mem_Wq, mem_Wk, mem_Wv, mem_Wg_w, mem_Wg_b, mem_Wout, gate_w, router_w, router_b, mixg_w, mixg_b, mix_w, mix_b):
        import jax, jax.numpy as jnp
        import numpy as np
        DILATIONS = [(1, 2, 4), (1, 1, 1), (4, 8, 16), (8, 16, 32), (32, 64, 128), (64, 128, 64), (64, 128, 256), (1, 100, 200), (1, 125, 250), (1, 256, 512), (3, 9, 27), (5, 25, 125)]
        MEM_HEADS = (6, 7, 8, 9)
        NUM_HEADS = 12
        HIDDEN = 192
        HEAD_DIM = HIDDEN // NUM_HEADS
        KSZ = 4
        MEM_DIM = 128
        STRIDE = 64

        def causal_dconv(h, w, b, dilation):
            pad = (KSZ - 1) * dilation
            hp = jnp.pad(h, ((0, 0), (0, 0), (pad, 0)))
            out = jax.lax.conv_general_dilated(hp, w[:, None, :], window_strides=(1,), padding='VALID', rhs_dilation=(dilation,), dimension_numbers=('NCH', 'OIH', 'NCH'), feature_group_count=h.shape[1])
            return out + b[None, :, None]

        def neural_memory(x, Wq, Wk, Wv, Wg_w, Wg_b, Wout):
            B, S, D = x.shape
            q = x @ Wq.T
            k = x @ Wk.T
            v = x @ Wv.T
            g = jax.nn.sigmoid(x @ Wg_w.T + Wg_b)
            nC = S // STRIDE
            qc = q.reshape(B, nC, STRIDE, D).transpose(1, 0, 2, 3)
            kc = k.reshape(B, nC, STRIDE, D).transpose(1, 0, 2, 3)
            vc = v.reshape(B, nC, STRIDE, MEM_DIM).transpose(1, 0, 2, 3)
            gc = g.reshape(B, nC, STRIDE, 1).transpose(1, 0, 2, 3)

            def step(M, inp):
                qi, ki, vi, gi = inp
                reads = jnp.einsum('bsd,bdm->bsm', qi, M)
                write = jnp.einsum('bsd,bsm->bdm', ki * gi, vi)
                avg_gate = gi.mean(axis=1, keepdims=True)
                return ((1.0 - avg_gate) * M + write, reads)
            M0 = jnp.zeros((B, D, MEM_DIM), x.dtype)
            _, reads = jax.lax.scan(step, M0, (qc, kc, vc, gc))
            reads = reads.transpose(1, 0, 2, 3).reshape(B, S, MEM_DIM)
            return reads @ Wout.T
        B, S, H = x.shape
        head_weights = jax.nn.sigmoid(x @ router_w.T + router_b)
        gp = x @ gate_w.T
        x_gated, gate = jnp.split(gp, 2, axis=-1)
        x_gated = x_gated * jax.nn.sigmoid(gate)
        xh = x_gated.reshape(B, S, NUM_HEADS, HEAD_DIM)
        mem_idx = {h: i for i, h in enumerate(MEM_HEADS)}
        outs = []
        for i in range(NUM_HEADS):
            h = xh[:, :, i, :].transpose(0, 2, 1)
            for j, d in enumerate(DILATIONS[i]):
                h = h + causal_dconv(h, conv_w[i, j], conv_b[i, j], d)
            h = h.transpose(0, 2, 1)
            if i in mem_idx:
                m = mem_idx[i]
                h = h + neural_memory(xh[:, :, i, :], mem_Wq[m], mem_Wk[m], mem_Wv[m], mem_Wg_w[m], mem_Wg_b[m], mem_Wout[m])
            h = h * head_weights[:, :, i:i + 1]
            outs.append(h)
        out = jnp.concatenate(outs, axis=-1)
        out = out * jax.nn.sigmoid(out @ mixg_w.T + mixg_b)
        return out @ mix_w.T + mix_b

    def _L0_ffn_ref(x, in_weight, in_bias, out_weight):
        import jax, jax.numpy as jnp
        import numpy as np
        B, S, D_IN, D_HID, D_OUT = (32, 128, 192, 768, 192)
        lead = x.shape[:-1]
        xt = x.reshape(-1, in_weight.shape[1])
        h = jax.nn.gelu(jnp.einsum('td,hd->th', xt, in_weight) + in_bias, approximate=False)
        out = jnp.einsum('th,ho->to', h, out_weight)
        return out.reshape(*lead, out_weight.shape[1])
    h = _L0_tok_ref(x, L0_tok_tok_table, L0_tok_pos_table, L0_tok_carry_W)
    h = h + _L0_attn_ref(_layernorm(h, axis=-1), L0_attn_conv_w, L0_attn_conv_b, L0_attn_mem_Wq, L0_attn_mem_Wk, L0_attn_mem_Wv, L0_attn_mem_Wg_w, L0_attn_mem_Wg_b, L0_attn_mem_Wout, L0_attn_gate_w, L0_attn_router_w, L0_attn_router_b, L0_attn_mixg_w, L0_attn_mixg_b, L0_attn_mix_w, L0_attn_mix_b)
    h = h + _L0_ffn_ref(_layernorm(h, axis=-1), L0_ffn_in_weight, L0_ffn_in_bias, L0_ffn_out_weight)
    return h

_drawn_inputs = setup_inputs


def setup_inputs(seed=0):
    import zlib

    import numpy as np

    out = dict(_drawn_inputs(seed))
    spreads = {'L0_attn_mem_Wg_b': (-2.0, 0.6),
     'L0_attn_router_b': (0.0, 0.8),
     'L0_attn_mixg_b': (2.0, 0.6),
     'L0_attn_mix_b': (0.0, 0.1)}
    factors = {'L0_attn_mem_Wq': 64.0,
     'L0_attn_mem_Wk': 64.0,
     'L0_attn_mem_Wv': 64.0,
     'L0_attn_mem_Wg_w': 64.0,
     'L0_attn_mem_Wout': 64.0,
     'L0_attn_mixg_w': 64.0,
     'L0_attn_conv_w': 3.278,
     'L0_attn_conv_b': 8.0,
     'L0_ffn_in_bias': 3.887}
    for name, (base, spread) in spreads.items():
        noise = np.random.default_rng([zlib.crc32(name.encode()), seed]).standard_normal(out[name].shape)
        drawn = base * np.exp(spread * noise) if base else spread * noise
        out[name] = jnp.asarray(drawn.astype(out[name].dtype))
    for name, factor in factors.items():
        out[name] = (out[name] * factor).astype(out[name].dtype)
    return out
```

```python
from contextlib import ExitStack

import concourse.bass as bass
from concourse import mybir

F32 = mybir.dt.float32
F32R = mybir.dt.float32r
I32 = mybir.dt.int32
U32 = mybir.dt.uint32
ALU = mybir.AluOpType
ACT = mybir.ActivationFunctionType

P = 128
C = 192
C2 = C - P
B, T = 8, 1024
HALF = 512
NG = B * T // HALF
NJ = HALF // P
HD = 16
NH = 12
HID = 768
NC = HID // P
CH = 64
EPS = 1e-5
TAPS = 4
DILATIONS = [(1, 2, 4), (1, 1, 1), (4, 8, 16), (8, 16, 32), (32, 64, 128), (64, 128, 64),
             (64, 128, 256), (1, 100, 200), (1, 125, 250), (1, 256, 512), (3, 9, 27), (5, 25, 125)]
MEM_HEADS = (6, 7, 8, 9)
ORDER = [h for h in range(NH) if h not in MEM_HEADS] + list(MEM_HEADS)
FIRST_MEM = NH - len(MEM_HEADS)
NM = len(MEM_HEADS)
TRI = 3
NT = NH // TRI
GW = 2 * C + NH


def history(place, stage):
    return min(HALF, (TAPS - 1) * DILATIONS[ORDER[place]][stage])


def tap_range(half, shift):
    lo = HALF + shift if half == 0 else max(HALF, shift)
    return (lo, 2 * HALF), (lo - shift, 2 * HALF - shift)


def lm_tower(nc, x, tok, posT, pos_tab, carryT, conv, memq, memk, memv, memo, memg, membg,
             gateT, router_b, mixgT, mixg_b, mixT, mix_b, finT, fin_b, fout, digits, ident, mask, out):
    with ExitStack() as ctx:
        def sb(name, shape, dt=F32):
            return ctx.enter_context(nc.sbuf_tensor(name, shape, dt))

        def sem(name):
            return ctx.enter_context(nc.semaphore(name))

        def scratch(name, shape):
            return nc.dram_tensor(name, shape, F32, kind="Internal").ap()

        bank = [ctx.enter_context(nc.psum_tensor(f"bank{i}", [P, 512], F32)) for i in range(8)]

        h_dram = scratch("h_dram", (NG, P, NJ * C))
        x_dram = scratch("x_dram", (B, C, T))
        hw_dram = scratch("hw_dram", (NH, B, T))
        y_dram = scratch("y_dram", (B, C2, T))
        o_dram = scratch("o_dram", (B, C, T))
        tail_dram = [scratch(f"tail{s}_dram", (NH, P, HALF)) for s in range(2)]

        id_sb = sb("id_sb", [P, P])
        mask_sb = sb("mask_sb", [C2, C2])
        zero_st = sb("zero_st", [C2, C2])
        xi = sb("xi", [B * T // P, P], I32)
        xf = sb("xf", [B * T // P, P])
        idx = sb("idx", [P, B * T // P], I32)
        pos = sb("pos", [P, T // P, C])
        gate_h, gate_l = sb("gate_h", [P, GW], F32R), sb("gate_l", [P, GW], F32R)
        gate2_h, gate2_l = sb("gate2_h", [P, GW], F32R), sb("gate2_l", [P, GW], F32R)
        mixg_h, mixg_l = sb("mixg_h", [P, C], F32R), sb("mixg_l", [P, C], F32R)
        mixg2_h, mixg2_l = sb("mixg2_h", [P, C], F32R), sb("mixg2_l", [P, C], F32R)
        mix_h, mix_l = sb("mix_h", [P, C], F32R), sb("mix_l", [P, C], F32R)
        mix2_h, mix2_l = sb("mix2_h", [P, C], F32R), sb("mix2_l", [P, C], F32R)
        fin_h, fin_l = sb("fin_h", [P, HID], F32R), sb("fin_l", [P, HID], F32R)
        fin2_h, fin2_l = sb("fin2_h", [P, HID], F32R), sb("fin2_l", [P, HID], F32R)
        fout_h, fout_l = sb("fout_h", [P, NC, C], F32R), sb("fout_l", [P, NC, C], F32R)
        conv_sb = sb("conv_sb", [P, NH * 3 * (TAPS + 1)])
        conv_w = conv_sb[:, 0:NH * 3 * TAPS].rearrange("p (h s k) -> p h s k", h=NH, s=3)
        conv_b = conv_sb[:, NH * 3 * TAPS:].rearrange("p (h s) -> p h s", h=NH)
        conv_w3 = sb("conv_w3", [P, NH, 3])
        mem_rhs = sb("mem_rhs", [C2 + 1, 3 * C2])
        router_bh = sb("router_bh", [NH, 1])
        mixg_bh, mixg_bh2 = sb("mixg_bh", [P, 1]), sb("mixg_bh2", [C2, 1])
        mix_b_sb = sb("mix_b_sb", [P, C])
        fin_b_sb = sb("fin_b_sb", [P, NC])
        warm = sb("warm", [P, 1])

        win = [sb(f"win{s}", [P, TRI, 2 * HALF]) for s in range(3)]
        heads = sb("heads", [P, TRI, HALF])
        hw_in = sb("hw_in", [P, TRI, HALF])
        y_in = sb("y_in", [P, TRI, HALF])

        res = sb("res", [P, 2, NJ, C])
        stats = sb("stats", [P, 2, NJ, 6])
        lnt = sb("lnt", [P, 2, 4, NJ])
        mean = sb("mean", [P, 2, NJ])
        var = sb("var", [P, 2, NJ])
        rstd = sb("rstd", [P, 2, NJ])
        half_neg = sb("half_neg", [P, NJ])
        nrm = sb("nrm", [P, NJ, C])
        n_hi = sb("n_hi", [P, 2, HALF], F32R)
        n_lo = sb("n_lo", [P, 2, HALF], F32R)
        n_2 = sb("n_2", [P, 2, HALF], F32R)
        big1 = sb("big1", [P, 2, HALF])
        big2 = sb("big2", [C2 + 1, 2, HALF])
        tg1, tg2 = sb("tg1", [P, HALF]), sb("tg2", [C2, HALF])
        hw_row = sb("hw_row", [NH, 2, HALF])
        mem_l = sb("mem_l", [P, NJ, P])
        mem_r = sb("mem_r", [P, NJ, C2 + 1])
        dec = sb("dec", [C2, 2, 8])
        st = sb("st", [C2, 7, C2])
        st_end = sb("st_end", [C2, C2])
        st_mid = sb("st_mid", [C2, B, C2])
        st_bd = sb("st_bd", [C2, 8, C2])
        y_sb = sb("y_sb", [C2, 2, HALF])
        o_hi, o_lo, o_2 = sb("o_hi", [P, HALF], F32R), sb("o_lo", [P, HALF], F32R), sb("o_2", [P, HALF], F32R)
        q1, q2 = sb("q1", [P, HALF]), sb("q2", [C2, HALF])
        q_hi, q_lo, q_2 = sb("q_hi", [P, HALF], F32R), sb("q_lo", [P, HALF], F32R), sb("q_2", [P, HALF], F32R)
        h2 = sb("h2", [P, 2, NJ, C])
        hid = sb("hid", [P, 2, HALF])
        hid_hi, hid_lo = sb("hid_hi", [P, 3, HALF], F32R), sb("hid_lo", [P, 3, HALF], F32R)
        raw1 = win[0][:, :, :].rearrange("p a b -> p (a b)")
        raw2 = win[1][:, :, :].rearrange("p a b -> p (a b)")
        small = win[2][:, :, :].rearrange("p a b -> p (a b)")

        names = """ld_idx ld_small ld_membg ld_gate ld_mixg ld_mix ld_fin ld_fout ld_conv ld_bias
            idx_f idx_t idx_ready pos_qt pos_qs pos_q pos_tab_ready pos_mm pos_ready mem_w_mm mem_w_ready consts gate_ready
            w_half w_hi weights_ready pool_consts
            h_ready stats_done halves_done aggr_done var_ready rstd_ready n_ready nT_ready nT_hi n_split
            gate_mm tanh_done hw_half x_ready mem_mm mem_act gx_ready G_ready dec_ready step_done masked y_mm y_ready
            gathered0 gathered1 h_stored0 h_stored1 x_stored0 x_stored1 y_stored0 y_stored1
            x0_loaded hy_loaded conv_init taps_done tail0_saved tail1_saved tail0_loaded tail1_loaded o_stored
            o_loaded0 o_loaded1 r_loaded0 r_loaded1 o_hi_ready o_lo_ready mixg_mm tg_ready q_ready q_hi_ready q_lo_ready
            res_biased mix_mm h2_ready in_mm gelu_done hid_hi_ready hid_lo_ready out_mm out_ready out_stored0 out_stored1""".split()
        S = {n: sem(n) for n in names}
        gathered, h_stored, x_stored, y_stored = ([S[f"{n}{p}"] for p in range(2)] for n in
                                                  ("gathered", "h_stored", "x_stored", "y_stored"))
        o_loaded, r_loaded, out_stored = ([S[f"{n}{p}"] for p in range(2)] for n in
                                          ("o_loaded", "r_loaded", "out_stored"))
        tail_saved = [S["tail0_saved"], S["tail1_saved"]]
        tail_loaded = [S["tail0_loaded"], S["tail1_loaded"]]

        spans, at1, at2 = {}, 0, 0
        for name, n1, n2 in (("gate", GW, GW), ("mixg", C, C), ("mix", C, C), ("fin", HID, HID), ("fout", NC * C, 0)):
            spans[name] = (raw1[:, at1:at1 + n1], raw2[:, at2:at2 + n2])
            at1, at2 = at1 + n1, at2 + n2
        assert at1 <= TRI * 2 * HALF and at2 <= TRI * 2 * HALF

        cols, at = {}, 0
        for name, n in (("carry1", C), ("carry2", C), ("posT1", HD), ("posT2", HD), ("qT1", HD), ("qT2", HD),
                        ("memk", C2), ("memq", C2), ("memv", C2), ("memo", C2), ("memg", 1), ("digits", 0), ("tabs", 3 * C)):
            cols[name] = slice(at, at + n)
            at += n
        digit_sb = heads[0:HD, :, :].rearrange("p a b -> p (a b)")
        digit0_sb = hw_in[0:HD, 0:2, :].rearrange("p a b -> p (a b)")
        digit2_sb = y_in[0:HD, 0:2, :].rearrange("p a b -> p (a b)")
        digit1_sb = digit_sb[:, 0:T]

        taps_at, init_at, hy_at = {}, {}, {}
        n_taps = n_init = n_hy = 0
        for half in range(2):
            for t in range(NT):
                n_hy += 16 * TRI
                n_hy += 16 * sum(t * TRI + s >= FIRST_MEM for s in range(TRI))
                hy_at[half, t] = n_hy
                for stage in range(3):
                    for s in range(TRI):
                        n_init += 1
                        init_at[half, t, stage, s] = n_init
                    ops = []
                    for k in range(1, TAPS):
                        for s in range(TRI):
                            shift = k * DILATIONS[ORDER[t * TRI + s]][stage]
                            (lo, hi), _ = tap_range(half, shift)
                            if lo < hi:
                                ops.append((s, "tap", k))
                    if stage == 2:
                        ops += [(s, "y", 0) for s in range(TRI) if t * TRI + s >= FIRST_MEM]
                        ops += [(s, "hw", 0) for s in range(TRI)]
                    for s, what, k in ops:
                        n_taps += 1
                        taps_at[half, t, stage, s, what, k] = n_taps
                        taps_at[half, t, stage, s] = n_taps
                    taps_at[half, t, stage] = n_taps

        def before(half, t):
            n = half * NT + t - 1
            return None if n < 0 else (n // NT, n % NT)

        def view(ap, name, rows=P):
            return ap[0:rows, cols[name]]

        def bank_jc(i):
            return bank[i][:, 0:2 * C].rearrange("p (j c) -> p j c", j=2)

        def bank_g(i):
            return bank[i][:, 0:4 * (C2 + 1)].rearrange("p (c n) -> p c n", c=4)

        block = ctx.enter_context(nc.Block())

        @block.sync
        def _(sp):
            sp.dma_start(xi[:, :], x.rearrange("b (r p) -> (b r) p", p=P)).then_inc(S["ld_idx"], 16)
            sp.dma_start(id_sb[:, :], ident).then_inc(S["ld_idx"], 16)
            for dst, src in ((view(small, "carry1"), carryT[0:P, :]), (view(small, "carry2", C2), carryT[P:C, :]),
                             (view(small, "posT1"), posT[0:P, :]), (view(small, "posT2", C2), posT[P:C, :]),
                             (view(small, "tabs", HD)[:, 2 * C:3 * C], pos_tab),
                             (digit2_sb, digits[0]), (digit1_sb, digits[1]), (digit0_sb, digits[2]),
                             (view(small, "memk", HD), memk), (view(small, "memq", HD), memq),
                             (view(small, "memv"), memv), (view(small, "memo"), memo),
                             (view(small, "memg", C2), memg), (mask_sb[:, :], mask)):
                sp.dma_start(dst, src).then_inc(S["ld_small"], 16)
            sp.wait_ge(S["consts"], 3)
            sp.dma_start(mem_rhs[C2:C2 + 1, 2 * C2:3 * C2], membg).then_inc(S["ld_membg"], 16)
            for dst, src in ((router_bh[:, :], router_b), (mixg_bh[:, :], mixg_b[0:P, :]), (mixg_bh2[:, :], mixg_b[P:C, :]),
                             (mix_b_sb[:, :], mix_b.partition_broadcast(P)), (fin_b_sb[:, :], fin_b),
                             ):
                sp.dma_start(dst, src).then_inc(S["ld_bias"], 16)
            for name, src in (("gate", gateT), ("mixg", mixgT), ("mix", mixT), ("fin", finT)):
                first, second = spans[name]
                sp.dma_start(first, src[0:P, :]).then_inc(S[f"ld_{name}"], 16)
                sp.dma_start(second[0:C2, :], src[P:C, :]).then_inc(S[f"ld_{name}"], 16)
                sp.dma_start(second[C2:P, :], src[P:C, :]).then_inc(S[f"ld_{name}"], 16)
            sp.dma_start(spans["fout"][0].rearrange("p (k c) -> p k c", k=NC),
                         fout.rearrange("(k p) c -> p k c", p=P)).then_inc(S["ld_fout"], 16)
            for b in range(B):
                sp.dma_start(conv_sb[b * HD:(b + 1) * HD, :], conv).then_inc(S["ld_conv"], 16)

            def store_h(g, p):
                sp.wait_ge(S["h_ready"], g + 1)
                sp.dma_start(h_dram[g], res[:, p, :, :].rearrange("p j c -> p (j c)")).then_inc(h_stored[p], 16)

            def store_x(g, p, b, half):
                span = slice(half * HALF, (half + 1) * HALF)
                sp.wait_ge(S["x_ready"], 2 * (g + 1))
                sp.dma_start(x_dram[b, 0:P, span], big1[:, p, :]).then_inc(x_stored[p], 16)
                sp.dma_start(x_dram[b, P:C, span], big2[0:C2, p, :]).then_inc(x_stored[p], 16)
                sp.wait_ge(S["hw_half"], g + 1)
                sp.dma_start(hw_dram[:, b, span], hw_row[:, p, :]).then_inc(x_stored[p], 16)

            def store_y(g, p, b, half):
                sp.wait_ge(S["y_ready"], g + 1)
                sp.dma_start(y_dram[b, :, half * HALF:(half + 1) * HALF], y_sb[:, p, :]).then_inc(y_stored[p], 16)

            def load_x0(half, t):
                prev = before(half, t)
                for p in range(2):
                    sp.wait_ge(x_stored[p], 48 * 4 * (half + 1))
                if prev:
                    sp.wait_ge(S["taps_done"], taps_at[(*prev, 0)])
                for s in range(TRI):
                    place = t * TRI + s
                    lo = HALF if half == 0 else HALF - history(place, 0)
                    at = lo - HALF * (1 - half)
                    sp.dma_start(win[0][:, s, lo:2 * HALF],
                                 x_dram[:, place * HD:(place + 1) * HD, at:HALF * (half + 1)]).then_inc(S["x0_loaded"], 16)

            def load_hy(half, t):
                prev = before(half, t)
                if prev:
                    sp.wait_ge(S["taps_done"], taps_at[(*prev, 2)])
                span = slice(half * HALF, (half + 1) * HALF)
                for s in range(TRI):
                    place = t * TRI + s
                    sp.dma_start(hw_in[:, s, :],
                                 hw_dram[place, :, span].rearrange("b (o t) -> b o t", o=1).to_broadcast((B, HD, HALF))
                                 ).then_inc(S["hy_loaded"], 16)
                    if place >= FIRST_MEM:
                        m = place - FIRST_MEM
                        for p in range(2):
                            sp.wait_ge(y_stored[p], 16 * 4 * (half + 1))
                        sp.dma_start(y_in[:, s, :], y_dram[:, m * HD:(m + 1) * HD, span]).then_inc(S["hy_loaded"], 16)

            def save_tail(half, t, stage):
                sp.wait_ge(S["taps_done"], taps_at[half, t, stage])
                for s in range(TRI):
                    place = t * TRI + s
                    n = history(place, stage + 1)
                    sp.dma_start(tail_dram[stage][place, :, HALF - n:HALF],
                                 win[stage + 1][:, s, 2 * HALF - n:2 * HALF]).then_inc(tail_saved[stage], 16)

            def load_tail(t, stage):
                prev = before(1, t)
                sp.wait_ge(tail_saved[stage], 16 * NH)
                sp.wait_ge(S["taps_done"], taps_at[(*prev, stage + 1)])
                for s in range(TRI):
                    place = t * TRI + s
                    n = history(place, stage + 1)
                    sp.dma_start(win[stage + 1][:, s, HALF - n:HALF],
                                 tail_dram[stage][place, :, HALF - n:HALF]).then_inc(tail_loaded[stage], 16)

            def store_heads(half, t):
                sp.wait_ge(S["taps_done"], taps_at[half, t, 2])
                for s in range(TRI):
                    place = t * TRI + s
                    sp.dma_start(o_dram[:, place * HD:(place + 1) * HD, half * HALF:(half + 1) * HALF],
                                 heads[:, s, :]).then_inc(S["o_stored"], 16)

            def after_unit(half, t, stage):
                more = t + 1 < NT
                if stage < 2 and half == 0:
                    save_tail(half, t, stage)
                if stage == 0 and more:
                    load_x0(half, t + 1)
                if stage == 1 and half == 1 and more:
                    load_tail(t + 1, 0)
                if stage == 2:
                    store_heads(half, t)
                    if more:
                        load_hy(half, t + 1)
                        if half == 1:
                            load_tail(t + 1, 1)

            def after_units(g, slots):
                for slot in slots:
                    for part in parts_in(g, slot):
                        if is_last(*part):
                            after_unit(*part[:3])

            def load_group(g, p, b, half):
                if not isinstance(g, int) or g >= 2:
                    sp.wait_ge(S["q_ready"], 2 * (g - 1))
                    sp.wait_ge(S["o_lo_ready"], 2 * (g - 1))
                    sp.wait_ge(S["h2_ready"], g - 1)
                span = slice(half * HALF, (half + 1) * HALF)
                sp.dma_start(big1[:, p, :], o_dram[b, 0:P, span]).then_inc(o_loaded[p], 16)
                sp.dma_start(big2[0:C2, p, :], o_dram[b, P:C, span]).then_inc(o_loaded[p], 16)
                sp.dma_start(res[:, p, :, :].rearrange("p j c -> p (j c)"), h_dram[g]).then_inc(r_loaded[p], 16)

            def store_out(g, p, b, half):
                sp.wait_ge(S["out_ready"], g + 1)
                sp.dma_start(out[b, half * HALF:(half + 1) * HALF, :].rearrange("(j p) c -> p j c", p=P),
                             h2[:, p, :, :]).then_inc(out_stored[p], 16)

            store_h(0, 0)
            store_h(1, 1)
            for g in (0, 1):
                store_x(g, g % 2, g, 0)
                if g:
                    store_y(g - 1, (g - 1) % 2, g - 1, 0)
                store_h(g + 2, g % 2)
            with sp.Fori(1, 4) as i:
                for k in range(2):
                    g = 2 * i + k
                    store_x(g, k, g, 0)
                    store_y(g - 1, 1 - k, g - 1, 0)
                    store_h(g + 2, k)
            load_x0(0, 0)
            for g in range(B, NG):
                store_x(g, g % 2, g - B, 1)
                store_y(g - 1, (g - 1) % 2, (g - 1) % B, (g - 1) // B)
                if g + 2 < NG:
                    store_h(g + 2, g % 2)
                if g == B:
                    load_hy(0, 0)
                after_units(g, range(4))
            store_y(NG - 1, (NG - 1) % 2, B - 1, 1)
            load_x0(1, 0)
            load_tail(0, 0)
            load_hy(1, 0)
            load_tail(0, 1)
            sp.wait_ge(S["o_stored"], 16 * NH)
            for p in range(2):
                sp.wait_ge(h_stored[p], 16 * NG // 2)
            load_group(0, 0, 0, 0)
            load_group(1, 1, 1, 0)
            for part in PARTS[1][:LEAD]:
                if is_last(*part):
                    after_unit(*part[:3])
            for g in range(B):
                after_units(NG + g, range(3))
                if g == B - 2:
                    sp.wait_ge(S["o_stored"], 2 * 16 * NH)
                load_group(g + 2, g % 2, (g + 2) % B, (g + 2) // B)
                after_units(NG + g, range(3, NC))
                store_out(g, g % 2, g, 0)
            with sp.Fori(B // 2, NG // 2 - 1) as i:
                for k in range(2):
                    g = 2 * i + k
                    load_group(g + 2, k, g + 2 - B, 1)
                    store_out(g, k, g - B, 1)
            for g in (NG - 2, NG - 1):
                store_out(g, g % 2, g - B, 1)
            for p in range(2):
                sp.wait_ge(out_stored[p], 16 * NG // 2)

        @block.gpsimd
        def _(pool):
            nc.gpsimd.memset(half_neg[:, :], -0.5).then_inc(S["pool_consts"], 1)

            def gather(g):
                p = g % 2
                if g >= 2:
                    pool.wait_ge(S["n_ready"], g - 1)
                    pool.wait_ge(h_stored[p], 16 * (g // 2))
                half, b = g // B, g % B
                for j in range(NJ):
                    row = (b * T + half * HALF) // P + j
                    nc.gpsimd.indirect_dma_start(
                        out=res[:, p, j, :], out_offset=None, in_=tok,
                        in_offset=bass.IndirectOffsetOnAxis(ap=idx[:, row:row + 1], axis=0)).then_inc(gathered[p], 16)

            def power(k, p):
                pool.wait_ge(S["var_ready"], k + 1)
                nc.gpsimd.tensor_tensor(rstd[:, p, :], var[:, p, :], half_neg[:, :], ALU.pow).then_inc(S["rstd_ready"], 1)

            pool.wait_ge(S["idx_ready"], 1)
            gather(0)
            gather(1)
            pool.wait_ge(S["pool_consts"], 1)
            power(0, 0)
            gather(2)

            def masks(g):
                if g == 0:
                    pool.wait_ge(S["ld_small"], 16 * 14)
                pool.wait_ge(S["step_done"], 8 * g + 7)
                if g:
                    pool.wait_ge(S["y_mm"], g)
                first = zero_st[:, :] if g < B else st_mid[:, g - B, :]
                nc.gpsimd.tensor_tensor(st_bd[:, 0, :], first, mask_sb[:, :], ALU.mult).then_inc(S["masked"], 1)
                nc.gpsimd.tensor_tensor(st_bd[:, 1:8, :], st[:, :, :],
                                        mask_sb[:, :].rearrange("p (o c) -> p o c", o=1).to_broadcast((C2, 7, C2)),
                                        ALU.mult).then_inc(S["masked"], 1)

            for g in range(NG):
                if g + 1 < NG:
                    power(g + 1, (g + 1) % 2)
                if g:
                    masks(g - 1)
                if g + 3 < NG:
                    gather(g + 3)
            masks(NG - 1)

            def low_parts(g, p):
                pool.wait_ge(S["o_hi_ready"], 2 * g + 1)
                nc.gpsimd.tensor_tensor(o_lo[:, :], big1[:, p, :], o_hi[:, :].bitcast(F32), ALU.subtract).then_inc(S["o_lo_ready"], 1)
                pool.wait_ge(S["o_hi_ready"], 2 * g + 2)
                pool.wait_ge(S["o_lo_ready"], 2 * g + 1)
                nc.gpsimd.tensor_tensor(o_2[C2:P, :], big2[0:C2, p, :], o_2[0:C2, :].bitcast(F32), ALU.subtract).then_inc(S["o_lo_ready"], 1)
                pool.wait_ge(r_loaded[p], 16 * (g // 2 + 1) if isinstance(g, int) else 8 * (g - p) + 16)
                pool.wait_ge(S["o_lo_ready"], 2 * g + 2)
                nc.gpsimd.tensor_tensor(res[:, p, :, :], res[:, p, :, :],
                                        mix_b_sb[:, :].rearrange("p (o c) -> p o c", o=1).to_broadcast((P, NJ, C)),
                                        ALU.add).then_inc(S["res_biased"], 1)
                pool.wait_ge(S["q_hi_ready"], 2 * g + 1)
                nc.gpsimd.tensor_tensor(q_lo[:, :], q1[:, :], q_hi[:, :].bitcast(F32), ALU.subtract).then_inc(S["q_lo_ready"], 1)
                pool.wait_ge(S["q_hi_ready"], 2 * g + 2)
                pool.wait_ge(S["q_lo_ready"], 2 * g + 1)
                nc.gpsimd.tensor_tensor(q_2[C2:P, :], q2[:, :], q_2[0:C2, :].bitcast(F32), ALU.subtract).then_inc(S["q_lo_ready"], 1)
                pool.wait_ge(S["q_lo_ready"], 2 * g + 2)
                power(NG + g, p)

            pool.wait_ge(S["ld_bias"], 16 * 5)
            with pool.Fori(0, NG // 2) as i:
                for k in range(2):
                    low_parts(2 * i + k, k)

        @block.scalar
        def _(act):

            act.wait_ge(S["pool_consts"], 1)
            nc.scalar.activation(warm[:, :], half_neg[:, 0:1], ACT.Gelu)
            act.wait_ge(S["pos_mm"], 1)
            for k in range(4):
                nc.scalar.copy(pos[:, 2 * k:2 * k + 2, :], bank_jc(4 + k)).then_inc(S["pos_ready"], 1)

            def high_n(g, p, second=False):
                act.wait_ge(S["nT_ready"], (NG if second else 0) + g + 1)
                if not isinstance(g, int) or g >= 2:
                    if second:
                        act.wait_ge(S["in_mm"], NC * (g - 1))
                    else:
                        act.wait_ge(S["gate_mm"], 4 * (g - 1))
                nc.scalar.copy(n_hi[:, p, :], bank[0][:, :]).then_inc(S["nT_hi"], 1)
                nc.scalar.copy(n_2[0:C2, p, :], bank[1][0:C2, :]).then_inc(S["nT_hi"], 1)

            def gates(g, p, first=False):
                act.wait_ge(S["gate_mm"], 4 * g + 1)
                if not first:
                    act.wait_ge(S["x_ready"], 2 * g)
                nc.scalar.activation(tg2[:, :], bank[4][C2:P, :], ACT.Tanh, scale=0.5).then_inc(S["tanh_done"], 1)
                act.wait_ge(S["gate_mm"], 4 * g + 3)
                nc.scalar.activation(tg1[:, :], bank[3][:, :], ACT.Tanh, scale=0.5).then_inc(S["tanh_done"], 1)
                act.wait_ge(S["gate_mm"], 4 * g + 4)
                act.wait_ge(S["w_half"], 2)
                if not (isinstance(g, int) and g < 2):
                    act.wait_ge(x_stored[p], 24 * (g - p))
                nc.scalar.activation(hw_row[:, p, :], bank[5][0:NH, :], ACT.Tanh, bias=router_bh[:, :], scale=0.5).then_inc(S["tanh_done"], 1)

            def read_y(g, p):
                act.wait_ge(S["y_mm"], g + 1)
                if not (isinstance(g, int) and g < 2):
                    act.wait_ge(y_stored[p], 8 * (g - p))
                nc.scalar.copy(y_sb[:, p, :], bank[1][C2:P, :]).then_inc(S["y_ready"], 1)

            def memory_rows(g, first=False):
                if not first:
                    act.wait_ge(S["G_ready"], g)
                for half in range(2):
                    act.wait_ge(S["mem_mm"], 2 * g + half + 1)
                    tiles = slice(2 * half, 2 * half + 2)
                    nc.scalar.activation(mem_l[:, tiles, C2:P], bank_jc(6 + half)[:, :, 2 * C2:3 * C2], ACT.Tanh, scale=0.5).then_inc(S["mem_act"], 1)
                    nc.scalar.copy(mem_r[:, tiles, 0:C2], bank_jc(6 + half)[:, :, C2:2 * C2]).then_inc(S["mem_act"], 1)

            def start_unit(half, t, stage):
                prev = before(half, t)
                if stage == 0:
                    act.wait_ge(S["x0_loaded"], 48 * (half * NT + t + 1))
                    act.wait_ge(S["gate_ready"], 2)
                for s in range(TRI):
                    if stage:
                        act.wait_ge(S["taps_done"], taps_at[half, t, stage - 1, s])
                    if s == 0 and prev:
                        if stage < 2:
                            act.wait_ge(S["taps_done"], taps_at[(*prev, stage + 1)])
                            act.wait_ge(tail_saved[stage], 48 * min(NT, half * NT + t))
                        else:
                            act.wait_ge(S["o_stored"], 48 * (half * NT + t))
                    place = t * TRI + s
                    dst = heads[:, s, :] if stage == 2 else win[stage + 1][:, s, HALF:2 * HALF]
                    nc.scalar.activation(dst, win[stage][:, s, HALF:2 * HALF], ACT.Identity,
                                         bias=conv_b[:, place, stage:stage + 1],
                                         scale=conv_w3[:, place, stage:stage + 1]).then_inc(S["conv_init"], 1)

            def split_o(g, p):
                act.wait_ge(o_loaded[p], 32 * (g // 2 + 1) if isinstance(g, int) else 16 * (g - p) + 32)
                if not (isinstance(g, int) and g == 0):
                    act.wait_ge(S["mixg_mm"], 2 * g)
                nc.scalar.copy(o_hi[:, :], big1[:, p, :]).then_inc(S["o_hi_ready"], 1)
                nc.scalar.copy(o_2[0:C2, :], big2[0:C2, p, :]).then_inc(S["o_hi_ready"], 1)

            def mix_gates(g):
                act.wait_ge(S["mixg_mm"], 2 * g + 1)
                if isinstance(g, int) and g == 0:
                    act.wait_ge(S["x_ready"], 2 * NG)
                else:
                    act.wait_ge(S["q_ready"], 2 * g)
                nc.scalar.activation(tg1[:, :], bank[4][:, :], ACT.Tanh, bias=mixg_bh[:, :], scale=0.5).then_inc(S["tg_ready"], 1)
                act.wait_ge(S["mixg_mm"], 2 * g + 2)
                nc.scalar.activation(tg2[:, :], bank[5][0:C2, :], ACT.Tanh, bias=mixg_bh2[:, :], scale=0.5).then_inc(S["tg_ready"], 1)

            def split_q(g):
                act.wait_ge(S["q_ready"], 2 * g + 1)
                if not (isinstance(g, int) and g == 0):
                    act.wait_ge(S["mix_mm"], 2 * g)
                nc.scalar.copy(q_hi[:, :], q1[:, :]).then_inc(S["q_hi_ready"], 1)
                act.wait_ge(S["q_ready"], 2 * g + 2)
                nc.scalar.copy(q_2[0:C2, :], q2[:, :]).then_inc(S["q_hi_ready"], 1)

            def gelu(g, c):
                act.wait_ge(S["in_mm"], NC * g + c + 1)
                if not (isinstance(g, int) and g == 0 and c < 2):
                    act.wait_ge(S["hid_lo_ready"], NC * g + c - 1)
                nc.scalar.activation(hid[:, c % 2, :], bank[2 + c % 2][:, :], ACT.Gelu, bias=fin_b_sb[:, c:c + 1]).then_inc(S["gelu_done"], 1)

            def high_hid(g, c):
                act.wait_ge(S["gelu_done"], NC * g + c + 1)
                if not (isinstance(g, int) and g == 0 and c < 3):
                    act.wait_ge(S["out_mm"], NC * g + c - 2)
                nc.scalar.copy(hid_hi[:, c % 3, :], hid[:, c % 2, :]).then_inc(S["hid_hi_ready"], 1)

            def beside(g, slot):
                for half, t, stage, k in parts_in(g, slot):
                    if k == 1:
                        start_unit(half, t, stage)

            def first_pass(g, p, convs=False, first=False, last=False):
                gates(g, p, first)
                if convs:
                    beside(g, 0)
                if not last:
                    high_n(g + 1, 1 - p)
                if not first:
                    read_y(g - 1, 1 - p)
                memory_rows(g, first)
                if convs:
                    for slot in (1, 2, 3):
                        beside(g, slot)

            def second_pass(g, p, convs=False, last=False):
                gelu(g, 0)
                gelu(g, 1)
                high_hid(g, 0)
                if not last:
                    mix_gates(g + 1)
                if convs:
                    beside(NG + g, 0)
                high_hid(g, 1)
                if not last:
                    split_q(g + 1)
                if convs:
                    beside(NG + g, 1)
                for c in range(2, NC):
                    gelu(g, c)
                    high_hid(g, c)
                    if convs and c < NC - 1:
                        beside(NG + g, c)
                if not last:
                    high_n(g + 1, 1 - p, second=True)
                if convs:
                    beside(NG + g, NC - 1)

            high_n(0, 0)
            first_pass(0, 0, first=True)
            with act.Fori(0, 3) as i:
                for k in range(2):
                    first_pass(2 * i + k + 1, 1 - k)
            first_pass(B - 1, 1)
            for g in range(B, NG):
                first_pass(g, g % 2, convs=True, last=g == NG - 1)
            read_y(NG - 1, 1)
            for half, t, stage, k in PARTS[1][:LEAD]:
                if k == 1:
                    start_unit(half, t, stage)
            split_o(0, 0)
            mix_gates(0)
            split_q(0)
            high_n(0, 0, second=True)
            split_o(1, 1)
            for g in range(B):
                second_pass(g, g % 2, convs=True)
                split_o(g + 2, g % 2)
            with act.Fori(B // 2, NG // 2 - 1) as i:
                for k in range(2):
                    second_pass(2 * i + k, k)
                    split_o(2 * i + k + 2, k)
            second_pass(NG - 2, 0)
            second_pass(NG - 1, 1, last=True)

        @block.vector
        def _(dve):
            nc.vector.memset(mem_r[:, :, C2:C2 + 1], 1.0 / CH).then_inc(S["consts"], 1)
            nc.vector.memset(zero_st[:, :], 0.0).then_inc(S["consts"], 1)
            nc.vector.memset(mem_rhs[:, :], 0.0).then_inc(S["consts"], 1)
            nc.vector.memset(big2[C2:C2 + 1, :, :], 1.0).then_inc(S["consts"], 1)
            dve.wait_ge(S["ld_idx"], 32)
            nc.vector.tensor_copy(xf[:, :], xi[:, :]).then_inc(S["idx_f"], 1)
            dve.wait_ge(S["idx_t"], 1)
            nc.vector.tensor_copy(idx[:, :], bank[0][:, 0:B * T // P]).then_inc(S["idx_ready"], 1)
            dve.wait_ge(S["pos_qt"], 2)
            nc.vector.tensor_copy(view(small, "qT1"), bank[1][:, 0:HD]).then_inc(S["pos_qs"], 1)
            nc.vector.tensor_copy(view(small, "qT2", C2), bank[2][0:C2, 0:HD]).then_inc(S["pos_qs"], 1)
            dve.wait_ge(S["pos_q"], 2)
            nc.vector.tensor_copy(view(small, "tabs", HD)[:, C:2 * C], bank[3][0:HD, 0:C]).then_inc(S["pos_tab_ready"], 1)
            nc.vector.tensor_copy(view(small, "tabs", HD)[:, 0:C], bank[3][0:HD, C:2 * C]).then_inc(S["pos_tab_ready"], 1)
            dve.wait_ge(S["mem_w_mm"], 2)
            dve.wait_ge(S["consts"], 4)
            nc.vector.scalar_tensor_tensor(mem_rhs[0:C2, 0:C2], bank[1][0:C2, 64:128], 0.5, mask_sb[:, :], ALU.mult, ALU.mult).then_inc(S["mem_w_ready"], 1)
            nc.vector.tensor_tensor(mem_rhs[0:C2, C2:2 * C2], bank[1][0:C2, 128:192], mask_sb[:, :], ALU.mult).then_inc(S["mem_w_ready"], 1)
            nc.vector.tensor_scalar(mem_rhs[0:C2, 2 * C2:3 * C2], mask_sb[:, :], view(small, "memg", C2), None, ALU.mult).then_inc(S["mem_w_ready"], 1)
            dve.wait_ge(S["ld_bias"], 16 * 5)
            nc.vector.tensor_scalar(router_bh[:, :], router_bh[:, :], 0.5, None, ALU.mult).then_inc(S["w_half"], 1)


            dve.wait_ge(S["ld_gate"], 48)
            for s in spans["gate"]:
                nc.vector.tensor_scalar(s[:, 0:P], s[:, 0:P], 0.5, None, ALU.mult)
                nc.vector.tensor_scalar(s[:, 2 * P:2 * P + C2], s[:, 2 * P:2 * P + C2], 0.5, None, ALU.mult).then_inc(S["w_half"], 1)
            dve.wait_ge(S["w_half"], 3)
            n_hi_w = [0]

            def split_weight(name, hi, lo, hi2=None, lo2=None, done="weights_ready"):
                first, second = spans[name]
                pairs = [(first, hi, lo)] + ([(second, hi2, lo2)] if hi2 is not None else [])
                for src, h, _ in pairs:
                    nc.vector.tensor_copy(h, src).then_inc(S["w_hi"], 1)
                    n_hi_w[0] += 1
                dve.wait_ge(S["w_hi"], n_hi_w[0])
                for src, h, l in pairs:
                    nc.vector.tensor_tensor(l, src, h.bitcast(F32), ALU.subtract).then_inc(S[done], 1)

            split_weight("gate", gate_h[:, :], gate_l[:, :], gate2_h[:, :], gate2_l[:, :], done="gate_ready")

            def other_weights():
                dve.wait_ge(S["ld_mixg"], 48)
                dve.wait_ge(S["ld_mix"], 48)
                nc.vector.tensor_scalar(mixg_bh[:, :], mixg_bh[:, :], 0.5, None, ALU.mult).then_inc(S["w_half"], 1)
                nc.vector.tensor_scalar(mixg_bh2[:, :], mixg_bh2[:, :], 0.5, None, ALU.mult).then_inc(S["w_half"], 1)
                for s in spans["mix"]:
                    nc.vector.tensor_scalar(s, s, 0.5, None, ALU.mult).then_inc(S["w_half"], 1)
                dve.wait_ge(S["w_half"], 7)
                split_weight("mixg", mixg_h[:, :], mixg_l[:, :], mixg2_h[:, :], mixg2_l[:, :])
                split_weight("mix", mix_h[:, :], mix_l[:, :], mix2_h[:, :], mix2_l[:, :])
                dve.wait_ge(S["ld_fin"], 48)
                split_weight("fin", fin_h[:, :], fin_l[:, :], fin2_h[:, :], fin2_l[:, :])
                dve.wait_ge(S["ld_fout"], 16)
                split_weight("fout", fout_h[:, :, :].rearrange("p k c -> p (k c)"), fout_l[:, :, :].rearrange("p k c -> p (k c)"))
                dve.wait_ge(S["ld_conv"], 16 * B)
                nc.vector.tensor_scalar(conv_w3[:, :, :], conv_w[:, :, :, TAPS - 1], 1.0, None, ALU.add).then_inc(S["weights_ready"], 1)

            def statistics(k, src, p):
                for j in range(NJ):
                    i = nc.vector.bn_stats(stats[:, p, j, :], src[:, j, :])
                i.then_inc(S["stats_done"], 1)
                dve.wait_ge(S["stats_done"], k + 1)
                mean_e, m2_e, mean_o, m2_o = (stats[:, p, :, n] for n in (1, 2, 4, 5))
                nc.vector.tensor_tensor(lnt[:, p, 0, :], mean_e, mean_o, ALU.subtract)
                nc.vector.scalar_tensor_tensor(lnt[:, p, 1, :], m2_e, C * EPS, m2_o, ALU.add, ALU.add)
                nc.vector.tensor_tensor(lnt[:, p, 2, :], mean_e, mean_o, ALU.add).then_inc(S["halves_done"], 1)
                dve.wait_ge(S["halves_done"], k + 1)
                nc.vector.tensor_scalar(mean[:, p, :], lnt[:, p, 2, :], 0.5, None, ALU.mult)
                nc.vector.scalar_tensor_tensor(lnt[:, p, 3, :], lnt[:, p, 0, :], 0.25, lnt[:, p, 0, :], ALU.mult, ALU.mult).then_inc(S["aggr_done"], 1)
                dve.wait_ge(S["aggr_done"], k + 1)
                nc.vector.scalar_tensor_tensor(var[:, p, :], lnt[:, p, 1, :], 1.0 / C, lnt[:, p, 3, :], ALU.mult, ALU.add).then_inc(S["var_ready"], 1)

            def embed(g, p, half):
                dve.wait_ge(gathered[p], 16 * NJ * (g // 2 + 1) if isinstance(g, int) else 32 * (g - p) + 64)
                nc.vector.tensor_tensor(res[:, p, :, :], res[:, p, :, :], pos[:, half * NJ:(half + 1) * NJ, :], ALU.add).then_inc(S["h_ready"], 1)
                dve.wait_ge(S["h_ready"], g + 1)
                statistics(g, res[:, p, :, :], p)

            def normalise(k, src, p, first=False):
                dve.wait_ge(S["rstd_ready"], k + 1)
                if not first:
                    dve.wait_ge(S["nT_ready"], k)
                for j in range(NJ):
                    i = nc.vector.tensor_scalar(nrm[:, j, :], src[:, j, :], mean[:, p, j:j + 1], rstd[:, p, j:j + 1], ALU.subtract, ALU.mult)
                i.then_inc(S["n_ready"], 1)

            def low_n(k, p):
                dve.wait_ge(S["nT_hi"], 2 * k + 1)
                nc.vector.tensor_tensor(n_lo[:, p, :], bank[0][:, :], n_hi[:, p, :].bitcast(F32), ALU.subtract)
                dve.wait_ge(S["nT_hi"], 2 * k + 2)
                nc.vector.tensor_tensor(n_2[C2:P, p, :], bank[1][0:C2, :], n_2[0:C2, p, :].bitcast(F32), ALU.subtract).then_inc(S["n_split"], 1)

            def gated2(g, p):
                if not (isinstance(g, int) and g < 2):
                    dve.wait_ge(x_stored[p], 24 * (g - p))
                    dve.wait_ge(S["y_mm"], g - 1)
                dve.wait_ge(S["tanh_done"], 3 * g + 1)
                nc.vector.scalar_tensor_tensor(big2[0:C2, p, :], tg2[:, :], 1.0, bank[4][0:C2, :], ALU.add, ALU.mult).then_inc(S["x_ready"], 1)

            def gated1(g, p):
                dve.wait_ge(S["tanh_done"], 3 * g + 2)
                nc.vector.scalar_tensor_tensor(big1[:, p, :], tg1[:, :], 1.0, bank[2][:, :], ALU.add, ALU.mult).then_inc(S["x_ready"], 1)
                dve.wait_ge(S["tanh_done"], 3 * g + 3)
                nc.vector.tensor_scalar(hw_row[:, p, :], hw_row[:, p, :], 0.5, 0.5, ALU.mult, ALU.add).then_inc(S["hw_half"], 1)

            def memory_keys(g):
                for half in range(2):
                    dve.wait_ge(S["mem_act"], 4 * g + 2 * half + 2)
                    tiles = slice(2 * half, 2 * half + 2)
                    nc.vector.scalar_tensor_tensor(mem_l[:, tiles, 0:C2], mem_l[:, tiles, C2:P], 1.0,
                                                   bank_jc(6 + half)[:, :, 0:C2], ALU.add, ALU.mult).then_inc(S["gx_ready"], 1)

            def recurrence(g, p, b, half):
                dve.wait_ge(S["G_ready"], g + 1)
                if not (isinstance(g, int) and g == 0):
                    dve.wait_ge(S["masked"], 2 * g)
                for k in range(2):
                    i = nc.vector.tensor_scalar(dec[:, p, 4 * k:4 * k + 4], bank_g(3 + 2 * k)[C2:P, :, C2], -0.5, 0.5, ALU.mult, ALU.add)
                i.then_inc(S["dec_ready"], 1)
                dve.wait_ge(S["dec_ready"], g + 1)
                for c in range(8):
                    if c:
                        dve.wait_ge(S["step_done"], 8 * g + c)
                    at = c % 2 * NJ + c // 2
                    old = st[:, c - 1, :] if c else (zero_st[:, :] if half == 0 else st_mid[:, b, :])
                    new = st[:, c, :] if c < 7 else st_mid[:, b, :]
                    if half and c == 7:
                        new = st_end[:, :]
                    nc.vector.scalar_tensor_tensor(new, old, dec[:, p, at:at + 1], bank_g(3 + 2 * (c % 2))[0:C2, c // 2, 0:C2],
                                                   ALU.mult, ALU.add).then_inc(S["step_done"], 1)

            def part_of_unit(half, t, stage, k):
                def last_write(s, before):
                    done = [taps_at[key] for key in (((half, t, stage, s, "tap", n)) for n in range(1, before)) if key in taps_at]
                    if done:
                        dve.wait_ge(S["taps_done"], done[-1])
                    else:
                        dve.wait_ge(S["conv_init"], init_at[half, t, stage, s])

                if k == FINISH:
                    dve.wait_ge(S["hy_loaded"], hy_at[half, t])
                    for s in range(TRI):
                        if t * TRI + s >= FIRST_MEM:
                            last_write(s, TAPS)
                            nc.vector.tensor_tensor(heads[:, s, :], heads[:, s, :], y_in[:, s, :], ALU.add).then_inc(S["taps_done"], 1)
                    for s in range(TRI):
                        if t * TRI + s >= FIRST_MEM:
                            dve.wait_ge(S["taps_done"], taps_at[half, t, stage, s, "y", 0])
                        else:
                            last_write(s, TAPS)
                        nc.vector.tensor_tensor(heads[:, s, :], heads[:, s, :], hw_in[:, s, :], ALU.mult).then_inc(S["taps_done"], 1)
                    return
                for s in range(TRI):
                    place = t * TRI + s
                    (lo, hi), (src_lo, src_hi) = tap_range(half, k * DILATIONS[ORDER[place]][stage])
                    if lo >= hi:
                        continue
                    last_write(s, k)
                    if half and stage and k == 1 and s == 0:
                        dve.wait_ge(tail_loaded[stage - 1], 48 * (t + 1))
                    if stage == 2:
                        acc = heads[:, s, lo - HALF:hi - HALF]
                    else:
                        acc = win[stage + 1][:, s, lo:hi]
                    nc.vector.scalar_tensor_tensor(acc, win[stage][:, s, src_lo:src_hi],
                                                   conv_w[:, place, stage, TAPS - 1 - k:TAPS - k],
                                                   acc, ALU.mult, ALU.add).then_inc(S["taps_done"], 1)

            def mixed(g, p):
                if isinstance(g, int) and g == 0:
                    dve.wait_ge(o_loaded[0], 32)
                else:
                    dve.wait_ge(S["q_lo_ready"], 2 * g)
                dve.wait_ge(S["tg_ready"], 2 * g + 1)
                nc.vector.scalar_tensor_tensor(q1[:, :], tg1[:, :], 1.0, big1[:, p, :], ALU.add, ALU.mult).then_inc(S["q_ready"], 1)
                dve.wait_ge(S["tg_ready"], 2 * g + 2)
                nc.vector.scalar_tensor_tensor(q2[:, :], tg2[:, :], 1.0, big2[0:C2, p, :], ALU.add, ALU.mult).then_inc(S["q_ready"], 1)

            def attended(g, p):
                dve.wait_ge(S["res_biased"], g + 1)
                if not (isinstance(g, int) and g < 2):
                    dve.wait_ge(out_stored[p], 8 * (g - p))
                for k in range(2):
                    dve.wait_ge(S["mix_mm"], 2 * g + k + 1)
                    i = nc.vector.tensor_tensor(h2[:, p, 2 * k:2 * k + 2, :], bank_jc(4 + k), res[:, p, 2 * k:2 * k + 2, :], ALU.add)
                i.then_inc(S["h2_ready"], 1)
                dve.wait_ge(S["h2_ready"], g + 1)
                statistics(NG + g, h2[:, p, :, :], p)

            def low_hid(g, c):
                dve.wait_ge(S["hid_hi_ready"], NC * g + c + 1)
                nc.vector.tensor_tensor(hid_lo[:, c % 3, :], hid[:, c % 2, :], hid_hi[:, c % 3, :].bitcast(F32), ALU.subtract).then_inc(S["hid_lo_ready"], 1)

            def result(g, p):
                dve.wait_ge(S["out_mm"], NC * g + NC)
                for k in range(2):
                    i = nc.vector.tensor_tensor(h2[:, p, 2 * k:2 * k + 2, :], bank_jc(6 + k), h2[:, p, 2 * k:2 * k + 2, :], ALU.add)
                i.then_inc(S["out_ready"], 1)

            def beside(g, slot):
                for part in parts_in(g, slot):
                    part_of_unit(*part)

            def first_pass(g, p, b, half):
                gated2(g, p)
                if half == 0 or b + 1 < B:
                    normalise(g + 1, res[:, 1 - p, :, :], 1 - p)
                gated1(g, p)
                if half:
                    beside(g, 0)
                if half == 0 or b + 1 < B:
                    low_n(g + 1, 1 - p)
                memory_keys(g)
                if half:
                    beside(g, 1)
                if half == 0:
                    embed(g + 2, p, 0 if not isinstance(g, int) or g + 2 < B else 1)
                elif b + 2 < B:
                    embed(g + 2, p, 1)
                if half:
                    beside(g, 2)
                recurrence(g, p, b, half)
                if half:
                    beside(g, 3)

            def second_pass(g, p, convs=False, last=False):
                for c in range(NC):
                    if c == 3 and not last:
                        attended(g + 1, 1 - p)
                    if c == 5 and not last:
                        normalise(NG + g + 1, h2[:, 1 - p, :, :], 1 - p)
                    low_hid(g, c)
                    if c == 0 and not last:
                        mixed(g + 1, 1 - p)
                    if c == 5:
                        if not last:
                            low_n(NG + g + 1, 1 - p)
                        result(g, p)
                    if convs:
                        beside(NG + g, c)

            dve.wait_ge(S["pos_ready"], 4)
            embed(0, 0, 0)
            normalise(0, res[:, 0, :, :], 0, first=True)
            embed(1, 1, 0)
            other_weights()
            low_n(0, 0)
            first_pass(0, 0, 0, 0)
            with dve.Fori(0, 2) as i:
                for k in range(2):
                    g = 2 * i + k + 1
                    first_pass(g, 1 - k, g, 0)
            for g in range(5, B):
                first_pass(g, g % 2, g, 0)
            for g in range(B, NG):
                first_pass(g, g % 2, g - B, 1)
            for part in PARTS[1][:LEAD]:
                part_of_unit(*part)
            mixed(0, 0)
            attended(0, 0)
            normalise(NG, h2[:, 0, :, :], 0)
            low_n(NG, 0)
            for g in range(B):
                second_pass(g, g % 2, convs=True)
            with dve.Fori(B // 2, NG // 2 - 1) as i:
                for k in range(2):
                    second_pass(2 * i + k, k)
            second_pass(NG - 2, 0)
            second_pass(NG - 1, 1, last=True)

        @block.tensor
        def _(pe):
            def mm(dst, lhsT, rhs, start, stop):
                return nc.tensor.matmul(dst, lhsT, rhs, start=start, stop=stop)

            def mm5(dst, pairs):
                for n, (lhsT, rhs) in enumerate(pairs):
                    i = mm(dst, lhsT, rhs, n == 0, n == len(pairs) - 1)
                return i

            pe.wait_ge(S["idx_f"], 1)
            nr = B * T // P
            nc.tensor.transpose(bank[0][:, 0:nr], xf[:, :], id_sb[0:nr, 0:nr]).then_inc(S["idx_t"], 1)
            pe.wait_ge(S["ld_small"], 16 * 14)
            carry = [view(small, "carry1"), view(small, "carry2", C2)]
            pT = [view(small, "posT1"), view(small, "posT2", C2)]
            qT = [view(small, "qT1"), view(small, "qT2", C2)]
            for m, (lo, hi) in enumerate(((0, P), (P, C))):
                for k in range(2):
                    i = mm(bank[1 + m][0:hi - lo, 0:HD], carry[k][:, lo:hi], pT[k], k == 0, k == 1)
                i.then_inc(S["pos_qt"], 1)
            for k in range(2):
                i = mm(bank[3][0:HD, 0:C], pT[k], carry[k], k == 0, k == 1)
            i.then_inc(S["pos_q"], 1)
            pe.wait_ge(S["pos_qs"], 2)
            for k in range(2):
                i = mm(bank[3][0:HD, C:2 * C], qT[k], carry[k], k == 0, k == 1)
            i.then_inc(S["pos_q"], 1)
            mm(bank[1][0:C2, 64:128], view(small, "memk", HD), view(small, "memq", HD), True, True).then_inc(S["mem_w_mm"], 1)
            mm(bank[1][0:C2, 128:192], view(small, "memv"), view(small, "memo"), True, True).then_inc(S["mem_w_mm"], 1)
            pe.wait_ge(S["pos_tab_ready"], 2)
            for r in range(T // P):
                for d, one_hot in enumerate((digit2_sb, digit1_sb, digit0_sb)):
                    i = mm(bank[4 + r // 2][:, (r % 2) * C:(r % 2 + 1) * C], one_hot[:, r * P:(r + 1) * P],
                           view(small, "tabs", HD)[:, d * C:(d + 1) * C], d == 0, d == 2)
            i.then_inc(S["pos_mm"], 1)

            def transposes(k):
                pe.wait_ge(S["n_ready"], k + 1)
                if not (isinstance(k, int) and k == 0):
                    pe.wait_ge(S["n_split"], k)
                for j in range(NJ):
                    nc.tensor.transpose(bank[0][:, j * P:(j + 1) * P], nrm[:, j, 0:P], id_sb[:, :])
                for j in range(NJ):
                    i = nc.tensor.transpose(bank[1][0:C2, j * P:(j + 1) * P], nrm[:, j, P:C], id_sb[:, :])
                i.then_inc(S["nT_ready"], 1)

            def gates(g, p, first=False):
                pe.wait_ge(S["n_split"], g + 1)
                for b, lo, hi in ((4, 2 * P, 3 * P), (2, 0, P), (3, P, 2 * P), (5, 3 * P, GW)):
                    if not first:
                        if b == 4:
                            pe.wait_ge(S["x_ready"], 2 * g)
                        if b == 3:
                            pe.wait_ge(S["step_done"], 8 * g)
                    mm5(bank[b][0:hi - lo, :], [(gate_h[:, lo:hi], n_hi[:, p, :]), (gate_l[:, lo:hi], n_hi[:, p, :]),
                                                (gate_h[:, lo:hi], n_lo[:, p, :]), (gate2_h[:, lo:hi], n_2[:, p, :]),
                                                (gate2_l[:, lo:hi], n_2[:, p, :])]).then_inc(S["gate_mm"], 1)

            def memory_rows(g, p, first=False):
                pe.wait_ge(S["x_ready"], 2 * g + 1)
                for j in range(NJ):
                    if j % 2 == 0 and not first:
                        pe.wait_ge(S["gx_ready"], 2 * g - 1 + j // 2)
                    i = mm(bank_jc(6 + j // 2)[:, j % 2, :], big2[:, p, j * P:(j + 1) * P], mem_rhs[:, :], True, True)
                    if j % 2:
                        i.then_inc(S["mem_mm"], 1)

            def writes(g):
                pe.wait_ge(S["tanh_done"], 3 * g + 3)
                for j in range(NJ):
                    if j % 2 == 0:
                        pe.wait_ge(S["gx_ready"], 2 * g + 1 + j // 2)
                    for r in range(2):
                        rows = slice(r * CH, (r + 1) * CH)
                        i = mm(bank_g(3 + 2 * r)[:, j, :], mem_l[rows, j, :], mem_r[rows, j, :], True, True)
                i.then_inc(S["G_ready"], 1)

            def reads_can_start(g, first=False):
                pe.wait_ge(S["masked"], 2 * g + 2)
                if not first:
                    pe.wait_ge(S["y_ready"], g)

            def reads(g, p):
                for c in range(8):
                    i = mm(bank[1][C2:P, c * CH:(c + 1) * CH], st_bd[:, c, :], big2[0:C2, p, c * CH:(c + 1) * CH], True, True)
                i.then_inc(S["y_mm"], 1)

            def first_pass(g, p, last=False):
                gates(g, p)
                reads_can_start(g - 1, first=isinstance(g, int) and g == 1)
                if not last:
                    transposes(g + 1)
                reads(g - 1, 1 - p)
                memory_rows(g, p)
                writes(g)

            def mix_gates(g):
                pe.wait_ge(S["o_lo_ready"], 2 * g + 2)
                if not (isinstance(g, int) and g == 0):
                    pe.wait_ge(S["h2_ready"], g)
                for b, lo, hi in ((4, 0, P), (5, P, C)):
                    mm5(bank[b][0:hi - lo, :], [(mixg_h[:, lo:hi], o_hi[:, :]), (mixg_l[:, lo:hi], o_hi[:, :]),
                                                (mixg_h[:, lo:hi], o_lo[:, :]), (mixg2_h[:, lo:hi], o_2[:, :]),
                                                (mixg2_l[:, lo:hi], o_2[:, :])]).then_inc(S["mixg_mm"], 1)

            def mix(g):
                pe.wait_ge(S["q_lo_ready"], 2 * g + 2)
                for j in range(NJ):
                    cut = slice(j * P, (j + 1) * P)
                    i = mm5(bank_jc(4 + j // 2)[:, j % 2, :],
                            [(q_hi[:, cut], mix_h[:, :]), (q_hi[:, cut], mix_l[:, :]), (q_lo[:, cut], mix_h[:, :]),
                             (q_2[:, cut], mix2_h[:, :]), (q_2[:, cut], mix2_l[:, :])])
                    if j % 2:
                        i.then_inc(S["mix_mm"], 1)

            def ffn_in(g, c, p):
                if c == 0:
                    pe.wait_ge(S["n_split"], NG + g + 1)
                if not (isinstance(g, int) and g == 0 and c < 2):
                    pe.wait_ge(S["gelu_done"], NC * g + c - 1)
                cut = slice(c * P, (c + 1) * P)
                mm5(bank[2 + c % 2][:, :], [(fin_h[:, cut], n_hi[:, p, :]), (fin_l[:, cut], n_hi[:, p, :]),
                                            (fin_h[:, cut], n_lo[:, p, :]), (fin2_h[:, cut], n_2[:, p, :]),
                                            (fin2_l[:, cut], n_2[:, p, :])]).then_inc(S["in_mm"], 1)

            def ffn_out(g, c):
                if c == 0 and not (isinstance(g, int) and g == 0):
                    pe.wait_ge(S["out_ready"], g)
                pe.wait_ge(S["hid_lo_ready"], NC * g + c + 1)
                for j in range(NJ):
                    cut = slice(j * P, (j + 1) * P)
                    dst = bank_jc(6 + j // 2)[:, j % 2, :]
                    for n, (a, w) in enumerate(((hid_hi, fout_h), (hid_hi, fout_l), (hid_lo, fout_h))):
                        i = nc.tensor.matmul(dst, a[:, c % 3, cut], w[:, c, :], start=c == 0 and n == 0 and j % 2 == 0,
                                             stop=c == NC - 1 and n == 2, skip_group_check=True)
                i.then_inc(S["out_mm"], 1)

            def second_pass(g, p, last=False):
                ffn_in(g, 0, p)
                ffn_in(g, 1, p)
                if not last:
                    mix_gates(g + 1)
                ffn_in(g, 2, p)
                ffn_out(g, 0)
                ffn_in(g, 3, p)
                ffn_out(g, 1)
                if not last:
                    mix(g + 1)
                ffn_in(g, 4, p)
                ffn_out(g, 2)
                ffn_in(g, 5, p)
                ffn_out(g, 3)
                if not last:
                    transposes(NG + g + 1)
                ffn_out(g, 4)
                ffn_out(g, 5)

            transposes(0)
            pe.wait_ge(S["gate_ready"], 2)
            pe.wait_ge(S["pos_ready"], 4)
            gates(0, 0, first=True)
            transposes(1)
            pe.wait_ge(S["mem_w_ready"], 3)
            pe.wait_ge(S["ld_membg"], 16)
            memory_rows(0, 0, first=True)
            writes(0)
            first_pass(1, 1)
            first_pass(2, 0)
            with pe.Fori(1, NG // 2 - 1) as i:
                for k in range(2):
                    first_pass(2 * i + k + 1, 1 - k)
            first_pass(NG - 1, 1, last=True)
            reads_can_start(NG - 1)
            reads(NG - 1, 1)
            pe.wait_ge(S["step_done"], 8 * NG)
            pe.wait_ge(S["gx_ready"], 2 * NG)
            pe.wait_ge(S["weights_ready"], 8)
            mix_gates(0)
            mix(0)
            transposes(NG)
            second_pass(0, 0)
            second_pass(1, 1)
            with pe.Fori(1, NG // 2 - 1) as i:
                for k in range(2):
                    second_pass(2 * i + k, k)
            second_pass(NG - 2, 0)
            second_pass(NG - 1, 1, last=True)


FINISH = TAPS
PARTS = [[(half, t, stage, k) for t in range(NT) for stage in range(3)
          for k in list(range(1, TAPS)) + ([FINISH] if stage == 2 else [])] for half in range(2)]
LEAD = 2 * (TAPS - 1)
FIRST_SLOTS = (0, 1, 2, 3, 3)


def is_last(half, t, stage, k):
    return k == (FINISH if stage == 2 else TAPS - 1)


def parts_in(g, slot):
    if g < NG:
        n = len(PARTS[0]) // B
        at = n * (g - B)
        return [PARTS[0][at + i] for i in range(n) if FIRST_SLOTS[i] == slot]
    at = LEAD + NC * (g - NG) + slot
    return PARTS[1][at:at + 1]


_IN_ORDER = ["x", "tok", "posT", "pos_tab", "carryT", "conv", "memq", "memk", "memv", "memo", "memg", "membg", "gateT",
             "router_b", "mixgT", "mixg_b", "mixT", "mix_b", "finT", "fin_b", "fout", "digits", "ident", "mask"]


def _layout(i):
    import numpy as np

    def order(a, axis):
        parts = np.split(a, NH, axis=axis)
        return np.concatenate([parts[h] for h in ORDER], axis=axis)

    gate = np.asarray(i["L0_attn_gate_w"])
    xg, gt = order(gate[0:C], 0), order(gate[C:2 * C], 0)
    router = np.asarray(i["L0_attn_router_w"])[ORDER]
    mixg = order(order(np.asarray(i["L0_attn_mixg_w"]), 0), 1)
    conv_w = np.asarray(i["L0_attn_conv_w"])[ORDER].transpose(2, 0, 1, 3).reshape(HD, -1)
    conv_b = np.asarray(i["L0_attn_conv_b"])[ORDER].transpose(2, 0, 1).reshape(HD, -1)
    wq, wk, wv, wo = (np.asarray(i[f"L0_attn_mem_W{n}"]) for n in ("q", "k", "v", "out"))
    u = T - 1 - np.arange(T)
    digits = np.stack([(np.arange(HD)[:, None] == (u // HD ** d % HD)[None, :]) for d in (2, 1, 0)]).astype(np.float32)
    lane = np.arange(C2) // HD
    return {
        "x": np.asarray(i["x"]),
        "tok": np.asarray(i["L0_tok_tok_table"]),
        "posT": np.asarray(i["L0_tok_pos_table"]).T,
        "pos_tab": np.asarray(i["L0_tok_pos_table"]),
        "carryT": np.asarray(i["L0_tok_carry_W"]).T,
        "conv": np.concatenate([conv_w, conv_b], axis=1),
        "memq": wq.transpose(1, 0, 2).reshape(HD, C2),
        "memk": wk.transpose(1, 0, 2).reshape(HD, C2),
        "memv": wv.transpose(1, 0, 2).reshape(P, C2),
        "memo": wo.transpose(2, 0, 1).reshape(P, C2),
        "memg": np.asarray(i["L0_attn_mem_Wg_w"]).reshape(C2, 1),
        "membg": np.repeat(np.asarray(i["L0_attn_mem_Wg_b"]).reshape(1, NM), HD, axis=1),
        "gateT": np.concatenate([xg[0:P], gt[0:P], xg[P:C], gt[P:C], router], axis=0).T,
        "router_b": np.asarray(i["L0_attn_router_b"])[ORDER].reshape(NH, 1),
        "mixgT": mixg.T,
        "mixg_b": order(np.asarray(i["L0_attn_mixg_b"]), 0).reshape(C, 1),
        "mixT": order(np.asarray(i["L0_attn_mix_w"]), 1).T,
        "mix_b": np.asarray(i["L0_attn_mix_b"]),
        "finT": np.asarray(i["L0_ffn_in_weight"]).T,
        "fin_b": np.asarray(i["L0_ffn_in_bias"]).reshape(NC, P).T,
        "fout": np.asarray(i["L0_ffn_out_weight"]),
        "digits": digits,
        "ident": np.eye(P, dtype=np.float32),
        "mask": (lane[:, None] == lane[None, :]).astype(np.float32),
    }


def kernel(**inputs):
    import numpy as np
    import concourse.bacc as bacc
    from concourse.bass_utils import run_bass_kernel_spmd as run

    nc = bacc.Bacc("TRN2", target_bir_lowering=False, num_devices=1)
    operands = _layout(inputs)
    arrays, args = {}, []
    for name in _IN_ORDER:
        a = np.ascontiguousarray(operands[name])
        arrays[f"in_{name}"] = a
        args.append(nc.dram_tensor(f"in_{name}", a.shape, mybir.dt.from_np(a.dtype), kind="ExternalInput").ap())
    args.append(nc.dram_tensor("out_h", (B, T, C), F32, kind="ExternalOutput").ap())
    lm_tower(nc, *args)
    r = run(nc, [arrays], core_ids=[0])
    return r.results[0]["out_h"]
```

```python
from contextlib import ExitStack

import concourse.bass as bass
from concourse import mybir

F32 = mybir.dt.float32
F32R = mybir.dt.float32r
I32 = mybir.dt.int32
U32 = mybir.dt.uint32
ALU = mybir.AluOpType
ACT = mybir.ActivationFunctionType

P = 128
C = 192
C2 = C - P
B, T = 8, 1024
HALF = 512
NG = B * T // HALF
NJ = HALF // P
HD = 16
NH = 12
HID = 768
NC = HID // P
CH = 64
EPS = 1e-5
TAPS = 4
DILATIONS = [(1, 2, 4), (1, 1, 1), (4, 8, 16), (8, 16, 32), (32, 64, 128), (64, 128, 64),
             (64, 128, 256), (1, 100, 200), (1, 125, 250), (1, 256, 512), (3, 9, 27), (5, 25, 125)]
MEM_HEADS = (6, 7, 8, 9)
ORDER = [h for h in range(NH) if h not in MEM_HEADS] + list(MEM_HEADS)
FIRST_MEM = NH - len(MEM_HEADS)
NM = len(MEM_HEADS)
TRI = 3
NT = NH // TRI
DIGIT_AT = 32
DIGIT_ROWS = 2 * DIGIT_AT + HD
GW = 2 * C + NH


def history(place, stage):
    return min(HALF, (TAPS - 1) * DILATIONS[ORDER[place]][stage])


def tap_range(half, shift):
    lo = HALF + shift if half == 0 else max(HALF, shift)
    return (lo, 2 * HALF), (lo - shift, 2 * HALF - shift)


def lm_tower(nc, x, tok, posT, pos_tab, carryT, conv, memq, memk, memv, memo, memg, membg,
             gateT, router_b, mixgT, mixg_b, mixT, mix_b, finT, fin_b, fout, digits, ident, mask, out):
    with ExitStack() as ctx:
        def sb(name, shape, dt=F32):
            return ctx.enter_context(nc.sbuf_tensor(name, shape, dt))

        def sem(name):
            return ctx.enter_context(nc.semaphore(name))

        def scratch(name, shape):
            return nc.dram_tensor(name, shape, F32, kind="Internal").ap()

        bank = [ctx.enter_context(nc.psum_tensor(f"bank{i}", [P, 512], F32)) for i in range(8)]

        h_dram = scratch("h_dram", (NG, P, NJ * C))
        x_dram = scratch("x_dram", (B, C, T))
        hw_dram = scratch("hw_dram", (NH, B, T))
        y_dram = scratch("y_dram", (B, C2, T))
        o_dram = scratch("o_dram", (B, C, T))
        tail_dram = [scratch(f"tail{s}_dram", (NH, P, HALF)) for s in range(2)]

        id_sb = sb("id_sb", [P, P])
        mask_sb = sb("mask_sb", [C2, C2])
        zero_st = sb("zero_st", [C2, C2])
        xi = sb("xi", [B * T // P, P], I32)
        xf = sb("xf", [B * T // P, P])
        idx = sb("idx", [P, B * T // P], I32)
        pos = sb("pos", [P, T // P, C])
        gate_h, gate_l = sb("gate_h", [P, GW], F32R), sb("gate_l", [P, GW], F32R)
        gate2_h, gate2_l = sb("gate2_h", [P, GW], F32R), sb("gate2_l", [P, GW], F32R)
        mixg_h, mixg_l = sb("mixg_h", [P, C], F32R), sb("mixg_l", [P, C], F32R)
        mixg2_h, mixg2_l = sb("mixg2_h", [P, C], F32R), sb("mixg2_l", [P, C], F32R)
        mix_h, mix_l = sb("mix_h", [P, C], F32R), sb("mix_l", [P, C], F32R)
        mix2_h, mix2_l = sb("mix2_h", [P, C], F32R), sb("mix2_l", [P, C], F32R)
        fin_h, fin_l = sb("fin_h", [P, HID], F32R), sb("fin_l", [P, HID], F32R)
        fin2_h, fin2_l = sb("fin2_h", [P, HID], F32R), sb("fin2_l", [P, HID], F32R)
        fout_h, fout_l = sb("fout_h", [P, NC, C], F32R), sb("fout_l", [P, NC, C], F32R)
        conv_sb = sb("conv_sb", [P, NH * 3 * (TAPS + 1)])
        conv_w = conv_sb[:, 0:NH * 3 * TAPS].rearrange("p (h s k) -> p h s k", h=NH, s=3)
        conv_b = conv_sb[:, NH * 3 * TAPS:].rearrange("p (h s) -> p h s", h=NH)
        conv_w3 = sb("conv_w3", [P, NH, 3])
        mem_rhs = sb("mem_rhs", [C2 + 1, 3 * C2])
        router_bh = sb("router_bh", [NH, 1])
        mixg_bh, mixg_bh2 = sb("mixg_bh", [P, 1]), sb("mixg_bh2", [C2, 1])
        mix_b_sb = sb("mix_b_sb", [P, C])
        fin_b_sb = sb("fin_b_sb", [P, NC])
        warm = sb("warm", [P, 1])

        win = [sb(f"win{s}", [P, TRI, 2 * HALF]) for s in range(3)]
        heads = sb("heads", [P, TRI, HALF])
        hw_in = sb("hw_in", [P, TRI, HALF])
        y_in = sb("y_in", [P, TRI, HALF])

        res = sb("res", [P, 2, NJ, C])
        stats = sb("stats", [P, 2, NJ, 6])
        lnt = sb("lnt", [P, 2, 4, NJ])
        mean = sb("mean", [P, 2, NJ])
        var = sb("var", [P, 2, NJ])
        rstd = sb("rstd", [P, 2, NJ])
        half_neg = sb("half_neg", [P, NJ])
        nrm = sb("nrm", [P, NJ, C])
        n_hi = sb("n_hi", [P, 2, HALF], F32R)
        n_lo = sb("n_lo", [P, 2, HALF], F32R)
        n_2 = sb("n_2", [P, 2, HALF], F32R)
        big1 = sb("big1", [P, 2, HALF])
        big2 = sb("big2", [C2 + 1, 2, HALF])
        tg1, tg2 = sb("tg1", [P, HALF]), sb("tg2", [C2, HALF])
        hw_row = sb("hw_row", [NH, 2, HALF])
        mem_l = sb("mem_l", [P, NJ, P])
        mem_r = sb("mem_r", [P, NJ, C2 + 1])
        dec = sb("dec", [C2, 2, 8])
        st = sb("st", [C2, 7, C2])
        st_end = sb("st_end", [C2, C2])
        st_mid = sb("st_mid", [C2, B, C2])
        st_bd = sb("st_bd", [C2, 8, C2])
        y_sb = sb("y_sb", [C2, 2, HALF])
        o_hi, o_lo, o_2 = sb("o_hi", [P, HALF], F32R), sb("o_lo", [P, HALF], F32R), sb("o_2", [P, HALF], F32R)
        q1, q2 = sb("q1", [P, HALF]), sb("q2", [C2, HALF])
        q_hi, q_lo, q_2 = sb("q_hi", [P, HALF], F32R), sb("q_lo", [P, HALF], F32R), sb("q_2", [P, HALF], F32R)
        h2 = sb("h2", [P, 2, NJ, C])
        hid = sb("hid", [P, 2, HALF])
        hid_hi, hid_lo = sb("hid_hi", [P, 3, HALF], F32R), sb("hid_lo", [P, 3, HALF], F32R)
        raw1 = win[0][:, :, :].rearrange("p a b -> p (a b)")
        raw2 = win[1][:, :, :].rearrange("p a b -> p (a b)")
        small = win[2][:, :, :].rearrange("p a b -> p (a b)")

        names = """ld_idx ld_carry ld_digits ld_mem ld_membg ld_gate ld_mixg ld_mix ld_fin ld_fout ld_conv ld_bias
            idx_f idx_t idx_ready pos_qt pos_qs pos_q pos_tab_ready pos_mm pos_ready mem_w_mm mem_w_ready consts gate_ready conv_w_ready
            w_half w_hi weights_ready pool_consts
            h_ready stats_done halves_done aggr_done var_ready rstd_ready n_ready nT_ready nT_hi n_split
            gate_mm tanh_done hw_half x_ready mem_mm mem_act gx_ready G_ready dec_ready step_done masked y_mm y_ready
            gathered0 gathered1 h_stored0 h_stored1 x_stored0 x_stored1 y_stored0 y_stored1
            x0_loaded hy_loaded conv_init taps_done tail0_saved tail1_saved tail0_loaded tail1_loaded o_stored
            o_loaded0 o_loaded1 r_loaded0 r_loaded1 o_hi_ready o_lo_ready mixg_mm tg_ready q_ready q_hi_ready q_lo_ready
            res_biased mix_mm h2_ready in_mm gelu_done hid_hi_ready hid_lo_ready out_mm out_ready out_stored0 out_stored1""".split()
        S = {n: sem(n) for n in names}
        gathered, h_stored, x_stored, y_stored = ([S[f"{n}{p}"] for p in range(2)] for n in
                                                  ("gathered", "h_stored", "x_stored", "y_stored"))
        o_loaded, r_loaded, out_stored = ([S[f"{n}{p}"] for p in range(2)] for n in
                                          ("o_loaded", "r_loaded", "out_stored"))
        tail_saved = [S["tail0_saved"], S["tail1_saved"]]
        tail_loaded = [S["tail0_loaded"], S["tail1_loaded"]]

        spans, at1, at2 = {}, 0, 0
        for name, n1, n2 in (("gate", GW, GW), ("mixg", C, C), ("mix", C, C), ("fin", HID, HID), ("fout", NC * C, 0)):
            spans[name] = (raw1[:, at1:at1 + n1], raw2[:, at2:at2 + n2])
            at1, at2 = at1 + n1, at2 + n2
        assert at1 <= TRI * 2 * HALF and at2 <= TRI * 2 * HALF

        WEIGHTS = {"gate": ((spans["gate"][0], gate_h[:, :], gate_l[:, :]), (spans["gate"][1], gate2_h[:, :], gate2_l[:, :])),
                   "mixg": ((spans["mixg"][0], mixg_h[:, :], mixg_l[:, :]), (spans["mixg"][1], mixg2_h[:, :], mixg2_l[:, :])),
                   "mix": ((spans["mix"][0], mix_h[:, :], mix_l[:, :]), (spans["mix"][1], mix2_h[:, :], mix2_l[:, :])),
                   "fin": ((spans["fin"][0], fin_h[:, :], fin_l[:, :]), (spans["fin"][1], fin2_h[:, :], fin2_l[:, :])),
                   "fout": ((spans["fout"][0], fout_h[:, :, :].rearrange("p k c -> p (k c)"),
                             fout_l[:, :, :].rearrange("p k c -> p (k c)")),)}

        SECOND_WEIGHTS = [w for name in ("mixg", "mix", "fin", "fout") for w in WEIGHTS[name]]

        cols, at = {}, 0
        for name, n in (("carry1", C), ("carry2", C), ("posT1", HD), ("posT2", HD), ("qT1", HD), ("qT2", HD),
                        ("memk", C2), ("memq", C2), ("memv", C2), ("memo", C2), ("memg", 1), ("tabs", C)):
            cols[name] = slice(at, at + n)
            at += n
        digit_sb = heads[0:DIGIT_ROWS, :, :].rearrange("p a b -> p (a b)")[:, 0:T]

        taps_at, init_at, hy_at = {}, {}, {}
        n_taps = n_init = n_hy = 0
        for half in range(2):
            for t in range(NT):
                n_hy += 16 * TRI
                n_hy += 16 * sum(t * TRI + s >= FIRST_MEM for s in range(TRI))
                hy_at[half, t] = n_hy
                for stage in range(3):
                    for s in range(TRI):
                        n_init += 1
                        init_at[half, t, stage, s] = n_init
                    ops = []
                    for k in range(1, TAPS):
                        for s in range(TRI):
                            shift = k * DILATIONS[ORDER[t * TRI + s]][stage]
                            (lo, hi), _ = tap_range(half, shift)
                            if lo < hi:
                                ops.append((s, "tap", k))
                    if stage == 2:
                        ops += [(s, "y", 0) for s in range(TRI) if t * TRI + s >= FIRST_MEM]
                        ops += [(s, "hw", 0) for s in range(TRI)]
                    for s, what, k in ops:
                        n_taps += 1
                        taps_at[half, t, stage, s, what, k] = n_taps
                        taps_at[half, t, stage, s] = n_taps
                    taps_at[half, t, stage] = n_taps

        def before(half, t):
            n = half * NT + t - 1
            return None if n < 0 else (n // NT, n % NT)

        def view(ap, name, rows=P):
            return ap[0:rows, cols[name]]

        def bank_jc(i):
            return bank[i][:, 0:2 * C].rearrange("p (j c) -> p j c", j=2)

        def bank_g(i):
            return bank[i][:, 0:4 * (C2 + 1)].rearrange("p (c n) -> p c n", c=4)

        block = ctx.enter_context(nc.Block())

        @block.sync
        def _(sp):
            sp.dma_start(xi[:, :], x.rearrange("b (r p) -> (b r) p", p=P)).then_inc(S["ld_idx"], 16)
            sp.dma_start(id_sb[:, :], ident).then_inc(S["ld_idx"], 16)
            for dst, src in ((view(small, "carry1"), carryT[0:P, :]), (view(small, "carry2", C2), carryT[P:C, :]),
                             (view(small, "posT1"), posT[0:P, :]), (view(small, "posT2", C2), posT[P:C, :])):
                sp.dma_start(dst, src).then_inc(S["ld_carry"], 16)
            for dst, src in ((view(small, "tabs", DIGIT_ROWS), pos_tab), (digit_sb, digits)):
                sp.dma_start(dst, src).then_inc(S["ld_digits"], 16)
            for name, src in (("gate", gateT), ("mixg", mixgT), ("mix", mixT), ("fin", finT)):
                first, second = spans[name]
                sp.dma_start(first, src[0:P, :]).then_inc(S[f"ld_{name}"], 16)
                sp.dma_start(second[0:C2, :], src[P:C, :]).then_inc(S[f"ld_{name}"], 16)
                sp.dma_start(second[C2:P, :], src[P:C, :]).then_inc(S[f"ld_{name}"], 16)
            sp.dma_start(spans["fout"][0].rearrange("p (k c) -> p k c", k=NC),
                         fout.rearrange("(k p) c -> p k c", p=P)).then_inc(S["ld_fout"], 16)
            for dst, src in ((mixg_bh[:, :], mixg_b[0:P, :]), (mixg_bh2[:, :], mixg_b[P:C, :]),
                             (mix_b_sb[:, :], mix_b.partition_broadcast(P)), (fin_b_sb[:, :], fin_b)):
                sp.dma_start(dst, src).then_inc(S["ld_bias"], 16)
            for b in range(B):
                sp.dma_start(conv_sb[b * HD:(b + 1) * HD, :], conv).then_inc(S["ld_conv"], 16)

            def store_h(g, p):
                sp.wait_ge(S["h_ready"], g + 1)
                sp.dma_start(h_dram[g], res[:, p, :, :].rearrange("p j c -> p (j c)")).then_inc(h_stored[p], 16)

            def store_x(g, p, b, half):
                span = slice(half * HALF, (half + 1) * HALF)
                sp.wait_ge(S["x_ready"], 2 * (g + 1))
                sp.dma_start(x_dram[b, 0:P, span], big1[:, p, :]).then_inc(x_stored[p], 16)
                sp.dma_start(x_dram[b, P:C, span], big2[0:C2, p, :]).then_inc(x_stored[p], 16)
                sp.wait_ge(S["hw_half"], g + 1)
                sp.dma_start(hw_dram[:, b, span], hw_row[:, p, :]).then_inc(x_stored[p], 16)

            def store_y(g, p, b, half):
                sp.wait_ge(S["y_ready"], g + 1)
                sp.dma_start(y_dram[b, :, half * HALF:(half + 1) * HALF], y_sb[:, p, :]).then_inc(y_stored[p], 16)

            def load_x0(half, t):
                prev = before(half, t)
                for p in range(2):
                    sp.wait_ge(x_stored[p], 48 * 4 * (half + 1))
                if prev:
                    sp.wait_ge(S["taps_done"], taps_at[(*prev, 0)])
                for s in range(TRI):
                    place = t * TRI + s
                    lo = HALF if half == 0 else HALF - history(place, 0)
                    at = lo - HALF * (1 - half)
                    sp.dma_start(win[0][:, s, lo:2 * HALF],
                                 x_dram[:, place * HD:(place + 1) * HD, at:HALF * (half + 1)]).then_inc(S["x0_loaded"], 16)

            def load_hy(half, t):
                prev = before(half, t)
                if prev:
                    sp.wait_ge(S["taps_done"], taps_at[(*prev, 2)])
                span = slice(half * HALF, (half + 1) * HALF)
                for s in range(TRI):
                    place = t * TRI + s
                    sp.dma_start(hw_in[:, s, :],
                                 hw_dram[place, :, span].rearrange("b (o t) -> b o t", o=1).to_broadcast((B, HD, HALF))
                                 ).then_inc(S["hy_loaded"], 16)
                    if place >= FIRST_MEM:
                        m = place - FIRST_MEM
                        for p in range(2):
                            sp.wait_ge(y_stored[p], 16 * 4 * (half + 1))
                        sp.dma_start(y_in[:, s, :], y_dram[:, m * HD:(m + 1) * HD, span]).then_inc(S["hy_loaded"], 16)

            def save_tail(half, t, stage):
                sp.wait_ge(S["taps_done"], taps_at[half, t, stage])
                for s in range(TRI):
                    place = t * TRI + s
                    n = history(place, stage + 1)
                    sp.dma_start(tail_dram[stage][place, :, HALF - n:HALF],
                                 win[stage + 1][:, s, 2 * HALF - n:2 * HALF]).then_inc(tail_saved[stage], 16)

            def load_tail(t, stage):
                prev = before(1, t)
                sp.wait_ge(tail_saved[stage], 16 * NH)
                sp.wait_ge(S["taps_done"], taps_at[(*prev, stage + 1)])
                for s in range(TRI):
                    place = t * TRI + s
                    n = history(place, stage + 1)
                    sp.dma_start(win[stage + 1][:, s, HALF - n:HALF],
                                 tail_dram[stage][place, :, HALF - n:HALF]).then_inc(tail_loaded[stage], 16)

            def store_heads(half, t):
                sp.wait_ge(S["taps_done"], taps_at[half, t, 2])
                for s in range(TRI):
                    place = t * TRI + s
                    sp.dma_start(o_dram[:, place * HD:(place + 1) * HD, half * HALF:(half + 1) * HALF],
                                 heads[:, s, :]).then_inc(S["o_stored"], 16)

            def after_unit(half, t, stage):
                more = t + 1 < NT
                if stage < 2 and half == 0:
                    save_tail(half, t, stage)
                if stage == 0 and more:
                    load_x0(half, t + 1)
                if stage == 1 and half == 1 and more:
                    load_tail(t + 1, 0)
                if stage == 2:
                    store_heads(half, t)
                    if more:
                        load_hy(half, t + 1)
                        if half == 1:
                            load_tail(t + 1, 1)

            def after_units(g, slots):
                for slot in slots:
                    for part in parts_in(g, slot):
                        if is_last(*part):
                            after_unit(*part[:3])

            def load_group(g, p, b, half):
                if not isinstance(g, int) or g >= 2:
                    sp.wait_ge(S["q_ready"], 2 * (g - 1))
                    sp.wait_ge(S["o_lo_ready"], 2 * (g - 1))
                    sp.wait_ge(S["h2_ready"], g - 1)
                span = slice(half * HALF, (half + 1) * HALF)
                sp.dma_start(big1[:, p, :], o_dram[b, 0:P, span]).then_inc(o_loaded[p], 16)
                sp.dma_start(big2[0:C2, p, :], o_dram[b, P:C, span]).then_inc(o_loaded[p], 16)
                sp.dma_start(res[:, p, :, :].rearrange("p j c -> p (j c)"), h_dram[g]).then_inc(r_loaded[p], 16)

            def store_out(g, p, b, half):
                sp.wait_ge(S["out_ready"], g + 1)
                sp.dma_start(out[b, half * HALF:(half + 1) * HALF, :].rearrange("(j p) c -> p j c", p=P),
                             h2[:, p, :, :]).then_inc(out_stored[p], 16)

            store_h(0, 0)
            store_h(1, 1)
            for g in (0, 1):
                store_x(g, g % 2, g, 0)
                store_h(g + 2, g % 2)
            with sp.Fori(1, 4) as i:
                for k in range(2):
                    g = 2 * i + k
                    store_x(g, k, g, 0)
                    store_y(g - 2, k, g - 2, 0)
                    store_h(g + 2, k)
            sp.wait_ge(S["weights_ready"], len(SECOND_WEIGHTS))
            load_x0(0, 0)
            for g in range(B, NG):
                store_x(g, g % 2, g - B, 1)
                store_y(g - 2, g % 2, (g - 2) % B, (g - 2) // B)
                if g + 2 < NG:
                    store_h(g + 2, g % 2)
                if g == B:
                    load_hy(0, 0)
                after_units(g, range(4))
            for g in (NG - 2, NG - 1):
                store_y(g, g % 2, g - B, 1)
            load_x0(1, 0)
            load_tail(0, 0)
            load_hy(1, 0)
            load_tail(0, 1)
            sp.wait_ge(S["o_stored"], 16 * NH)
            for p in range(2):
                sp.wait_ge(h_stored[p], 16 * NG // 2)
            load_group(0, 0, 0, 0)
            load_group(1, 1, 1, 0)
            for part in PARTS[1][:LEAD]:
                if is_last(*part):
                    after_unit(*part[:3])
            for g in range(B):
                if g == B - 2:
                    sp.wait_ge(S["o_stored"], 2 * 16 * NH)
                load_group(g + 2, g % 2, (g + 2) % B, (g + 2) // B)
                after_units(NG + g, range(NC))
                store_out(g, g % 2, g, 0)
            with sp.Fori(B // 2, NG // 2 - 1) as i:
                for k in range(2):
                    g = 2 * i + k
                    load_group(g + 2, k, g + 2 - B, 1)
                    store_out(g, k, g - B, 1)
            for g in (NG - 2, NG - 1):
                store_out(g, g % 2, g - B, 1)
            for p in range(2):
                sp.wait_ge(out_stored[p], 16 * NG // 2)

        @block.gpsimd
        def _(pool):
            nc.gpsimd.memset(half_neg[:, :], -0.5).then_inc(S["pool_consts"], 1)

            def gather(g):
                p = g % 2
                if g >= 2:
                    pool.wait_ge(S["n_ready"], g - 1)
                    pool.wait_ge(h_stored[p], 16 * (g // 2))
                half, b = g // B, g % B
                for j in range(NJ):
                    row = (b * T + half * HALF) // P + j
                    nc.gpsimd.indirect_dma_start(
                        out=res[:, p, j, :], out_offset=None, in_=tok,
                        in_offset=bass.IndirectOffsetOnAxis(ap=idx[:, row:row + 1], axis=0)).then_inc(gathered[p], 16)

            def power(k, p):
                pool.wait_ge(S["var_ready"], k + 1)
                nc.gpsimd.tensor_tensor(rstd[:, p, :], var[:, p, :], half_neg[:, :], ALU.pow).then_inc(S["rstd_ready"], 1)

            pool.wait_ge(S["idx_ready"], 1)
            gather(0)
            gather(1)
            pool.wait_ge(S["pool_consts"], 1)
            power(0, 0)
            gather(2)

            def masks(g):
                if g == 0:
                    pool.wait_ge(S["ld_mem"], 16 * 7)
                pool.wait_ge(S["step_done"], 8 * g + 7)
                if g:
                    pool.wait_ge(S["y_mm"], g)
                first = zero_st[:, :] if g < B else st_mid[:, g - B, :]
                nc.gpsimd.tensor_tensor(st_bd[:, 0, :], first, mask_sb[:, :], ALU.mult).then_inc(S["masked"], 1)
                nc.gpsimd.tensor_tensor(st_bd[:, 1:8, :], st[:, :, :],
                                        mask_sb[:, :].rearrange("p (o c) -> p o c", o=1).to_broadcast((C2, 7, C2)),
                                        ALU.mult).then_inc(S["masked"], 1)

            def low_weight(n):
                raw, high, low = SECOND_WEIGHTS[n]
                pool.wait_ge(S["w_hi"], 3 + n)
                nc.gpsimd.tensor_tensor(low, raw, high.bitcast(F32), ALU.subtract).then_inc(S["weights_ready"], 1)

            for g in range(NG):
                if g + 1 < NG:
                    power(g + 1, (g + 1) % 2)
                if g >= 2:
                    masks(g - 2)
                if g + 3 < NG:
                    gather(g + 3)
                if 1 <= g <= len(SECOND_WEIGHTS):
                    low_weight(g - 1)
            masks(NG - 2)
            masks(NG - 1)

            def low_o(g, p):
                pool.wait_ge(S["o_hi_ready"], 2 * g + 1)
                nc.gpsimd.tensor_tensor(o_lo[:, :], big1[:, p, :], o_hi[:, :].bitcast(F32), ALU.subtract).then_inc(S["o_lo_ready"], 1)
                pool.wait_ge(S["o_hi_ready"], 2 * g + 2)
                pool.wait_ge(S["o_lo_ready"], 2 * g + 1)
                nc.gpsimd.tensor_tensor(o_2[C2:P, :], big2[0:C2, p, :], o_2[0:C2, :].bitcast(F32), ALU.subtract).then_inc(S["o_lo_ready"], 1)
                pool.wait_ge(r_loaded[p], 16 * (g // 2 + 1) if isinstance(g, int) else 8 * (g - p) + 16)
                pool.wait_ge(S["o_lo_ready"], 2 * g + 2)
                nc.gpsimd.tensor_tensor(res[:, p, :, :], res[:, p, :, :],
                                        mix_b_sb[:, :].rearrange("p (o c) -> p o c", o=1).to_broadcast((P, NJ, C)),
                                        ALU.add).then_inc(S["res_biased"], 1)

            def low_q(g):
                pool.wait_ge(S["q_hi_ready"], 2 * g + 1)
                nc.gpsimd.tensor_tensor(q_lo[:, :], q1[:, :], q_hi[:, :].bitcast(F32), ALU.subtract).then_inc(S["q_lo_ready"], 1)
                pool.wait_ge(S["q_hi_ready"], 2 * g + 2)
                pool.wait_ge(S["q_lo_ready"], 2 * g + 1)
                nc.gpsimd.tensor_tensor(q_2[C2:P, :], q2[:, :], q_2[0:C2, :].bitcast(F32), ALU.subtract).then_inc(S["q_lo_ready"], 1)
                pool.wait_ge(S["q_lo_ready"], 2 * g + 2)

            pool.wait_ge(S["ld_bias"], 16 * 4)
            low_o(0, 0)
            low_q(0)
            low_o(1, 1)
            power(NG, 0)
            with pool.Fori(0, NG // 2 - 1) as i:
                for k in range(2):
                    g = 2 * i + k
                    low_q(g + 1)
                    low_o(g + 2, k)
                    power(NG + g + 1, 1 - k)
            low_q(NG - 1)
            power(2 * NG - 1, 1)

        @block.scalar
        def _(act):
            for dst, src in ((view(small, "memk", HD), memk), (view(small, "memq", HD), memq),
                             (view(small, "memv"), memv), (view(small, "memo"), memo),
                             (view(small, "memg", C2), memg), (mask_sb[:, :], mask), (router_bh[:, :], router_b)):
                act.dma_start(dst, src).then_inc(S["ld_mem"], 16)
            act.wait_ge(S["consts"], 3)
            act.dma_start(mem_rhs[C2:C2 + 1, 2 * C2:3 * C2], membg).then_inc(S["ld_membg"], 16)
            act.wait_ge(S["pool_consts"], 1)
            nc.scalar.activation(warm[:, :], half_neg[:, 0:1], ACT.Gelu)
            for k in range(4):
                act.wait_ge(S["pos_mm"], k + 1)
                nc.scalar.copy(pos[:, 2 * k:2 * k + 2, :], bank_jc(4 + k)).then_inc(S["pos_ready"], 1)

            def high_weights():
                act.wait_ge(S["w_half"], 7)
                for name in ("mixg", "mix", "fin", "fout"):
                    act.wait_ge(S[f"ld_{name}"], 16 if name == "fout" else 48)
                    for raw, high, _ in WEIGHTS[name]:
                        nc.scalar.copy(high, raw).then_inc(S["w_hi"], 1)

            def high_n(g, p, second=False):
                act.wait_ge(S["nT_ready"], (NG if second else 0) + g + 1)
                if not isinstance(g, int) or g >= 2:
                    if second:
                        act.wait_ge(S["in_mm"], NC * (g - 1))
                    else:
                        act.wait_ge(S["gate_mm"], 4 * (g - 1))
                nc.scalar.copy(n_hi[:, p, :], bank[0][:, :]).then_inc(S["nT_hi"], 1)
                nc.scalar.copy(n_2[0:C2, p, :], bank[1][0:C2, :]).then_inc(S["nT_hi"], 1)

            def gates(g, p, first=False):
                act.wait_ge(S["gate_mm"], 4 * g + 1)
                if not first:
                    act.wait_ge(S["x_ready"], 2 * g)
                nc.scalar.activation(tg2[:, :], bank[4][C2:P, :], ACT.Tanh, scale=0.5).then_inc(S["tanh_done"], 1)
                act.wait_ge(S["gate_mm"], 4 * g + 3)
                nc.scalar.activation(tg1[:, :], bank[3][:, :], ACT.Tanh, scale=0.5).then_inc(S["tanh_done"], 1)
                act.wait_ge(S["gate_mm"], 4 * g + 4)
                act.wait_ge(S["w_half"], 3)
                if not (isinstance(g, int) and g < 2):
                    act.wait_ge(x_stored[p], 24 * (g - p))
                nc.scalar.activation(hw_row[:, p, :], bank[5][0:NH, :], ACT.Tanh, bias=router_bh[:, :], scale=0.5).then_inc(S["tanh_done"], 1)

            def read_y(g, p):
                act.wait_ge(S["y_mm"], g + 1)
                if not (isinstance(g, int) and g < 2):
                    act.wait_ge(y_stored[p], 8 * (g - p))
                nc.scalar.copy(y_sb[:, p, :], bank[1][C2:P, :]).then_inc(S["y_ready"], 1)

            def memory_rows(g, first=False):
                if not first:
                    act.wait_ge(S["G_ready"], g)
                for half in range(2):
                    act.wait_ge(S["mem_mm"], 2 * g + half + 1)
                    tiles = slice(2 * half, 2 * half + 2)
                    nc.scalar.activation(mem_l[:, tiles, C2:P], bank_jc(6 + half)[:, :, 2 * C2:3 * C2], ACT.Tanh, scale=0.5).then_inc(S["mem_act"], 1)
                    nc.scalar.copy(mem_r[:, tiles, 0:C2], bank_jc(6 + half)[:, :, C2:2 * C2]).then_inc(S["mem_act"], 1)

            def start_unit(half, t, stage):
                prev = before(half, t)
                if stage == 0:
                    act.wait_ge(S["x0_loaded"], 48 * (half * NT + t + 1))
                    act.wait_ge(S["conv_w_ready"], 1)
                for s in range(TRI):
                    if stage:
                        act.wait_ge(S["taps_done"], taps_at[half, t, stage - 1, s])
                    if s == 0 and prev:
                        if stage < 2:
                            act.wait_ge(S["taps_done"], taps_at[(*prev, stage + 1)])
                            act.wait_ge(tail_saved[stage], 48 * min(NT, half * NT + t))
                        else:
                            act.wait_ge(S["o_stored"], 48 * (half * NT + t))
                    place = t * TRI + s
                    dst = heads[:, s, :] if stage == 2 else win[stage + 1][:, s, HALF:2 * HALF]
                    nc.scalar.activation(dst, win[stage][:, s, HALF:2 * HALF], ACT.Identity,
                                         bias=conv_b[:, place, stage:stage + 1],
                                         scale=conv_w3[:, place, stage:stage + 1]).then_inc(S["conv_init"], 1)

            def split_o(g, p):
                act.wait_ge(o_loaded[p], 32 * (g // 2 + 1) if isinstance(g, int) else 16 * (g - p) + 32)
                if not (isinstance(g, int) and g == 0):
                    act.wait_ge(S["mixg_mm"], 2 * g)
                nc.scalar.copy(o_hi[:, :], big1[:, p, :]).then_inc(S["o_hi_ready"], 1)
                nc.scalar.copy(o_2[0:C2, :], big2[0:C2, p, :]).then_inc(S["o_hi_ready"], 1)

            def mix_gates(g):
                act.wait_ge(S["mixg_mm"], 2 * g + 1)
                if isinstance(g, int) and g == 0:
                    act.wait_ge(S["x_ready"], 2 * NG)
                else:
                    act.wait_ge(S["q_ready"], 2 * g)
                nc.scalar.activation(tg1[:, :], bank[4][:, :], ACT.Tanh, bias=mixg_bh[:, :], scale=0.5).then_inc(S["tg_ready"], 1)
                act.wait_ge(S["mixg_mm"], 2 * g + 2)
                nc.scalar.activation(tg2[:, :], bank[5][0:C2, :], ACT.Tanh, bias=mixg_bh2[:, :], scale=0.5).then_inc(S["tg_ready"], 1)

            def split_q(g):
                act.wait_ge(S["q_ready"], 2 * g + 1)
                if not (isinstance(g, int) and g == 0):
                    act.wait_ge(S["mix_mm"], 2 * g)
                nc.scalar.copy(q_hi[:, :], q1[:, :]).then_inc(S["q_hi_ready"], 1)
                act.wait_ge(S["q_ready"], 2 * g + 2)
                nc.scalar.copy(q_2[0:C2, :], q2[:, :]).then_inc(S["q_hi_ready"], 1)

            def gelu(g, c):
                act.wait_ge(S["in_mm"], NC * g + c + 1)
                if not (isinstance(g, int) and g == 0 and c < 2):
                    act.wait_ge(S["hid_lo_ready"], NC * g + c - 1)
                nc.scalar.activation(hid[:, c % 2, :], bank[2 + c % 2][:, :], ACT.Gelu, bias=fin_b_sb[:, c:c + 1]).then_inc(S["gelu_done"], 1)

            def high_hid(g, c):
                act.wait_ge(S["gelu_done"], NC * g + c + 1)
                if not (isinstance(g, int) and g == 0 and c < 3):
                    act.wait_ge(S["out_mm"], NC * g + c - 2)
                nc.scalar.copy(hid_hi[:, c % 3, :], hid[:, c % 2, :]).then_inc(S["hid_hi_ready"], 1)

            def beside(g, slot):
                for half, t, stage, k in parts_in(g, slot):
                    if k == 1:
                        start_unit(half, t, stage)

            def first_pass(g, p, convs=False, first=False, reads_before=True, last=False):
                gates(g, p, first)
                if convs:
                    beside(g, 0)
                if not last:
                    high_n(g + 1, 1 - p)
                if reads_before:
                    read_y(g - 2, p)
                if convs:
                    beside(g, 1)
                memory_rows(g, first)
                if convs:
                    beside(g, 2)
                    beside(g, 3)

            def second_pass(g, p, convs=False, ahead=2):
                if ahead:
                    mix_gates(g + 1)
                gelu(g, 0)
                high_hid(g, 0)
                if ahead:
                    split_q(g + 1)
                if convs:
                    beside(NG + g, 0)
                gelu(g, 1)
                high_hid(g, 1)
                if convs:
                    beside(NG + g, 1)
                for c in range(2, NC):
                    gelu(g, c)
                    high_hid(g, c)
                    if c == 2 and ahead == 2:
                        split_o(g + 2, p)
                    if c == NC - 1 and ahead:
                        high_n(g + 1, 1 - p, second=True)
                    if convs:
                        beside(NG + g, c)

            high_n(0, 0)
            first_pass(0, 0, first=True, reads_before=False)
            high_weights()
            first_pass(1, 1, reads_before=False)
            with act.Fori(1, B // 2) as i:
                for k in range(2):
                    first_pass(2 * i + k, k)
            for g in range(B, NG):
                first_pass(g, g % 2, convs=True, last=g == NG - 1)
            for g in (NG - 2, NG - 1):
                read_y(g, g % 2)
            for half, t, stage, k in PARTS[1][:LEAD]:
                if k == 1:
                    start_unit(half, t, stage)
            split_o(0, 0)
            mix_gates(0)
            split_q(0)
            split_o(1, 1)
            high_n(0, 0, second=True)
            for g in range(B):
                second_pass(g, g % 2, convs=True)
            with act.Fori(B // 2, NG // 2 - 1) as i:
                for k in range(2):
                    second_pass(2 * i + k, k)
            second_pass(NG - 2, 0, ahead=1)
            second_pass(NG - 1, 1, ahead=0)

        @block.vector
        def _(dve):
            nc.vector.memset(mem_r[:, :, C2:C2 + 1], 1.0 / CH).then_inc(S["consts"], 1)
            nc.vector.memset(zero_st[:, :], 0.0).then_inc(S["consts"], 1)
            nc.vector.memset(mem_rhs[:, :], 0.0).then_inc(S["consts"], 1)
            nc.vector.memset(big2[C2:C2 + 1, :, :], 1.0).then_inc(S["consts"], 1)
            dve.wait_ge(S["ld_idx"], 32)
            nc.vector.tensor_copy(xf[:, :], xi[:, :]).then_inc(S["idx_f"], 1)
            dve.wait_ge(S["idx_t"], 1)
            nc.vector.tensor_copy(idx[:, :], bank[0][:, 0:B * T // P]).then_inc(S["idx_ready"], 1)
            dve.wait_ge(S["pos_qt"], 2)
            nc.vector.tensor_copy(view(small, "qT1"), bank[1][:, 0:HD]).then_inc(S["pos_qs"], 1)
            nc.vector.tensor_copy(view(small, "qT2", C2), bank[2][0:C2, 0:HD]).then_inc(S["pos_qs"], 1)
            dve.wait_ge(S["pos_q"], 2)
            dve.wait_ge(S["ld_digits"], 32)
            tabs = view(small, "tabs", DIGIT_ROWS)
            for d in (1, 2):
                nc.vector.tensor_copy(tabs[d * DIGIT_AT:d * DIGIT_AT + HD, :],
                                      bank[3][0:HD, (d - 1) * C:d * C]).then_inc(S["pos_tab_ready"], 1)
            dve.wait_ge(S["ld_gate"], 48)
            for raw, _, _ in WEIGHTS["gate"]:
                nc.vector.tensor_scalar(raw[:, 0:P], raw[:, 0:P], 0.5, None, ALU.mult)
                nc.vector.tensor_scalar(raw[:, 2 * P:2 * P + C2], raw[:, 2 * P:2 * P + C2], 0.5, None, ALU.mult).then_inc(S["w_half"], 1)
            dve.wait_ge(S["w_half"], 2)
            for raw, high, _ in WEIGHTS["gate"]:
                nc.vector.tensor_copy(high, raw).then_inc(S["w_hi"], 1)
            dve.wait_ge(S["w_hi"], 2)
            for raw, high, low in WEIGHTS["gate"]:
                nc.vector.tensor_tensor(low, raw, high.bitcast(F32), ALU.subtract).then_inc(S["gate_ready"], 1)

            def memory_weights():
                dve.wait_ge(S["mem_w_mm"], 2)
                dve.wait_ge(S["ld_mem"], 16 * 7)
                dve.wait_ge(S["consts"], 4)
                nc.vector.scalar_tensor_tensor(mem_rhs[0:C2, 0:C2], bank[1][0:C2, 64:128], 0.5, mask_sb[:, :], ALU.mult, ALU.mult).then_inc(S["mem_w_ready"], 1)
                nc.vector.tensor_tensor(mem_rhs[0:C2, C2:2 * C2], bank[1][0:C2, 128:192], mask_sb[:, :], ALU.mult).then_inc(S["mem_w_ready"], 1)
                nc.vector.tensor_scalar(mem_rhs[0:C2, 2 * C2:3 * C2], mask_sb[:, :], view(small, "memg", C2), None, ALU.mult).then_inc(S["mem_w_ready"], 1)
                nc.vector.tensor_scalar(router_bh[:, :], router_bh[:, :], 0.5, None, ALU.mult).then_inc(S["w_half"], 1)

            def second_pass_weights():
                dve.wait_ge(S["ld_bias"], 16 * 4)
                dve.wait_ge(S["ld_mix"], 48)
                nc.vector.tensor_scalar(mixg_bh[:, :], mixg_bh[:, :], 0.5, None, ALU.mult).then_inc(S["w_half"], 1)
                nc.vector.tensor_scalar(mixg_bh2[:, :], mixg_bh2[:, :], 0.5, None, ALU.mult).then_inc(S["w_half"], 1)
                for raw, _, _ in WEIGHTS["mix"]:
                    nc.vector.tensor_scalar(raw, raw, 0.5, None, ALU.mult).then_inc(S["w_half"], 1)
                dve.wait_ge(S["ld_conv"], 16 * B)
                nc.vector.tensor_scalar(conv_w3[:, :, :], conv_w[:, :, :, TAPS - 1], 1.0, None, ALU.add).then_inc(S["conv_w_ready"], 1)

            def statistics(k, src, p, between=lambda n: None):
                for j in range(NJ):
                    i = nc.vector.bn_stats(stats[:, p, j, :], src[:, j, :])
                    if j == NJ - 1:
                        i.then_inc(S["stats_done"], 1)
                    between(j)
                dve.wait_ge(S["stats_done"], k + 1)
                mean_e, m2_e, mean_o, m2_o = (stats[:, p, :, n] for n in (1, 2, 4, 5))
                nc.vector.tensor_tensor(lnt[:, p, 0, :], mean_e, mean_o, ALU.subtract)
                nc.vector.scalar_tensor_tensor(lnt[:, p, 1, :], m2_e, C * EPS, m2_o, ALU.add, ALU.add)
                nc.vector.tensor_tensor(lnt[:, p, 2, :], mean_e, mean_o, ALU.add).then_inc(S["halves_done"], 1)
                between(NJ)
                dve.wait_ge(S["halves_done"], k + 1)
                nc.vector.tensor_scalar(mean[:, p, :], lnt[:, p, 2, :], 0.5, None, ALU.mult)
                nc.vector.scalar_tensor_tensor(lnt[:, p, 3, :], lnt[:, p, 0, :], 0.25, lnt[:, p, 0, :], ALU.mult, ALU.mult).then_inc(S["aggr_done"], 1)
                between(NJ + 1)
                dve.wait_ge(S["aggr_done"], k + 1)
                nc.vector.scalar_tensor_tensor(var[:, p, :], lnt[:, p, 1, :], 1.0 / C, lnt[:, p, 3, :], ALU.mult, ALU.add).then_inc(S["var_ready"], 1)

            def add_positions(g, p, half):
                dve.wait_ge(gathered[p], 16 * NJ * (g // 2 + 1) if isinstance(g, int) else 32 * (g - p) + 64)
                nc.vector.tensor_tensor(res[:, p, :, :], res[:, p, :, :], pos[:, half * NJ:(half + 1) * NJ, :], ALU.add).then_inc(S["h_ready"], 1)

            def embed(g, p, half):
                add_positions(g, p, half)
                dve.wait_ge(S["h_ready"], g + 1)
                statistics(g, res[:, p, :, :], p)

            def normalise(k, src, p, first=False):
                dve.wait_ge(S["rstd_ready"], k + 1)
                if not first:
                    dve.wait_ge(S["nT_ready"], k)
                for j in range(NJ):
                    i = nc.vector.tensor_scalar(nrm[:, j, :], src[:, j, :], mean[:, p, j:j + 1], rstd[:, p, j:j + 1], ALU.subtract, ALU.mult)
                i.then_inc(S["n_ready"], 1)

            def low_n(k, p):
                dve.wait_ge(S["nT_hi"], 2 * k + 1)
                nc.vector.tensor_tensor(n_lo[:, p, :], bank[0][:, :], n_hi[:, p, :].bitcast(F32), ALU.subtract)
                dve.wait_ge(S["nT_hi"], 2 * k + 2)
                nc.vector.tensor_tensor(n_2[C2:P, p, :], bank[1][0:C2, :], n_2[0:C2, p, :].bitcast(F32), ALU.subtract).then_inc(S["n_split"], 1)

            def gated1(g, p):
                if not (isinstance(g, int) and g < 2):
                    dve.wait_ge(x_stored[p], 24 * (g - p))
                dve.wait_ge(S["tanh_done"], 3 * g + 2)
                nc.vector.scalar_tensor_tensor(big1[:, p, :], tg1[:, :], 1.0, bank[2][:, :], ALU.add, ALU.mult).then_inc(S["x_ready"], 1)
                dve.wait_ge(S["tanh_done"], 3 * g + 3)
                nc.vector.tensor_scalar(hw_row[:, p, :], hw_row[:, p, :], 0.5, 0.5, ALU.mult, ALU.add).then_inc(S["hw_half"], 1)

            def gated2(g, p):
                if not (isinstance(g, int) and g < 2):
                    dve.wait_ge(S["y_mm"], g - 1)
                nc.vector.scalar_tensor_tensor(big2[0:C2, p, :], tg2[:, :], 1.0, bank[4][0:C2, :], ALU.add, ALU.mult).then_inc(S["x_ready"], 1)

            def memory_keys(g):
                for half in range(2):
                    dve.wait_ge(S["mem_act"], 4 * g + 2 * half + 2)
                    tiles = slice(2 * half, 2 * half + 2)
                    nc.vector.scalar_tensor_tensor(mem_l[:, tiles, 0:C2], mem_l[:, tiles, C2:P], 1.0,
                                                   bank_jc(6 + half)[:, :, 0:C2], ALU.add, ALU.mult).then_inc(S["gx_ready"], 1)

            def decays(g, p):
                dve.wait_ge(S["G_ready"], g + 1)
                if not (isinstance(g, int) and g == 0):
                    dve.wait_ge(S["masked"], 2 * g)
                for k in range(2):
                    i = nc.vector.tensor_scalar(dec[:, p, 4 * k:4 * k + 4], bank_g(3 + 2 * k)[C2:P, :, C2], -0.5, 0.5, ALU.mult, ALU.add)
                i.then_inc(S["dec_ready"], 1)

            def state_step(g, p, b, half, c):
                if c:
                    dve.wait_ge(S["step_done"], 8 * g + c)
                else:
                    dve.wait_ge(S["dec_ready"], g + 1)
                at = c % 2 * NJ + c // 2
                old = st[:, c - 1, :] if c else (zero_st[:, :] if half == 0 else st_mid[:, b, :])
                new = st[:, c, :] if c < 7 else st_mid[:, b, :]
                if half and c == 7:
                    new = st_end[:, :]
                nc.vector.scalar_tensor_tensor(new, old, dec[:, p, at:at + 1], bank_g(3 + 2 * (c % 2))[0:C2, c // 2, 0:C2],
                                               ALU.mult, ALU.add).then_inc(S["step_done"], 1)

            def recurrence(g, p, b, half, embed_next=True):
                decays(g, p)
                if embed_next:
                    dve.wait_ge(S["h_ready"], g + 4)
                    statistics(g + 3, res[:, 1 - p, :, :], 1 - p, between=lambda n: state_step(g, p, b, half, n))
                for c in range(NJ + 2 if embed_next else 0, 8):
                    state_step(g, p, b, half, c)

            def part_of_unit(half, t, stage, k):
                def last_write(s, before):
                    done = [taps_at[key] for key in (((half, t, stage, s, "tap", n)) for n in range(1, before)) if key in taps_at]
                    if done:
                        dve.wait_ge(S["taps_done"], done[-1])
                    else:
                        dve.wait_ge(S["conv_init"], init_at[half, t, stage, s])

                if k == FINISH:
                    dve.wait_ge(S["hy_loaded"], hy_at[half, t])
                    for s in range(TRI):
                        if t * TRI + s >= FIRST_MEM:
                            last_write(s, TAPS)
                            nc.vector.tensor_tensor(heads[:, s, :], heads[:, s, :], y_in[:, s, :], ALU.add).then_inc(S["taps_done"], 1)
                    for s in range(TRI):
                        if t * TRI + s >= FIRST_MEM:
                            dve.wait_ge(S["taps_done"], taps_at[half, t, stage, s, "y", 0])
                        else:
                            last_write(s, TAPS)
                        nc.vector.tensor_tensor(heads[:, s, :], heads[:, s, :], hw_in[:, s, :], ALU.mult).then_inc(S["taps_done"], 1)
                    return
                for s in range(TRI):
                    place = t * TRI + s
                    (lo, hi), (src_lo, src_hi) = tap_range(half, k * DILATIONS[ORDER[place]][stage])
                    if lo >= hi:
                        continue
                    last_write(s, k)
                    if half and stage and k == 1 and s == 0:
                        dve.wait_ge(tail_loaded[stage - 1], 48 * (t + 1))
                    if stage == 2:
                        acc = heads[:, s, lo - HALF:hi - HALF]
                    else:
                        acc = win[stage + 1][:, s, lo:hi]
                    nc.vector.scalar_tensor_tensor(acc, win[stage][:, s, src_lo:src_hi],
                                                   conv_w[:, place, stage, TAPS - 1 - k:TAPS - k],
                                                   acc, ALU.mult, ALU.add).then_inc(S["taps_done"], 1)

            def mixed(g, p):
                if isinstance(g, int) and g == 0:
                    dve.wait_ge(o_loaded[0], 32)
                else:
                    dve.wait_ge(S["q_lo_ready"], 2 * g)
                dve.wait_ge(S["tg_ready"], 2 * g + 1)
                nc.vector.scalar_tensor_tensor(q1[:, :], tg1[:, :], 1.0, big1[:, p, :], ALU.add, ALU.mult).then_inc(S["q_ready"], 1)
                dve.wait_ge(S["tg_ready"], 2 * g + 2)
                nc.vector.scalar_tensor_tensor(q2[:, :], tg2[:, :], 1.0, big2[0:C2, p, :], ALU.add, ALU.mult).then_inc(S["q_ready"], 1)

            def attended(g, p):
                dve.wait_ge(S["res_biased"], g + 1)
                if not (isinstance(g, int) and g < 2):
                    dve.wait_ge(out_stored[p], 8 * (g - p))
                for k in range(2):
                    dve.wait_ge(S["mix_mm"], 2 * g + k + 1)
                    i = nc.vector.tensor_tensor(h2[:, p, 2 * k:2 * k + 2, :], bank_jc(4 + k), res[:, p, 2 * k:2 * k + 2, :], ALU.add)
                i.then_inc(S["h2_ready"], 1)
                dve.wait_ge(S["h2_ready"], g + 1)
                statistics(NG + g, h2[:, p, :, :], p)

            def low_hid(g, c):
                dve.wait_ge(S["hid_hi_ready"], NC * g + c + 1)
                nc.vector.tensor_tensor(hid_lo[:, c % 3, :], hid[:, c % 2, :], hid_hi[:, c % 3, :].bitcast(F32), ALU.subtract).then_inc(S["hid_lo_ready"], 1)

            def result(g, p):
                dve.wait_ge(S["out_mm"], NC * g + NC)
                for k in range(2):
                    i = nc.vector.tensor_tensor(h2[:, p, 2 * k:2 * k + 2, :], bank_jc(6 + k), h2[:, p, 2 * k:2 * k + 2, :], ALU.add)
                i.then_inc(S["out_ready"], 1)

            def beside(g, slot):
                for part in parts_in(g, slot):
                    part_of_unit(*part)

            def first_pass(g, p, b, half):
                if half == 0 or b + 1 < B:
                    normalise(g + 1, res[:, 1 - p, :, :], 1 - p)
                if half == 0:
                    add_positions(g + 2, p, 0 if not isinstance(g, int) or g + 2 < B else 1)
                elif b + 2 < B:
                    add_positions(g + 2, p, 1)
                gated1(g, p)
                gated2(g, p)
                if half:
                    beside(g, 0)
                if half == 0 or b + 1 < B:
                    low_n(g + 1, 1 - p)
                if half:
                    beside(g, 1)
                if isinstance(g, int) and g == 0:
                    dve.wait_ge(S["h_ready"], 3)
                    statistics(2, res[:, 0, :, :], 0)
                elif isinstance(g, int) and g == B:
                    recurrence(g - 1, 1 - p, B - 1, 0)
                else:
                    recurrence(g - 1, 1 - p, b - 1, half, embed_next=half == 0 or b + 2 < B)
                if half:
                    beside(g, 2)
                memory_keys(g)
                if half:
                    beside(g, 3)

            def second_pass(g, p, convs=False, last=False, before_last=False):
                for c in range(NC):
                    if c == 3 and not last:
                        attended(g + 1, 1 - p)
                    if c == 4 and not last:
                        normalise(NG + g + 1, h2[:, 1 - p, :, :], 1 - p)
                    low_hid(g, c)
                    if c == NC - 1:
                        if not last:
                            low_n(NG + g + 1, 1 - p)
                            if not before_last:
                                mixed(g + 2, p)
                        result(g, p)
                    if convs:
                        beside(NG + g, c)

            memory_weights()
            dve.wait_ge(S["pos_ready"], 2)
            embed(0, 0, 0)
            normalise(0, res[:, 0, :, :], 0, first=True)
            embed(1, 1, 0)
            low_n(0, 0)
            second_pass_weights()
            first_pass(0, 0, 0, 0)
            with dve.Fori(0, 2) as i:
                for k in range(2):
                    g = 2 * i + k + 1
                    first_pass(g, 1 - k, g, 0)
            for g in range(5, B):
                first_pass(g, g % 2, g, 0)
            for g in range(B, NG):
                first_pass(g, g % 2, g - B, 1)
            recurrence(NG - 1, 1, B - 1, 1, embed_next=False)
            for part in PARTS[1][:LEAD]:
                part_of_unit(*part)
            mixed(0, 0)
            attended(0, 0)
            normalise(NG, h2[:, 0, :, :], 0)
            low_n(NG, 0)
            mixed(1, 1)
            for g in range(B):
                second_pass(g, g % 2, convs=True)
            with dve.Fori(B // 2, NG // 2 - 1) as i:
                for k in range(2):
                    second_pass(2 * i + k, k)
            second_pass(NG - 2, 0, before_last=True)
            second_pass(NG - 1, 1, last=True)

        @block.tensor
        def _(pe):
            def mm(dst, lhsT, rhs, start, stop):
                return nc.tensor.matmul(dst, lhsT, rhs, start=start, stop=stop)

            def mm5(dst, pairs):
                for n, (lhsT, rhs) in enumerate(pairs):
                    i = mm(dst, lhsT, rhs, n == 0, n == len(pairs) - 1)
                return i

            pe.wait_ge(S["idx_f"], 1)
            nr = B * T // P
            nc.tensor.transpose(bank[0][:, 0:nr], xf[:, :], id_sb[0:nr, 0:nr]).then_inc(S["idx_t"], 1)
            pe.wait_ge(S["ld_carry"], 16 * 4)
            carry = [view(small, "carry1"), view(small, "carry2", C2)]
            pT = [view(small, "posT1"), view(small, "posT2", C2)]
            qT = [view(small, "qT1"), view(small, "qT2", C2)]
            for m, (lo, hi) in enumerate(((0, P), (P, C))):
                for k in range(2):
                    i = mm(bank[1 + m][0:hi - lo, 0:HD], carry[k][:, lo:hi], pT[k], k == 0, k == 1)
                i.then_inc(S["pos_qt"], 1)
            for k in range(2):
                i = mm(bank[3][0:HD, 0:C], pT[k], carry[k], k == 0, k == 1)
            i.then_inc(S["pos_q"], 1)
            pe.wait_ge(S["pos_qs"], 2)
            for k in range(2):
                i = mm(bank[3][0:HD, C:2 * C], qT[k], carry[k], k == 0, k == 1)
            i.then_inc(S["pos_q"], 1)
            pe.wait_ge(S["pos_tab_ready"], 2)
            for r in range(T // P):
                i = mm(bank[4 + r // 2][:, (r % 2) * C:(r % 2 + 1) * C], digit_sb[:, r * P:(r + 1) * P],
                       view(small, "tabs", DIGIT_ROWS), True, True)
                if r % 2:
                    i.then_inc(S["pos_mm"], 1)
            pe.wait_ge(S["ld_mem"], 16 * 7)
            mm(bank[1][0:C2, 64:128], view(small, "memk", HD), view(small, "memq", HD), True, True).then_inc(S["mem_w_mm"], 1)
            mm(bank[1][0:C2, 128:192], view(small, "memv"), view(small, "memo"), True, True).then_inc(S["mem_w_mm"], 1)

            def transposes(k):
                pe.wait_ge(S["n_ready"], k + 1)
                if not (isinstance(k, int) and k == 0):
                    pe.wait_ge(S["n_split"], k)
                for j in range(NJ):
                    nc.tensor.transpose(bank[0][:, j * P:(j + 1) * P], nrm[:, j, 0:P], id_sb[:, :])
                for j in range(NJ):
                    i = nc.tensor.transpose(bank[1][0:C2, j * P:(j + 1) * P], nrm[:, j, P:C], id_sb[:, :])
                i.then_inc(S["nT_ready"], 1)

            def gate(g, p, b, lo, hi):
                mm5(bank[b][0:hi - lo, :], [(gate_h[:, lo:hi], n_hi[:, p, :]), (gate_l[:, lo:hi], n_hi[:, p, :]),
                                            (gate_h[:, lo:hi], n_lo[:, p, :]), (gate2_h[:, lo:hi], n_2[:, p, :]),
                                            (gate2_l[:, lo:hi], n_2[:, p, :])]).then_inc(S["gate_mm"], 1)

            def gates(g, p, first=False, reads_before=True):
                pe.wait_ge(S["n_split"], g + 1)
                if not first:
                    pe.wait_ge(S["x_ready"], 2 * g)
                gate(g, p, 4, 2 * P, 3 * P)
                gate(g, p, 2, 0, P)
                if reads_before:
                    pe.wait_ge(S["step_done"], 8 * (g - 1))
                gate(g, p, 3, P, 2 * P)
                gate(g, p, 5, 3 * P, GW)
                if reads_before:
                    reads_can_start(g - 2)

            def memory_rows(g, p, first=False):
                pe.wait_ge(S["x_ready"], 2 * g + 2)
                for j in range(NJ):
                    if j % 2 == 0 and not first:
                        pe.wait_ge(S["gx_ready"], 2 * g - 1 + j // 2)
                    i = mm(bank_jc(6 + j // 2)[:, j % 2, :], big2[:, p, j * P:(j + 1) * P], mem_rhs[:, :], True, True)
                    if j % 2:
                        i.then_inc(S["mem_mm"], 1)

            def writes(g):
                pe.wait_ge(S["tanh_done"], 3 * min(NG, g + 2) if isinstance(g, int) else 3 * g + 6)
                pe.wait_ge(S["gx_ready"], 2 * g + 2)
                for j in range(NJ):
                    for r in range(2):
                        rows = slice(r * CH, (r + 1) * CH)
                        i = mm(bank_g(3 + 2 * r)[:, j, :], mem_l[rows, j, :], mem_r[rows, j, :], True, True)
                i.then_inc(S["G_ready"], 1)

            def reads_can_start(g):
                pe.wait_ge(S["masked"], 2 * g + 2)
                if not (isinstance(g, int) and g == 0):
                    pe.wait_ge(S["y_ready"], g)

            def reads(g, p):
                for c in range(8):
                    i = mm(bank[1][C2:P, c * CH:(c + 1) * CH], st_bd[:, c, :], big2[0:C2, p, c * CH:(c + 1) * CH], True, True)
                i.then_inc(S["y_mm"], 1)

            def first_pass(g, p, reads_before=True, last=False):
                gates(g, p, reads_before=reads_before)
                if not last:
                    transposes(g + 1)
                if reads_before:
                    reads(g - 2, p)
                writes(g - 1)
                memory_rows(g, p)

            def mix_gates(g):
                pe.wait_ge(S["o_lo_ready"], 2 * g + 2)
                if not (isinstance(g, int) and g == 0):
                    pe.wait_ge(S["h2_ready"], g)
                for b, lo, hi in ((4, 0, P), (5, P, C)):
                    mm5(bank[b][0:hi - lo, :], [(mixg_h[:, lo:hi], o_hi[:, :]), (mixg_l[:, lo:hi], o_hi[:, :]),
                                                (mixg_h[:, lo:hi], o_lo[:, :]), (mixg2_h[:, lo:hi], o_2[:, :]),
                                                (mixg2_l[:, lo:hi], o_2[:, :])]).then_inc(S["mixg_mm"], 1)

            def mix(g):
                pe.wait_ge(S["q_lo_ready"], 2 * g + 2)
                for j in range(NJ):
                    cut = slice(j * P, (j + 1) * P)
                    i = mm5(bank_jc(4 + j // 2)[:, j % 2, :],
                            [(q_hi[:, cut], mix_h[:, :]), (q_hi[:, cut], mix_l[:, :]), (q_lo[:, cut], mix_h[:, :]),
                             (q_2[:, cut], mix2_h[:, :]), (q_2[:, cut], mix2_l[:, :])])
                    if j % 2:
                        i.then_inc(S["mix_mm"], 1)

            def ffn_in(g, c, p):
                if c == 0:
                    pe.wait_ge(S["n_split"], NG + g + 1)
                if not (isinstance(g, int) and g == 0 and c < 2):
                    pe.wait_ge(S["gelu_done"], NC * g + c - 1)
                cut = slice(c * P, (c + 1) * P)
                mm5(bank[2 + c % 2][:, :], [(fin_h[:, cut], n_hi[:, p, :]), (fin_l[:, cut], n_hi[:, p, :]),
                                            (fin_h[:, cut], n_lo[:, p, :]), (fin2_h[:, cut], n_2[:, p, :]),
                                            (fin2_l[:, cut], n_2[:, p, :])]).then_inc(S["in_mm"], 1)

            def ffn_out(g, c):
                if c == 0 and not (isinstance(g, int) and g == 0):
                    pe.wait_ge(S["out_ready"], g)
                pe.wait_ge(S["hid_lo_ready"], NC * g + c + 1)
                for j in range(NJ):
                    cut = slice(j * P, (j + 1) * P)
                    dst = bank_jc(6 + j // 2)[:, j % 2, :]
                    for n, (a, w) in enumerate(((hid_hi, fout_h), (hid_hi, fout_l), (hid_lo, fout_h))):
                        i = nc.tensor.matmul(dst, a[:, c % 3, cut], w[:, c, :], start=c == 0 and n == 0 and j % 2 == 0,
                                             stop=c == NC - 1 and n == 2, skip_group_check=True)
                i.then_inc(S["out_mm"], 1)

            def second_pass(g, p, ahead=2):
                ffn_in(g, 1, p)
                ffn_in(g, 2, p)
                ffn_out(g, 0)
                ffn_in(g, 3, p)
                ffn_out(g, 1)
                if ahead:
                    mix(g + 1)
                ffn_in(g, 4, p)
                ffn_out(g, 2)
                ffn_in(g, 5, p)
                ffn_out(g, 3)
                if ahead:
                    transposes(NG + g + 1)
                ffn_out(g, 4)
                if ahead == 2:
                    mix_gates(g + 2)
                if ahead:
                    ffn_in(g + 1, 0, 1 - p)
                ffn_out(g, 5)

            pe.wait_ge(S["mem_w_ready"], 3)
            transposes(0)
            pe.wait_ge(S["gate_ready"], 2)
            pe.wait_ge(S["pos_ready"], 4)
            gates(0, 0, first=True, reads_before=False)
            transposes(1)
            pe.wait_ge(S["ld_membg"], 16)
            memory_rows(0, 0, first=True)
            first_pass(1, 1, reads_before=False)
            first_pass(2, 0)
            first_pass(3, 1)
            with pe.Fori(2, NG // 2 - 1) as i:
                for k in range(2):
                    first_pass(2 * i + k, k)
            first_pass(NG - 2, 0)
            first_pass(NG - 1, 1, last=True)
            reads_can_start(NG - 2)
            reads(NG - 2, 0)
            pe.wait_ge(S["step_done"], 8 * (NG - 1))
            writes(NG - 1)
            reads_can_start(NG - 1)
            reads(NG - 1, 1)
            pe.wait_ge(S["step_done"], 8 * NG)
            pe.wait_ge(S["gx_ready"], 2 * NG)
            pe.wait_ge(S["weights_ready"], len(SECOND_WEIGHTS))
            mix_gates(0)
            mix(0)
            mix_gates(1)
            transposes(NG)
            ffn_in(0, 0, 0)
            second_pass(0, 0)
            second_pass(1, 1)
            with pe.Fori(1, NG // 2 - 1) as i:
                for k in range(2):
                    second_pass(2 * i + k, k)
            second_pass(NG - 2, 0, ahead=1)
            second_pass(NG - 1, 1, ahead=0)


FINISH = TAPS
PARTS = [[(half, t, stage, k) for t in range(NT) for stage in range(3)
          for k in list(range(1, TAPS)) + ([FINISH] if stage == 2 else [])] for half in range(2)]
LEAD = 2 * (TAPS - 1)
FIRST_SLOTS = (0, 1, 2, 3, 3)


def is_last(half, t, stage, k):
    return k == (FINISH if stage == 2 else TAPS - 1)


def parts_in(g, slot):
    if g < NG:
        n = len(PARTS[0]) // B
        at = n * (g - B)
        return [PARTS[0][at + i] for i in range(n) if FIRST_SLOTS[i] == slot]
    at = LEAD + NC * (g - NG) + slot
    return PARTS[1][at:at + 1]


_IN_ORDER = ["x", "tok", "posT", "pos_tab", "carryT", "conv", "memq", "memk", "memv", "memo", "memg", "membg", "gateT",
             "router_b", "mixgT", "mixg_b", "mixT", "mix_b", "finT", "fin_b", "fout", "digits", "ident", "mask"]


def _layout(i):
    import numpy as np

    def order(a, axis):
        parts = np.split(a, NH, axis=axis)
        return np.concatenate([parts[h] for h in ORDER], axis=axis)

    gate = np.asarray(i["L0_attn_gate_w"])
    xg, gt = order(gate[0:C], 0), order(gate[C:2 * C], 0)
    router = np.asarray(i["L0_attn_router_w"])[ORDER]
    mixg = order(order(np.asarray(i["L0_attn_mixg_w"]), 0), 1)
    conv_w = np.asarray(i["L0_attn_conv_w"])[ORDER].transpose(2, 0, 1, 3).reshape(HD, -1)
    conv_b = np.asarray(i["L0_attn_conv_b"])[ORDER].transpose(2, 0, 1).reshape(HD, -1)
    wq, wk, wv, wo = (np.asarray(i[f"L0_attn_mem_W{n}"]) for n in ("q", "k", "v", "out"))
    u = T - 1 - np.arange(T)
    digits = np.zeros((DIGIT_ROWS, T), np.float32)
    for d in range(3):
        digits[DIGIT_AT * d:DIGIT_AT * d + HD] = np.arange(HD)[:, None] == (u // HD ** d % HD)[None, :]
    pos_tab = np.zeros((DIGIT_ROWS, C), np.float32)
    pos_tab[0:HD] = np.asarray(i["L0_tok_pos_table"])
    lane = np.arange(C2) // HD
    return {
        "x": np.asarray(i["x"]),
        "tok": np.asarray(i["L0_tok_tok_table"]),
        "posT": np.asarray(i["L0_tok_pos_table"]).T,
        "pos_tab": pos_tab,
        "carryT": np.asarray(i["L0_tok_carry_W"]).T,
        "conv": np.concatenate([conv_w, conv_b], axis=1),
        "memq": wq.transpose(1, 0, 2).reshape(HD, C2),
        "memk": wk.transpose(1, 0, 2).reshape(HD, C2),
        "memv": wv.transpose(1, 0, 2).reshape(P, C2),
        "memo": wo.transpose(2, 0, 1).reshape(P, C2),
        "memg": np.asarray(i["L0_attn_mem_Wg_w"]).reshape(C2, 1),
        "membg": np.repeat(np.asarray(i["L0_attn_mem_Wg_b"]).reshape(1, NM), HD, axis=1),
        "gateT": np.concatenate([xg[0:P], gt[0:P], xg[P:C], gt[P:C], router], axis=0).T,
        "router_b": np.asarray(i["L0_attn_router_b"])[ORDER].reshape(NH, 1),
        "mixgT": mixg.T,
        "mixg_b": order(np.asarray(i["L0_attn_mixg_b"]), 0).reshape(C, 1),
        "mixT": order(np.asarray(i["L0_attn_mix_w"]), 1).T,
        "mix_b": np.asarray(i["L0_attn_mix_b"]),
        "finT": np.asarray(i["L0_ffn_in_weight"]).T,
        "fin_b": np.asarray(i["L0_ffn_in_bias"]).reshape(NC, P).T,
        "fout": np.asarray(i["L0_ffn_out_weight"]),
        "digits": digits,
        "ident": np.eye(P, dtype=np.float32),
        "mask": (lane[:, None] == lane[None, :]).astype(np.float32),
    }


def kernel(**inputs):
    import numpy as np
    import concourse.bacc as bacc
    from concourse.bass_utils import run_bass_kernel_spmd as run

    nc = bacc.Bacc("TRN2", target_bir_lowering=False, num_devices=1)
    operands = _layout(inputs)
    arrays, args = {}, []
    for name in _IN_ORDER:
        a = np.ascontiguousarray(operands[name])
        arrays[f"in_{name}"] = a
        args.append(nc.dram_tensor(f"in_{name}", a.shape, mybir.dt.from_np(a.dtype), kind="ExternalInput").ap())
    args.append(nc.dram_tensor("out_h", (B, T, C), F32, kind="ExternalOutput").ap())
    lm_tower(nc, *args)
    r = run(nc, [arrays], core_ids=[0])
    return r.results[0]["out_h"]
```

```python
from contextlib import ExitStack

import concourse.bass as bass
from concourse import mybir

F32 = mybir.dt.float32
F32R = mybir.dt.float32r
I32 = mybir.dt.int32
U32 = mybir.dt.uint32
ALU = mybir.AluOpType
ACT = mybir.ActivationFunctionType

P = 128
C = 192
C2 = C - P
B, T = 8, 1024
HALF = 512
NG = B * T // HALF
NJ = HALF // P
HD = 16
NH = 12
HID = 768
NC = HID // P
CH = 64
EPS = 1e-5
TAPS = 4
DILATIONS = [(1, 2, 4), (1, 1, 1), (4, 8, 16), (8, 16, 32), (32, 64, 128), (64, 128, 64),
             (64, 128, 256), (1, 100, 200), (1, 125, 250), (1, 256, 512), (3, 9, 27), (5, 25, 125)]
MEM_HEADS = (6, 7, 8, 9)
ORDER = [h for h in range(NH) if h not in MEM_HEADS] + list(MEM_HEADS)
FIRST_MEM = NH - len(MEM_HEADS)
NM = len(MEM_HEADS)
TRI = 3
NT = NH // TRI
DIGIT_AT = 32
DIGIT_ROWS = 2 * DIGIT_AT + HD
GW = 2 * C + NH


def history(place, stage):
    return min(HALF, (TAPS - 1) * DILATIONS[ORDER[place]][stage])


def tap_range(half, shift):
    lo = HALF + shift if half == 0 else max(HALF, shift)
    return (lo, 2 * HALF), (lo - shift, 2 * HALF - shift)


def lm_tower(nc, x, tok, posT, pos_tab, carryT, conv, memq, memk, memv, memo, memg, membg,
             gateT, router_b, mixgT, mixg_b, mixT, mix_b, finT, fin_b, fout, digits, ident, mask, out):
    with ExitStack() as ctx:
        def sb(name, shape, dt=F32):
            return ctx.enter_context(nc.sbuf_tensor(name, shape, dt))

        def sem(name):
            return ctx.enter_context(nc.semaphore(name))

        def scratch(name, shape):
            return nc.dram_tensor(name, shape, F32, kind="Internal").ap()

        bank = [ctx.enter_context(nc.psum_tensor(f"bank{i}", [P, 512], F32)) for i in range(8)]

        h_dram = scratch("h_dram", (NG, P, NJ * C))
        x_dram = scratch("x_dram", (B, C, T))
        hw_dram = scratch("hw_dram", (NH, B, T))
        y_dram = scratch("y_dram", (B, C2, T))
        o_dram = scratch("o_dram", (B, C, T))
        tail_dram = [scratch(f"tail{s}_dram", (NH, P, HALF)) for s in range(2)]

        id_sb = sb("id_sb", [P, P])
        mask_sb = sb("mask_sb", [C2, C2])
        zero_st = sb("zero_st", [C2, C2])
        xi = sb("xi", [B * T // P, P], I32)
        xf = sb("xf", [B * T // P, P])
        idx = sb("idx", [P, B * T // P], I32)
        pos = sb("pos", [P, T // P, C])
        gate_h, gate_l = sb("gate_h", [P, GW], F32R), sb("gate_l", [P, GW], F32R)
        gate2_h, gate2_l = sb("gate2_h", [P, GW], F32R), sb("gate2_l", [P, GW], F32R)
        mixg_h, mixg_l = sb("mixg_h", [P, C], F32R), sb("mixg_l", [P, C], F32R)
        mixg2_h, mixg2_l = sb("mixg2_h", [P, C], F32R), sb("mixg2_l", [P, C], F32R)
        mix_h, mix_l = sb("mix_h", [P, C], F32R), sb("mix_l", [P, C], F32R)
        mix2_h, mix2_l = sb("mix2_h", [P, C], F32R), sb("mix2_l", [P, C], F32R)
        fin_h, fin_l = sb("fin_h", [P, HID], F32R), sb("fin_l", [P, HID], F32R)
        fin2_h, fin2_l = sb("fin2_h", [P, HID], F32R), sb("fin2_l", [P, HID], F32R)
        fout_h, fout_l = sb("fout_h", [P, NC, C], F32R), sb("fout_l", [P, NC, C], F32R)
        conv_sb = sb("conv_sb", [P, NH * 3 * (TAPS + 1)])
        conv_w = conv_sb[:, 0:NH * 3 * TAPS].rearrange("p (h s k) -> p h s k", h=NH, s=3)
        conv_b = conv_sb[:, NH * 3 * TAPS:].rearrange("p (h s) -> p h s", h=NH)
        conv_w3 = sb("conv_w3", [P, NH, 3])
        mem_rhs = sb("mem_rhs", [C2 + 1, 3 * C2])
        router_bh = sb("router_bh", [NH, 1])
        mixg_bh, mixg_bh2 = sb("mixg_bh", [P, 1]), sb("mixg_bh2", [C2, 1])
        mix_b_sb = sb("mix_b_sb", [P, C])
        fin_b_sb = sb("fin_b_sb", [P, NC])
        warm = sb("warm", [P, 1])

        win = [sb(f"win{s}", [P, TRI, 2 * HALF]) for s in range(3)]
        heads = sb("heads", [P, TRI, HALF])
        hw_in = sb("hw_in", [P, TRI, HALF])
        y_in = sb("y_in", [P, TRI, HALF])

        res = sb("res", [P, 2, NJ, C])
        stats = sb("stats", [P, 2, NJ, 6])
        lnt = sb("lnt", [P, 2, 4, NJ])
        neg_mean = sb("neg_mean", [P, 2, NJ])
        centre = sb("centre", [P, 2, NJ])
        var = sb("var", [P, 2, NJ])
        rstd = sb("rstd", [P, 2, NJ])
        half_neg = sb("half_neg", [P, NJ])
        nrm = sb("nrm", [P, NJ, C])
        n_hi = sb("n_hi", [P, 2, HALF], F32R)
        n_lo = sb("n_lo", [P, 2, HALF], F32R)
        n_2 = sb("n_2", [P, 2, HALF], F32R)
        big1 = sb("big1", [P, 2, HALF])
        big2 = sb("big2", [C2 + 1, 2, HALF])
        tg1, tg2 = sb("tg1", [P, HALF]), sb("tg2", [C2, HALF])
        hw_row = sb("hw_row", [NH, 2, HALF])
        mem_l = sb("mem_l", [P, NJ, P])
        mem_r = sb("mem_r", [P, NJ, C2 + 1])
        dec = sb("dec", [C2, 2, 8])
        st = sb("st", [C2, 7, C2])
        st_end = sb("st_end", [C2, C2])
        st_mid = sb("st_mid", [C2, B, C2])
        st_bd = sb("st_bd", [C2, 8, C2])
        y_sb = sb("y_sb", [C2, 2, HALF])
        o1, o2 = sb("o1", [P, 2, HALF]), sb("o2", [C2, 2, HALF])
        o_hi, o_lo, o_2 = sb("o_hi", [P, HALF], F32R), sb("o_lo", [P, HALF], F32R), sb("o_2", [P, HALF], F32R)
        q1, q2 = sb("q1", [P, HALF]), sb("q2", [C2, HALF])
        q_hi, q_lo, q_2 = sb("q_hi", [P, HALF], F32R), sb("q_lo", [P, HALF], F32R), sb("q_2", [P, HALF], F32R)
        h2 = sb("h2", [P, 2, NJ, C])
        hid = sb("hid", [P, 2, HALF])
        hid_hi, hid_lo = sb("hid_hi", [P, 3, HALF], F32R), sb("hid_lo", [P, 3, HALF], F32R)
        raw1 = win[0][:, :, :].rearrange("p a b -> p (a b)")
        raw2 = win[1][:, :, :].rearrange("p a b -> p (a b)")
        small = win[2][:, :, :].rearrange("p a b -> p (a b)")

        names = """ld_idx ld_carry ld_digits ld_mem ld_membg ld_gate ld_mixg ld_mix ld_fin ld_fout ld_conv ld_bias
            idx_f idx_t idx_ready pos_qt pos_qs pos_q pos_tab_ready pos_mm pos_ready mem_w_mm mem_w_ready consts gate_ready conv_w_ready
            w_half w_hi weights_ready pool_consts
            h_ready stats_done halves_done aggr_done var_ready rstd_ready centre_ready n_ready nT_ready nT_hi n_split
            gate_mm tanh_done hw_half x_ready mem_mm mem_act gx_ready G_ready dec_ready step_done masked y_mm y_ready
            gathered0 gathered1 h_stored0 h_stored1 x_stored0 x_stored1 y_stored0 y_stored1
            x0_loaded hy_loaded conv_init taps_done finished tail0_saved tail1_saved tail0_loaded tail1_loaded o_stored
            o_loaded0 o_loaded1 r_loaded0 r_loaded1 o_hi_ready o_lo_ready mixg_mm tg_ready q_ready q_hi_ready q_lo_ready
            res_biased mix_mm h2_ready in_mm gelu_done hid_hi_ready hid_lo_ready out_mm out_ready out_stored0 out_stored1""".split()
        S = {n: sem(n) for n in names}
        gathered, h_stored, x_stored, y_stored = ([S[f"{n}{p}"] for p in range(2)] for n in
                                                  ("gathered", "h_stored", "x_stored", "y_stored"))
        o_loaded, r_loaded, out_stored = ([S[f"{n}{p}"] for p in range(2)] for n in
                                          ("o_loaded", "r_loaded", "out_stored"))
        tail_saved = [S["tail0_saved"], S["tail1_saved"]]
        tail_loaded = [S["tail0_loaded"], S["tail1_loaded"]]

        spans, at1, at2 = {}, 0, 0
        for name, n1, n2 in (("gate", GW, GW), ("mixg", C, C), ("mix", C, C), ("fin", HID, HID), ("fout", NC * C, 0)):
            spans[name] = (raw1[:, at1:at1 + n1], raw2[:, at2:at2 + n2])
            at1, at2 = at1 + n1, at2 + n2
        assert at1 <= TRI * 2 * HALF and at2 <= TRI * 2 * HALF

        WEIGHTS = {"gate": ((spans["gate"][0], gate_h[:, :], gate_l[:, :]), (spans["gate"][1], gate2_h[:, :], gate2_l[:, :])),
                   "mixg": ((spans["mixg"][0], mixg_h[:, :], mixg_l[:, :]), (spans["mixg"][1], mixg2_h[:, :], mixg2_l[:, :])),
                   "mix": ((spans["mix"][0], mix_h[:, :], mix_l[:, :]), (spans["mix"][1], mix2_h[:, :], mix2_l[:, :])),
                   "fin": ((spans["fin"][0], fin_h[:, :], fin_l[:, :]), (spans["fin"][1], fin2_h[:, :], fin2_l[:, :])),
                   "fout": ((spans["fout"][0], fout_h[:, :, :].rearrange("p k c -> p (k c)"),
                             fout_l[:, :, :].rearrange("p k c -> p (k c)")),)}

        SECOND_WEIGHTS = [w for name in ("mixg", "mix", "fin", "fout") for w in WEIGHTS[name]]

        cols, at = {}, 0
        for name, n in (("carry1", C), ("carry2", C), ("posT1", HD), ("posT2", HD), ("qT1", HD), ("qT2", HD),
                        ("memk", C2), ("memq", C2), ("memv", C2), ("memo", C2), ("memg", 1), ("tabs", C)):
            cols[name] = slice(at, at + n)
            at += n
        digit_sb = heads[0:DIGIT_ROWS, :, :].rearrange("p a b -> p (a b)")[:, 0:T]

        taps_at, init_at, hy_at, finished_at = {}, {}, {}, {}
        n_taps = n_init = n_hy = n_finished = 0
        for half in range(2):
            for t in range(NT):
                n_hy += 16 * TRI
                n_hy += 16 * sum(t * TRI + s >= FIRST_MEM for s in range(TRI))
                hy_at[half, t] = n_hy
                for stage in range(3):
                    for s in range(TRI):
                        n_init += 1
                        init_at[half, t, stage, s] = n_init
                    ops = []
                    for k in range(1, TAPS):
                        for s in range(TRI):
                            shift = k * DILATIONS[ORDER[t * TRI + s]][stage]
                            (lo, hi), _ = tap_range(half, shift)
                            if lo < hi:
                                ops.append((s, "tap", k))
                    for s, what, k in ops:
                        n_taps += 1
                        taps_at[half, t, stage, s, what, k] = n_taps
                        taps_at[half, t, stage, s] = n_taps
                    taps_at[half, t, stage] = n_taps
                n_finished += TRI + sum(t * TRI + s >= FIRST_MEM for s in range(TRI))
                finished_at[half, t] = n_finished

        def before(half, t):
            n = half * NT + t - 1
            return None if n < 0 else (n // NT, n % NT)

        def view(ap, name, rows=P):
            return ap[0:rows, cols[name]]

        def bank_jc(i):
            return bank[i][:, 0:2 * C].rearrange("p (j c) -> p j c", j=2)

        def bank_g(i):
            return bank[i][:, 0:4 * (C2 + 1)].rearrange("p (c n) -> p c n", c=4)

        block = ctx.enter_context(nc.Block())

        @block.sync
        def _(sp):
            sp.dma_start(xi[:, :], x.rearrange("b (r p) -> (b r) p", p=P)).then_inc(S["ld_idx"], 16)
            sp.dma_start(id_sb[:, :], ident).then_inc(S["ld_idx"], 16)
            for dst, src in ((view(small, "carry1"), carryT[0:P, :]), (view(small, "carry2", C2), carryT[P:C, :]),
                             (view(small, "posT1"), posT[0:P, :]), (view(small, "posT2", C2), posT[P:C, :])):
                sp.dma_start(dst, src).then_inc(S["ld_carry"], 16)
            for dst, src in ((view(small, "tabs", DIGIT_ROWS), pos_tab), (digit_sb, digits)):
                sp.dma_start(dst, src).then_inc(S["ld_digits"], 16)
            for name, src in (("gate", gateT), ("mixg", mixgT), ("mix", mixT), ("fin", finT)):
                first, second = spans[name]
                sp.dma_start(first, src[0:P, :]).then_inc(S[f"ld_{name}"], 16)
                sp.dma_start(second[0:C2, :], src[P:C, :]).then_inc(S[f"ld_{name}"], 16)
                sp.dma_start(second[C2:P, :], src[P:C, :]).then_inc(S[f"ld_{name}"], 16)
            sp.dma_start(spans["fout"][0].rearrange("p (k c) -> p k c", k=NC),
                         fout.rearrange("(k p) c -> p k c", p=P)).then_inc(S["ld_fout"], 16)
            for dst, src in ((mixg_bh[:, :], mixg_b[0:P, :]), (mixg_bh2[:, :], mixg_b[P:C, :]),
                             (mix_b_sb[:, :], mix_b.partition_broadcast(P)), (fin_b_sb[:, :], fin_b)):
                sp.dma_start(dst, src).then_inc(S["ld_bias"], 16)
            for b in range(B):
                sp.dma_start(conv_sb[b * HD:(b + 1) * HD, :], conv).then_inc(S["ld_conv"], 16)

            def store_h(g, p):
                sp.wait_ge(S["h_ready"], g + 1)
                sp.dma_start(h_dram[g], res[:, p, :, :].rearrange("p j c -> p (j c)")).then_inc(h_stored[p], 16)

            def store_x(g, p, b, half):
                span = slice(half * HALF, (half + 1) * HALF)
                sp.wait_ge(S["x_ready"], 2 * (g + 1))
                sp.dma_start(x_dram[b, 0:P, span], big1[:, p, :]).then_inc(x_stored[p], 16)
                sp.dma_start(x_dram[b, P:C, span], big2[0:C2, p, :]).then_inc(x_stored[p], 16)
                sp.wait_ge(S["hw_half"], g + 1)
                sp.dma_start(hw_dram[:, b, span], hw_row[:, p, :]).then_inc(x_stored[p], 16)

            def store_y(g, p, b, half):
                sp.wait_ge(S["y_ready"], g + 1)
                sp.dma_start(y_dram[b, :, half * HALF:(half + 1) * HALF], y_sb[:, p, :]).then_inc(y_stored[p], 16)

            def load_x0(half, t):
                prev = before(half, t)
                for p in range(2):
                    sp.wait_ge(x_stored[p], 48 * 4 * (half + 1))
                if prev:
                    sp.wait_ge(S["taps_done"], taps_at[(*prev, 0)])
                for s in range(TRI):
                    place = t * TRI + s
                    lo = HALF if half == 0 else HALF - history(place, 0)
                    at = lo - HALF * (1 - half)
                    sp.dma_start(win[0][:, s, lo:2 * HALF],
                                 x_dram[:, place * HD:(place + 1) * HD, at:HALF * (half + 1)]).then_inc(S["x0_loaded"], 16)

            def load_hy(half, t):
                prev = before(half, t)
                if prev:
                    sp.wait_ge(S["finished"], finished_at[prev])
                span = slice(half * HALF, (half + 1) * HALF)
                for s in range(TRI):
                    place = t * TRI + s
                    sp.dma_start(hw_in[:, s, :],
                                 hw_dram[place, :, span].rearrange("b (o t) -> b o t", o=1).to_broadcast((B, HD, HALF))
                                 ).then_inc(S["hy_loaded"], 16)
                    if place >= FIRST_MEM:
                        m = place - FIRST_MEM
                        for p in range(2):
                            sp.wait_ge(y_stored[p], 16 * 4 * (half + 1))
                        sp.dma_start(y_in[:, s, :], y_dram[:, m * HD:(m + 1) * HD, span]).then_inc(S["hy_loaded"], 16)

            def save_tail(half, t, stage):
                sp.wait_ge(S["taps_done"], taps_at[half, t, stage])
                for s in range(TRI):
                    place = t * TRI + s
                    n = history(place, stage + 1)
                    sp.dma_start(tail_dram[stage][place, :, HALF - n:HALF],
                                 win[stage + 1][:, s, 2 * HALF - n:2 * HALF]).then_inc(tail_saved[stage], 16)

            def load_tail(t, stage):
                prev = before(1, t)
                sp.wait_ge(tail_saved[stage], 16 * NH)
                sp.wait_ge(S["taps_done"], taps_at[(*prev, stage + 1)])
                for s in range(TRI):
                    place = t * TRI + s
                    n = history(place, stage + 1)
                    sp.dma_start(win[stage + 1][:, s, HALF - n:HALF],
                                 tail_dram[stage][place, :, HALF - n:HALF]).then_inc(tail_loaded[stage], 16)

            def store_heads(half, t):
                sp.wait_ge(S["finished"], finished_at[half, t])
                for s in range(TRI):
                    place = t * TRI + s
                    sp.dma_start(o_dram[:, place * HD:(place + 1) * HD, half * HALF:(half + 1) * HALF],
                                 heads[:, s, :]).then_inc(S["o_stored"], 16)

            def after_unit(half, t, stage):
                more = t + 1 < NT
                if stage < 2 and half == 0:
                    save_tail(half, t, stage)
                if stage == 0 and more:
                    load_x0(half, t + 1)
                if stage == 1 and half == 1 and more:
                    load_tail(t + 1, 0)
                if stage == 2 and half == 1 and more:
                    load_tail(t + 1, 1)

            def after_parts(parts):
                for part in parts:
                    if is_last(*part):
                        after_unit(*part[:3])

            def after_finish(g):
                for half, t in finished_in(g):
                    store_heads(half, t)
                    if t + 1 < NT:
                        load_hy(half, t + 1)

            def load_group(g, p, b, half):
                if not isinstance(g, int) or g >= 2:
                    sp.wait_ge(S["q_ready"], 2 * (g - 1))
                    sp.wait_ge(S["o_lo_ready"], 2 * (g - 1))
                    sp.wait_ge(S["h2_ready"], g - 1)
                span = slice(half * HALF, (half + 1) * HALF)
                sp.dma_start(o1[:, p, :], o_dram[b, 0:P, span]).then_inc(o_loaded[p], 16)
                sp.dma_start(o2[:, p, :], o_dram[b, P:C, span]).then_inc(o_loaded[p], 16)
                sp.dma_start(res[:, p, :, :].rearrange("p j c -> p (j c)"), h_dram[g]).then_inc(r_loaded[p], 16)

            def store_out(g, p, b, half):
                sp.wait_ge(S["out_ready"], g + 1)
                sp.dma_start(out[b, half * HALF:(half + 1) * HALF, :].rearrange("(j p) c -> p j c", p=P),
                             h2[:, p, :, :]).then_inc(out_stored[p], 16)

            store_h(0, 0)
            store_h(1, 1)
            for g in (0, 1):
                store_x(g, g % 2, g, 0)
                store_h(g + 2, g % 2)
            with sp.Fori(1, 4) as i:
                for k in range(2):
                    g = 2 * i + k
                    store_x(g, k, g, 0)
                    store_y(g - 2, k, g - 2, 0)
                    store_h(g + 2, k)
            sp.wait_ge(S["weights_ready"], len(SECOND_WEIGHTS))
            load_x0(0, 0)
            for g in range(B, NG):
                if g == NG - 1:
                    sp.wait_ge(S["o_stored"], 16 * NH)
                    sp.wait_ge(S["n_ready"], NG)
                    for k in range(2):
                        sp.wait_ge(h_stored[k], 16 * NG // 2)
                    load_group(0, 0, 0, 0)
                    load_group(1, 1, 1, 0)
                store_x(g, g % 2, g - B, 1)
                store_y(g - 2, g % 2, (g - 2) % B, (g - 2) // B)
                if g + 2 < NG:
                    store_h(g + 2, g % 2)
                if g == B:
                    load_hy(0, 0)
                after_finish(g)
                after_parts(parts_of(g))
            load_x0(1, 0)
            load_tail(0, 0)
            store_y(NG - 2, 0, B - 2, 1)
            load_tail(0, 1)
            store_y(NG - 1, 1, B - 1, 1)
            load_hy(1, 0)
            after_parts(turn_parts(0) + turn_parts(1))
            load_group(2, 0, 2, 0)
            after_parts(turn_parts(2) + turn_parts(3) + turn_parts(4))
            for g in range(B):
                for slot in range(SECOND_SLOTS // 2):
                    after_parts(parts_in(NG + g, slot))
                if g + 3 < B:
                    load_group(g + 3, (g + 3) % 2, g + 3, 0)
                elif g == B - 2:
                    sp.wait_ge(S["o_stored"], 2 * 16 * NH)
                    load_group(B, 0, 0, 1)
                    load_group(B + 1, 1, 1, 1)
                elif g == B - 1:
                    load_group(B + 2, 0, 2, 1)
                for slot in range(SECOND_SLOTS // 2, SECOND_SLOTS):
                    after_parts(parts_in(NG + g, slot))
                after_finish(NG + g)
                store_out(g, g % 2, g, 0)
            with sp.Fori(B // 2, NG // 2 - 2) as i:
                for k in range(2):
                    g = 2 * i + k
                    load_group(g + 3, 1 - k, g + 3 - B, 1)
                    store_out(g, k, g - B, 1)
            for g in range(NG - 4, NG):
                if g + 3 < NG:
                    load_group(g + 3, (g + 3) % 2, g + 3 - B, 1)
                store_out(g, g % 2, g - B, 1)
            for p in range(2):
                sp.wait_ge(out_stored[p], 16 * NG // 2)

        @block.gpsimd
        def _(pool):
            nc.gpsimd.memset(half_neg[:, :], -0.5).then_inc(S["pool_consts"], 1)

            def gather(g):
                p = g % 2
                if g >= 2:
                    pool.wait_ge(S["n_ready"], g - 1)
                    pool.wait_ge(h_stored[p], 16 * (g // 2))
                half, b = g // B, g % B
                for j in range(NJ):
                    row = (b * T + half * HALF) // P + j
                    nc.gpsimd.indirect_dma_start(
                        out=res[:, p, j, :], out_offset=None, in_=tok,
                        in_offset=bass.IndirectOffsetOnAxis(ap=idx[:, row:row + 1], axis=0)).then_inc(gathered[p], 16)

            def power(k, p):
                pool.wait_ge(S["var_ready"], k + 1)
                nc.gpsimd.tensor_tensor(rstd[:, p, :], var[:, p, :], half_neg[:, :], ALU.pow).then_inc(S["rstd_ready"], 1)

            def power_and_centre(k, p):
                power(k, p)
                pool.wait_ge(S["rstd_ready"], k + 1)
                nc.gpsimd.tensor_tensor(centre[:, p, :], neg_mean[:, p, :], rstd[:, p, :], ALU.mult).then_inc(S["centre_ready"], 1)

            pool.wait_ge(S["idx_ready"], 1)
            gather(0)
            gather(1)
            pool.wait_ge(S["pool_consts"], 1)
            power_and_centre(0, 0)
            gather(2)

            def masks(g):
                if g == 0:
                    pool.wait_ge(S["ld_mem"], 16 * 7)
                pool.wait_ge(S["step_done"], 8 * g + 7)
                if g:
                    pool.wait_ge(S["y_mm"], g)
                first = zero_st[:, :] if g < B else st_mid[:, g - B, :]
                nc.gpsimd.tensor_tensor(st_bd[:, 0, :], first, mask_sb[:, :], ALU.mult).then_inc(S["masked"], 1)
                nc.gpsimd.tensor_tensor(st_bd[:, 1:8, :], st[:, :, :],
                                        mask_sb[:, :].rearrange("p (o c) -> p o c", o=1).to_broadcast((C2, 7, C2)),
                                        ALU.mult).then_inc(S["masked"], 1)

            def low_weight(n):
                raw, high, low = SECOND_WEIGHTS[n]
                pool.wait_ge(S["w_hi"], 3 + n)
                nc.gpsimd.tensor_tensor(low, raw, high.bitcast(F32), ALU.subtract).then_inc(S["weights_ready"], 1)

            def add_positions(g):
                p = g % 2
                pool.wait_ge(gathered[p], 16 * NJ * (g // 2 + 1))
                nc.gpsimd.tensor_tensor(res[:, p, :, :], res[:, p, :, :], pos[:, NJ:2 * NJ, :], ALU.add).then_inc(S["h_ready"], 1)

            def finish(half, t):
                pool.wait_ge(S["hy_loaded"], hy_at[half, t])
                pool.wait_ge(S["taps_done"], taps_at[half, t, 2])
                pool.wait_ge(S["conv_init"], init_at[half, t, 2, TRI - 1])
                done = finished_at[before(half, t)] if before(half, t) else 0
                added = {}
                for s in range(TRI):
                    if t * TRI + s >= FIRST_MEM:
                        nc.gpsimd.tensor_tensor(heads[:, s, :], heads[:, s, :], y_in[:, s, :], ALU.add).then_inc(S["finished"], 1)
                        done += 1
                        added[s] = done
                for s in range(TRI):
                    if s in added:
                        pool.wait_ge(S["finished"], added[s])
                    nc.gpsimd.tensor_tensor(heads[:, s, :], heads[:, s, :], hw_in[:, s, :], ALU.mult).then_inc(S["finished"], 1)

            for g in range(NG):
                if g + 1 < NG:
                    power_and_centre(g + 1, (g + 1) % 2)
                if g >= 2:
                    masks(g - 2)
                if B <= g < NG - 2:
                    add_positions(g + 2)
                if g + 3 < NG:
                    gather(g + 3)
                if 1 <= g <= len(SECOND_WEIGHTS):
                    low_weight(g - 1)
                for half, t in finished_in(g):
                    finish(half, t)
            def low_o(g, p):
                pool.wait_ge(S["o_hi_ready"], 2 * g + 1)
                nc.gpsimd.tensor_tensor(o_lo[:, :], o1[:, p, :], o_hi[:, :].bitcast(F32), ALU.subtract).then_inc(S["o_lo_ready"], 1)
                pool.wait_ge(S["o_hi_ready"], 2 * g + 2)
                pool.wait_ge(S["o_lo_ready"], 2 * g + 1)
                nc.gpsimd.tensor_tensor(o_2[C2:P, :], o2[:, p, :], o_2[0:C2, :].bitcast(F32), ALU.subtract).then_inc(S["o_lo_ready"], 1)
                pool.wait_ge(r_loaded[p], 16 * (g // 2 + 1) if isinstance(g, int) else 8 * (g - p) + 16)
                pool.wait_ge(S["o_lo_ready"], 2 * g + 2)
                nc.gpsimd.tensor_tensor(res[:, p, :, :], res[:, p, :, :],
                                        mix_b_sb[:, :].rearrange("p (o c) -> p o c", o=1).to_broadcast((P, NJ, C)),
                                        ALU.add).then_inc(S["res_biased"], 1)

            def low_q(g):
                pool.wait_ge(S["q_hi_ready"], 2 * g + 1)
                nc.gpsimd.tensor_tensor(q_lo[:, :], q1[:, :], q_hi[:, :].bitcast(F32), ALU.subtract).then_inc(S["q_lo_ready"], 1)
                pool.wait_ge(S["q_hi_ready"], 2 * g + 2)
                pool.wait_ge(S["q_lo_ready"], 2 * g + 1)
                nc.gpsimd.tensor_tensor(q_2[C2:P, :], q2[:, :], q_2[0:C2, :].bitcast(F32), ALU.subtract).then_inc(S["q_lo_ready"], 1)
                pool.wait_ge(S["q_lo_ready"], 2 * g + 2)

            pool.wait_ge(S["ld_bias"], 16 * 4)
            low_o(0, 0)
            masks(NG - 2)
            masks(NG - 1)
            low_q(0)
            low_o(1, 1)
            power(NG, 0)
            for g in range(B):
                low_q(g + 1)
                if g == B - 2:
                    power(NG + g + 1, (g + 1) % 2)
                low_o(g + 2, g % 2)
                if g != B - 2:
                    power(NG + g + 1, (g + 1) % 2)
                for half, t in finished_in(NG + g):
                    finish(half, t)
            with pool.Fori(B // 2, NG // 2 - 1) as i:
                for k in range(2):
                    g = 2 * i + k
                    low_q(g + 1)
                    low_o(g + 2, k)
                    power(NG + g + 1, 1 - k)
            low_q(NG - 1)
            power(2 * NG - 1, 1)

        @block.scalar
        def _(act):
            for dst, src in ((view(small, "memk", HD), memk), (view(small, "memq", HD), memq),
                             (view(small, "memv"), memv), (view(small, "memo"), memo),
                             (view(small, "memg", C2), memg), (mask_sb[:, :], mask), (router_bh[:, :], router_b)):
                act.dma_start(dst, src).then_inc(S["ld_mem"], 16)
            act.wait_ge(S["consts"], 3)
            act.dma_start(mem_rhs[C2:C2 + 1, 2 * C2:3 * C2], membg).then_inc(S["ld_membg"], 16)
            act.wait_ge(S["pool_consts"], 1)
            nc.scalar.activation(warm[:, :], half_neg[:, 0:1], ACT.Gelu)
            for k in range(4):
                act.wait_ge(S["pos_mm"], k + 1)
                nc.scalar.copy(pos[:, 2 * k:2 * k + 2, :], bank_jc(4 + k)).then_inc(S["pos_ready"], 1)

            def high_weights():
                act.wait_ge(S["w_half"], 7)
                for name in ("mixg", "mix", "fin", "fout"):
                    act.wait_ge(S[f"ld_{name}"], 16 if name == "fout" else 48)
                    for raw, high, _ in WEIGHTS[name]:
                        nc.scalar.copy(high, raw).then_inc(S["w_hi"], 1)

            def high_n(g, p, second=False):
                act.wait_ge(S["nT_ready"], (NG if second else 0) + g + 1)
                if not isinstance(g, int) or g >= 2:
                    if second:
                        act.wait_ge(S["in_mm"], NC * (g - 1))
                    else:
                        act.wait_ge(S["gate_mm"], 4 * (g - 1))
                nc.scalar.copy(n_hi[:, p, :], bank[0][:, :]).then_inc(S["nT_hi"], 1)
                nc.scalar.copy(n_2[0:C2, p, :], bank[1][0:C2, :]).then_inc(S["nT_hi"], 1)

            def normalise(g, p):
                act.wait_ge(S["centre_ready"], g + 1)
                if not (isinstance(g, int) and g == 0):
                    act.wait_ge(S["nT_ready"], g)
                for j in range(NJ):
                    i = nc.scalar.activation(nrm[:, j, :], res[:, p, j, :], ACT.Identity, bias=centre[:, p, j:j + 1],
                                             scale=rstd[:, p, j:j + 1])
                i.then_inc(S["n_ready"], 1)

            def gates(g, p, first=False, last=False):
                act.wait_ge(S["gate_mm"], 4 * g + 1)
                if not first:
                    act.wait_ge(S["x_ready"], 2 * g)
                nc.scalar.activation(tg2[:, :], bank[4][C2:P, :], ACT.Tanh, scale=0.5).then_inc(S["tanh_done"], 1)
                if not last:
                    normalise(g + 1, 1 - p)
                act.wait_ge(S["gate_mm"], 4 * g + 3)
                nc.scalar.activation(tg1[:, :], bank[3][:, :], ACT.Tanh, scale=0.5).then_inc(S["tanh_done"], 1)
                act.wait_ge(S["gate_mm"], 4 * g + 4)
                act.wait_ge(S["w_half"], 3)
                if not (isinstance(g, int) and g < 2):
                    act.wait_ge(x_stored[p], 24 * (g - p))
                nc.scalar.activation(hw_row[:, p, :], bank[5][0:NH, :], ACT.Tanh, bias=router_bh[:, :], scale=0.5).then_inc(S["tanh_done"], 1)

            def read_y(g, p):
                act.wait_ge(S["y_mm"], g + 1)
                if not (isinstance(g, int) and g < 2):
                    act.wait_ge(y_stored[p], 8 * (g - p))
                nc.scalar.copy(y_sb[:, p, :], bank[1][C2:P, :]).then_inc(S["y_ready"], 1)

            def memory_rows(g, first=False):
                if not first:
                    act.wait_ge(S["G_ready"], g)
                for half in range(2):
                    act.wait_ge(S["mem_mm"], 2 * g + half + 1)
                    tiles = slice(2 * half, 2 * half + 2)
                    nc.scalar.activation(mem_l[:, tiles, C2:P], bank_jc(6 + half)[:, :, 2 * C2:3 * C2], ACT.Tanh, scale=0.5).then_inc(S["mem_act"], 1)
                    nc.scalar.copy(mem_r[:, tiles, 0:C2], bank_jc(6 + half)[:, :, C2:2 * C2]).then_inc(S["mem_act"], 1)

            def start_unit(half, t, stage):
                prev = before(half, t)
                if stage == 0:
                    act.wait_ge(S["x0_loaded"], 48 * (half * NT + t + 1))
                    act.wait_ge(S["conv_w_ready"], 1)
                for s in range(TRI):
                    if stage:
                        act.wait_ge(S["taps_done"], taps_at[half, t, stage - 1, s])
                    if s == 0 and prev:
                        if stage < 2:
                            act.wait_ge(S["taps_done"], taps_at[(*prev, stage + 1)])
                            act.wait_ge(tail_saved[stage], 48 * min(NT, half * NT + t))
                        else:
                            act.wait_ge(S["o_stored"], 48 * (half * NT + t))
                    place = t * TRI + s
                    dst = heads[:, s, :] if stage == 2 else win[stage + 1][:, s, HALF:2 * HALF]
                    nc.scalar.activation(dst, win[stage][:, s, HALF:2 * HALF], ACT.Identity,
                                         bias=conv_b[:, place, stage:stage + 1],
                                         scale=conv_w3[:, place, stage:stage + 1]).then_inc(S["conv_init"], 1)

            def split_o(g, p):
                act.wait_ge(o_loaded[p], 32 * (g // 2 + 1) if isinstance(g, int) else 16 * (g - p) + 32)
                if not (isinstance(g, int) and g == 0):
                    act.wait_ge(S["mixg_mm"], 2 * g)
                nc.scalar.copy(o_hi[:, :], o1[:, p, :]).then_inc(S["o_hi_ready"], 1)
                nc.scalar.copy(o_2[0:C2, :], o2[:, p, :]).then_inc(S["o_hi_ready"], 1)

            def mix_gates(g, second=5):
                act.wait_ge(S["mixg_mm"], 2 * g + 1)
                if isinstance(g, int) and g == 0:
                    act.wait_ge(S["x_ready"], 2 * NG)
                else:
                    act.wait_ge(S["q_ready"], 2 * g)
                nc.scalar.activation(tg1[:, :], bank[4][:, :], ACT.Tanh, bias=mixg_bh[:, :], scale=0.5).then_inc(S["tg_ready"], 1)
                act.wait_ge(S["mixg_mm"], 2 * g + 2)
                nc.scalar.activation(tg2[:, :], bank[second][0:C2, :], ACT.Tanh, bias=mixg_bh2[:, :], scale=0.5).then_inc(S["tg_ready"], 1)

            def split_q(g):
                act.wait_ge(S["q_ready"], 2 * g + 1)
                if not (isinstance(g, int) and g == 0):
                    act.wait_ge(S["mix_mm"], 2 * g)
                nc.scalar.copy(q_hi[:, :], q1[:, :]).then_inc(S["q_hi_ready"], 1)
                act.wait_ge(S["q_ready"], 2 * g + 2)
                nc.scalar.copy(q_2[0:C2, :], q2[:, :]).then_inc(S["q_hi_ready"], 1)

            def gelu(g, c):
                act.wait_ge(S["in_mm"], NC * g + c + 1)
                if not (isinstance(g, int) and g == 0 and c < 2):
                    act.wait_ge(S["hid_lo_ready"], NC * g + c - 1)
                nc.scalar.activation(hid[:, c % 2, :], bank[2 + c % 2][:, :], ACT.Gelu, bias=fin_b_sb[:, c:c + 1]).then_inc(S["gelu_done"], 1)

            def high_hid(g, c):
                act.wait_ge(S["gelu_done"], NC * g + c + 1)
                if not (isinstance(g, int) and g == 0 and c < 3):
                    act.wait_ge(S["out_mm"], NC * g + c - 2)
                nc.scalar.copy(hid_hi[:, c % 3, :], hid[:, c % 2, :]).then_inc(S["hid_hi_ready"], 1)

            def start_parts(parts):
                for half, t, stage, k in parts:
                    if k == 1:
                        start_unit(half, t, stage)

            def beside(g, slot):
                start_parts(parts_in(g, slot))

            def first_pass(g, p, convs=False, first=False, reads_before=True, last=False):
                gates(g, p, first, last)
                if convs:
                    beside(g, 0)
                if not last:
                    high_n(g + 1, 1 - p)
                if reads_before:
                    read_y(g - 2, p)
                if convs:
                    beside(g, 1)
                memory_rows(g, first)
                if convs:
                    beside(g, 2)
                    beside(g, 3)

            def second_pass(g, p, convs=False, ahead=2):
                if ahead:
                    mix_gates(g + 1)
                gelu(g, 0)
                high_hid(g, 0)
                if ahead:
                    split_q(g + 1)
                if convs:
                    beside(NG + g, 0)
                gelu(g, 1)
                high_hid(g, 1)
                if convs:
                    beside(NG + g, 1)
                for c in range(2, NC):
                    gelu(g, c)
                    high_hid(g, c)
                    if ahead == 2 and c == (4 if isinstance(g, int) and g == B - 2 else 2):
                        split_o(g + 2, p)
                    if c == NC - 1 and ahead:
                        high_n(g + 1, 1 - p, second=True)
                    if convs:
                        beside(NG + g, c)

            normalise(0, 0)
            high_n(0, 0)
            first_pass(0, 0, first=True, reads_before=False)
            high_weights()
            first_pass(1, 1, reads_before=False)
            first_pass(2, 0)
            first_pass(3, 1)
            with act.Fori(2, B // 2) as i:
                for k in range(2):
                    first_pass(2 * i + k, k)
            for g in range(B, NG):
                first_pass(g, g % 2, convs=True, last=g == NG - 1)
            split_o(0, 0)
            start_parts(turn_parts(0))
            mix_gates(0, second=2)
            read_y(NG - 2, 0)
            split_q(0)
            split_o(1, 1)
            start_parts(turn_parts(1))
            read_y(NG - 1, 1)
            start_parts(turn_parts(2))
            high_n(0, 0, second=True)
            start_parts(turn_parts(3) + turn_parts(4))
            for g in range(B):
                second_pass(g, g % 2, convs=True)
            with act.Fori(B // 2, NG // 2 - 1) as i:
                for k in range(2):
                    second_pass(2 * i + k, k)
            second_pass(NG - 2, 0, ahead=1)
            second_pass(NG - 1, 1, ahead=0)

        @block.vector
        def _(dve):
            nc.vector.memset(mem_r[:, :, C2:C2 + 1], 1.0 / CH).then_inc(S["consts"], 1)
            nc.vector.memset(zero_st[:, :], 0.0).then_inc(S["consts"], 1)
            nc.vector.memset(mem_rhs[:, :], 0.0).then_inc(S["consts"], 1)
            nc.vector.memset(big2[C2:C2 + 1, :, :], 1.0).then_inc(S["consts"], 1)
            dve.wait_ge(S["ld_idx"], 32)
            nc.vector.tensor_copy(xf[:, :], xi[:, :]).then_inc(S["idx_f"], 1)
            dve.wait_ge(S["idx_t"], 1)
            nc.vector.tensor_copy(idx[:, :], bank[0][:, 0:B * T // P]).then_inc(S["idx_ready"], 1)
            dve.wait_ge(S["pos_qt"], 2)
            nc.vector.tensor_copy(view(small, "qT1"), bank[1][:, 0:HD]).then_inc(S["pos_qs"], 1)
            nc.vector.tensor_copy(view(small, "qT2", C2), bank[2][0:C2, 0:HD]).then_inc(S["pos_qs"], 1)
            dve.wait_ge(S["pos_q"], 2)
            dve.wait_ge(S["ld_digits"], 32)
            tabs = view(small, "tabs", DIGIT_ROWS)
            for d in (1, 2):
                nc.vector.tensor_copy(tabs[d * DIGIT_AT:d * DIGIT_AT + HD, :],
                                      bank[3][0:HD, (d - 1) * C:d * C]).then_inc(S["pos_tab_ready"], 1)
            dve.wait_ge(S["ld_gate"], 48)
            for raw, _, _ in WEIGHTS["gate"]:
                nc.vector.tensor_scalar(raw[:, 0:P], raw[:, 0:P], 0.5, None, ALU.mult)
                nc.vector.tensor_scalar(raw[:, 2 * P:2 * P + C2], raw[:, 2 * P:2 * P + C2], 0.5, None, ALU.mult).then_inc(S["w_half"], 1)
            dve.wait_ge(S["w_half"], 2)
            for raw, high, _ in WEIGHTS["gate"]:
                nc.vector.tensor_copy(high, raw).then_inc(S["w_hi"], 1)
            dve.wait_ge(S["w_hi"], 2)
            for raw, high, low in WEIGHTS["gate"]:
                nc.vector.tensor_tensor(low, raw, high.bitcast(F32), ALU.subtract).then_inc(S["gate_ready"], 1)

            def memory_weights():
                dve.wait_ge(S["mem_w_mm"], 2)
                dve.wait_ge(S["ld_mem"], 16 * 7)
                dve.wait_ge(S["consts"], 4)
                nc.vector.scalar_tensor_tensor(mem_rhs[0:C2, 0:C2], bank[1][0:C2, 64:128], 0.5, mask_sb[:, :], ALU.mult, ALU.mult).then_inc(S["mem_w_ready"], 1)
                nc.vector.tensor_tensor(mem_rhs[0:C2, C2:2 * C2], bank[1][0:C2, 128:192], mask_sb[:, :], ALU.mult).then_inc(S["mem_w_ready"], 1)
                nc.vector.tensor_scalar(mem_rhs[0:C2, 2 * C2:3 * C2], mask_sb[:, :], view(small, "memg", C2), None, ALU.mult).then_inc(S["mem_w_ready"], 1)
                nc.vector.tensor_scalar(router_bh[:, :], router_bh[:, :], 0.5, None, ALU.mult).then_inc(S["w_half"], 1)

            def second_pass_weights():
                dve.wait_ge(S["ld_bias"], 16 * 4)
                dve.wait_ge(S["ld_mix"], 48)
                nc.vector.tensor_scalar(mixg_bh[:, :], mixg_bh[:, :], 0.5, None, ALU.mult).then_inc(S["w_half"], 1)
                nc.vector.tensor_scalar(mixg_bh2[:, :], mixg_bh2[:, :], 0.5, None, ALU.mult).then_inc(S["w_half"], 1)
                for raw, _, _ in WEIGHTS["mix"]:
                    nc.vector.tensor_scalar(raw, raw, 0.5, None, ALU.mult).then_inc(S["w_half"], 1)
                dve.wait_ge(S["ld_conv"], 16 * B)
                nc.vector.tensor_scalar(conv_w3[:, :, :], conv_w[:, :, :, TAPS - 1], 1.0, None, ALU.add).then_inc(S["conv_w_ready"], 1)

            def statistics(k, src, p, between=lambda n: None):
                for j in range(NJ):
                    i = nc.vector.bn_stats(stats[:, p, j, :], src[:, j, :])
                    if j == NJ - 1:
                        i.then_inc(S["stats_done"], 1)
                    between(j)
                dve.wait_ge(S["stats_done"], k + 1)
                mean_e, m2_e, mean_o, m2_o = (stats[:, p, :, n] for n in (1, 2, 4, 5))
                nc.vector.tensor_tensor(lnt[:, p, 0, :], mean_e, mean_o, ALU.subtract)
                nc.vector.scalar_tensor_tensor(lnt[:, p, 1, :], m2_e, C * EPS, m2_o, ALU.add, ALU.add)
                nc.vector.tensor_tensor(lnt[:, p, 2, :], mean_e, mean_o, ALU.add).then_inc(S["halves_done"], 1)
                between(NJ)
                dve.wait_ge(S["halves_done"], k + 1)
                nc.vector.tensor_scalar(neg_mean[:, p, :], lnt[:, p, 2, :], -0.5, None, ALU.mult)
                nc.vector.scalar_tensor_tensor(lnt[:, p, 3, :], lnt[:, p, 0, :], 0.25, lnt[:, p, 0, :], ALU.mult, ALU.mult).then_inc(S["aggr_done"], 1)
                between(NJ + 1)
                dve.wait_ge(S["aggr_done"], k + 1)
                nc.vector.scalar_tensor_tensor(var[:, p, :], lnt[:, p, 1, :], 1.0 / C, lnt[:, p, 3, :], ALU.mult, ALU.add).then_inc(S["var_ready"], 1)

            def add_positions(g, p, half):
                dve.wait_ge(gathered[p], 16 * NJ * (g // 2 + 1) if isinstance(g, int) else 32 * (g - p) + 64)
                nc.vector.tensor_tensor(res[:, p, :, :], res[:, p, :, :], pos[:, half * NJ:(half + 1) * NJ, :], ALU.add).then_inc(S["h_ready"], 1)

            def embed(g, p, half):
                add_positions(g, p, half)
                dve.wait_ge(S["h_ready"], g + 1)
                statistics(g, res[:, p, :, :], p)

            def normalise(k, src, p):
                dve.wait_ge(S["rstd_ready"], k + 1)
                dve.wait_ge(S["nT_ready"], k)
                for j in range(NJ):
                    i = nc.vector.tensor_scalar(nrm[:, j, :], src[:, j, :], neg_mean[:, p, j:j + 1], rstd[:, p, j:j + 1], ALU.add, ALU.mult)
                i.then_inc(S["n_ready"], 1)

            def low_n(k, p):
                dve.wait_ge(S["nT_hi"], 2 * k + 1)
                nc.vector.tensor_tensor(n_lo[:, p, :], bank[0][:, :], n_hi[:, p, :].bitcast(F32), ALU.subtract)
                dve.wait_ge(S["nT_hi"], 2 * k + 2)
                nc.vector.tensor_tensor(n_2[C2:P, p, :], bank[1][0:C2, :], n_2[0:C2, p, :].bitcast(F32), ALU.subtract).then_inc(S["n_split"], 1)

            def gated1(g, p):
                if not (isinstance(g, int) and g < 2):
                    dve.wait_ge(x_stored[p], 24 * (g - p))
                dve.wait_ge(S["tanh_done"], 3 * g + 2)
                nc.vector.scalar_tensor_tensor(big1[:, p, :], tg1[:, :], 1.0, bank[2][:, :], ALU.add, ALU.mult).then_inc(S["x_ready"], 1)
                dve.wait_ge(S["tanh_done"], 3 * g + 3)
                nc.vector.tensor_scalar(hw_row[:, p, :], hw_row[:, p, :], 0.5, 0.5, ALU.mult, ALU.add).then_inc(S["hw_half"], 1)

            def gated2(g, p):
                if not (isinstance(g, int) and g < 2):
                    dve.wait_ge(S["y_mm"], g - 1)
                nc.vector.scalar_tensor_tensor(big2[0:C2, p, :], tg2[:, :], 1.0, bank[4][0:C2, :], ALU.add, ALU.mult).then_inc(S["x_ready"], 1)

            def memory_keys(g):
                for half in range(2):
                    dve.wait_ge(S["mem_act"], 4 * g + 2 * half + 2)
                    tiles = slice(2 * half, 2 * half + 2)
                    nc.vector.scalar_tensor_tensor(mem_l[:, tiles, 0:C2], mem_l[:, tiles, C2:P], 1.0,
                                                   bank_jc(6 + half)[:, :, 0:C2], ALU.add, ALU.mult).then_inc(S["gx_ready"], 1)

            def decays(g, p):
                dve.wait_ge(S["G_ready"], g + 1)
                if not (isinstance(g, int) and g == 0):
                    dve.wait_ge(S["masked"], 2 * g)
                for k in range(2):
                    i = nc.vector.tensor_scalar(dec[:, p, 4 * k:4 * k + 4], bank_g(3 + 2 * k)[C2:P, :, C2], -0.5, 0.5, ALU.mult, ALU.add)
                i.then_inc(S["dec_ready"], 1)

            def state_step(g, p, b, half, c):
                if c:
                    dve.wait_ge(S["step_done"], 8 * g + c)
                else:
                    dve.wait_ge(S["dec_ready"], g + 1)
                at = c % 2 * NJ + c // 2
                old = st[:, c - 1, :] if c else (zero_st[:, :] if half == 0 else st_mid[:, b, :])
                new = st[:, c, :] if c < 7 else st_mid[:, b, :]
                if half and c == 7:
                    new = st_end[:, :]
                nc.vector.scalar_tensor_tensor(new, old, dec[:, p, at:at + 1], bank_g(3 + 2 * (c % 2))[0:C2, c // 2, 0:C2],
                                               ALU.mult, ALU.add).then_inc(S["step_done"], 1)

            def recurrence(g, p, b, half, embed_next=True):
                decays(g, p)
                if embed_next:
                    dve.wait_ge(S["h_ready"], g + 4)
                    statistics(g + 3, res[:, 1 - p, :, :], 1 - p, between=lambda n: state_step(g, p, b, half, n))
                for c in range(NJ + 2 if embed_next else 0, 8):
                    state_step(g, p, b, half, c)

            def part_of_unit(half, t, stage, k):
                def last_write(s, before):
                    done = [taps_at[key] for key in (((half, t, stage, s, "tap", n)) for n in range(1, before)) if key in taps_at]
                    if done:
                        dve.wait_ge(S["taps_done"], done[-1])
                    else:
                        dve.wait_ge(S["conv_init"], init_at[half, t, stage, s])

                for s in range(TRI):
                    place = t * TRI + s
                    (lo, hi), (src_lo, src_hi) = tap_range(half, k * DILATIONS[ORDER[place]][stage])
                    if lo >= hi:
                        continue
                    last_write(s, k)
                    if half and stage and k == 1 and s == 0:
                        dve.wait_ge(tail_loaded[stage - 1], 48 * (t + 1))
                    if stage == 2:
                        acc = heads[:, s, lo - HALF:hi - HALF]
                    else:
                        acc = win[stage + 1][:, s, lo:hi]
                    nc.vector.scalar_tensor_tensor(acc, win[stage][:, s, src_lo:src_hi],
                                                   conv_w[:, place, stage, TAPS - 1 - k:TAPS - k],
                                                   acc, ALU.mult, ALU.add).then_inc(S["taps_done"], 1)

            def mixed(g, p):
                if isinstance(g, int) and g == 0:
                    dve.wait_ge(o_loaded[0], 32)
                else:
                    dve.wait_ge(S["q_lo_ready"], 2 * g)
                dve.wait_ge(S["tg_ready"], 2 * g + 1)
                nc.vector.scalar_tensor_tensor(q1[:, :], tg1[:, :], 1.0, o1[:, p, :], ALU.add, ALU.mult).then_inc(S["q_ready"], 1)
                dve.wait_ge(S["tg_ready"], 2 * g + 2)
                nc.vector.scalar_tensor_tensor(q2[:, :], tg2[:, :], 1.0, o2[:, p, :], ALU.add, ALU.mult).then_inc(S["q_ready"], 1)

            def attended(g, p, second=5):
                dve.wait_ge(S["res_biased"], g + 1)
                if not (isinstance(g, int) and g < 2):
                    dve.wait_ge(out_stored[p], 8 * (g - p))
                for k in range(2):
                    dve.wait_ge(S["mix_mm"], 2 * g + k + 1)
                    i = nc.vector.tensor_tensor(h2[:, p, 2 * k:2 * k + 2, :], bank_jc((4, second)[k]), res[:, p, 2 * k:2 * k + 2, :], ALU.add)
                i.then_inc(S["h2_ready"], 1)
                dve.wait_ge(S["h2_ready"], g + 1)
                statistics(NG + g, h2[:, p, :, :], p)

            def low_hid(g, c):
                dve.wait_ge(S["hid_hi_ready"], NC * g + c + 1)
                nc.vector.tensor_tensor(hid_lo[:, c % 3, :], hid[:, c % 2, :], hid_hi[:, c % 3, :].bitcast(F32), ALU.subtract).then_inc(S["hid_lo_ready"], 1)

            def result(g, p):
                dve.wait_ge(S["out_mm"], NC * g + NC)
                for k in range(2):
                    i = nc.vector.tensor_tensor(h2[:, p, 2 * k:2 * k + 2, :], bank_jc(6 + k), h2[:, p, 2 * k:2 * k + 2, :], ALU.add)
                i.then_inc(S["out_ready"], 1)

            def beside(g, slot):
                for part in parts_in(g, slot):
                    part_of_unit(*part)

            def first_pass(g, p, b, half):
                if half == 0:
                    add_positions(g + 2, p, 0 if not isinstance(g, int) or g + 2 < B else 1)
                gated1(g, p)
                gated2(g, p)
                if half:
                    beside(g, 0)
                if half == 0 or b + 1 < B:
                    low_n(g + 1, 1 - p)
                if half:
                    beside(g, 1)
                if isinstance(g, int) and g == 0:
                    dve.wait_ge(S["h_ready"], 3)
                    statistics(2, res[:, 0, :, :], 0)
                elif isinstance(g, int) and g == B:
                    recurrence(g - 1, 1 - p, B - 1, 0)
                else:
                    recurrence(g - 1, 1 - p, b - 1, half, embed_next=half == 0 or b + 2 < B)
                if half:
                    beside(g, 2)
                memory_keys(g)
                if half:
                    beside(g, 3)

            def second_pass(g, p, convs=False, last=False, before_last=False):
                for c in range(NC):
                    if c == 3 and not last:
                        attended(g + 1, 1 - p)
                    if c == 4 and not last:
                        normalise(NG + g + 1, h2[:, 1 - p, :, :], 1 - p)
                    low_hid(g, c)
                    if c == NC - 1:
                        if not last:
                            low_n(NG + g + 1, 1 - p)
                            if not before_last:
                                mixed(g + 2, p)
                        result(g, p)
                    if convs:
                        beside(NG + g, c)

            memory_weights()
            dve.wait_ge(S["pos_ready"], 2)
            embed(0, 0, 0)
            embed(1, 1, 0)
            low_n(0, 0)
            second_pass_weights()
            first_pass(0, 0, 0, 0)
            first_pass(1, 1, 1, 0)
            with dve.Fori(1, B // 2 - 1) as i:
                for k in range(2):
                    g = 2 * i + k
                    first_pass(g, k, g, 0)
            for g in (B - 2, B - 1):
                first_pass(g, g % 2, g, 0)
            for g in range(B, NG):
                first_pass(g, g % 2, g - B, 1)
            recurrence(NG - 1, 1, B - 1, 1, embed_next=False)
            for slot, step in enumerate((lambda: mixed(0, 0), lambda: attended(0, 0, second=2),
                                         lambda: normalise(NG, h2[:, 0, :, :], 0), lambda: low_n(NG, 0))):
                for part in turn_parts(slot):
                    part_of_unit(*part)
                step()
            mixed(1, 1)
            for part in turn_parts(4):
                part_of_unit(*part)
            for g in range(B):
                second_pass(g, g % 2, convs=True)
            with dve.Fori(B // 2, NG // 2 - 1) as i:
                for k in range(2):
                    second_pass(2 * i + k, k)
            second_pass(NG - 2, 0, before_last=True)
            second_pass(NG - 1, 1, last=True)

        @block.tensor
        def _(pe):
            def mm(dst, lhsT, rhs, start, stop):
                return nc.tensor.matmul(dst, lhsT, rhs, start=start, stop=stop)

            def mm5(dst, pairs):
                for n, (lhsT, rhs) in enumerate(pairs):
                    i = mm(dst, lhsT, rhs, n == 0, n == len(pairs) - 1)
                return i

            pe.wait_ge(S["idx_f"], 1)
            nr = B * T // P
            nc.tensor.transpose(bank[0][:, 0:nr], xf[:, :], id_sb[0:nr, 0:nr]).then_inc(S["idx_t"], 1)
            pe.wait_ge(S["ld_carry"], 16 * 4)
            carry = [view(small, "carry1"), view(small, "carry2", C2)]
            pT = [view(small, "posT1"), view(small, "posT2", C2)]
            qT = [view(small, "qT1"), view(small, "qT2", C2)]
            for m, (lo, hi) in enumerate(((0, P), (P, C))):
                for k in range(2):
                    i = mm(bank[1 + m][0:hi - lo, 0:HD], carry[k][:, lo:hi], pT[k], k == 0, k == 1)
                i.then_inc(S["pos_qt"], 1)
            for k in range(2):
                i = mm(bank[3][0:HD, 0:C], pT[k], carry[k], k == 0, k == 1)
            i.then_inc(S["pos_q"], 1)
            pe.wait_ge(S["pos_qs"], 2)
            for k in range(2):
                i = mm(bank[3][0:HD, C:2 * C], qT[k], carry[k], k == 0, k == 1)
            i.then_inc(S["pos_q"], 1)
            pe.wait_ge(S["pos_tab_ready"], 2)
            for r in range(T // P):
                i = mm(bank[4 + r // 2][:, (r % 2) * C:(r % 2 + 1) * C], digit_sb[:, r * P:(r + 1) * P],
                       view(small, "tabs", DIGIT_ROWS), True, True)
                if r % 2:
                    i.then_inc(S["pos_mm"], 1)
            pe.wait_ge(S["ld_mem"], 16 * 7)
            mm(bank[1][0:C2, 64:128], view(small, "memk", HD), view(small, "memq", HD), True, True).then_inc(S["mem_w_mm"], 1)
            mm(bank[1][0:C2, 128:192], view(small, "memv"), view(small, "memo"), True, True).then_inc(S["mem_w_mm"], 1)

            def transposes(k):
                pe.wait_ge(S["n_ready"], k + 1)
                if not (isinstance(k, int) and k == 0):
                    pe.wait_ge(S["n_split"], k)
                for j in range(NJ):
                    nc.tensor.transpose(bank[0][:, j * P:(j + 1) * P], nrm[:, j, 0:P], id_sb[:, :])
                for j in range(NJ):
                    i = nc.tensor.transpose(bank[1][0:C2, j * P:(j + 1) * P], nrm[:, j, P:C], id_sb[:, :])
                i.then_inc(S["nT_ready"], 1)

            def gate(g, p, b, lo, hi):
                mm5(bank[b][0:hi - lo, :], [(gate_h[:, lo:hi], n_hi[:, p, :]), (gate_l[:, lo:hi], n_hi[:, p, :]),
                                            (gate_h[:, lo:hi], n_lo[:, p, :]), (gate2_h[:, lo:hi], n_2[:, p, :]),
                                            (gate2_l[:, lo:hi], n_2[:, p, :])]).then_inc(S["gate_mm"], 1)

            def gates(g, p, first=False, reads_before=True):
                pe.wait_ge(S["n_split"], g + 1)
                if not first:
                    pe.wait_ge(S["x_ready"], 2 * g)
                gate(g, p, 4, 2 * P, 3 * P)
                gate(g, p, 2, 0, P)
                if reads_before:
                    pe.wait_ge(S["step_done"], 8 * (g - 1))
                gate(g, p, 3, P, 2 * P)
                gate(g, p, 5, 3 * P, GW)
                if reads_before:
                    reads_can_start(g - 2)

            def memory_rows(g, p, first=False):
                pe.wait_ge(S["x_ready"], 2 * g + 2)
                for j in range(NJ):
                    if j % 2 == 0 and not first:
                        pe.wait_ge(S["gx_ready"], 2 * g - 1 + j // 2)
                    i = mm(bank_jc(6 + j // 2)[:, j % 2, :], big2[:, p, j * P:(j + 1) * P], mem_rhs[:, :], True, True)
                    if j % 2:
                        i.then_inc(S["mem_mm"], 1)

            def writes(g):
                pe.wait_ge(S["tanh_done"], 3 * min(NG, g + 2) if isinstance(g, int) else 3 * g + 6)
                pe.wait_ge(S["gx_ready"], 2 * g + 2)
                for j in range(NJ):
                    for r in range(2):
                        rows = slice(r * CH, (r + 1) * CH)
                        i = mm(bank_g(3 + 2 * r)[:, j, :], mem_l[rows, j, :], mem_r[rows, j, :], True, True)
                i.then_inc(S["G_ready"], 1)

            def reads_can_start(g):
                pe.wait_ge(S["masked"], 2 * g + 2)
                if not (isinstance(g, int) and g == 0):
                    pe.wait_ge(S["y_ready"], g)

            def reads(g, p):
                for c in range(8):
                    i = mm(bank[1][C2:P, c * CH:(c + 1) * CH], st_bd[:, c, :], big2[0:C2, p, c * CH:(c + 1) * CH], True, True)
                i.then_inc(S["y_mm"], 1)

            def first_pass(g, p, reads_before=True, last=False):
                gates(g, p, reads_before=reads_before)
                if not last:
                    transposes(g + 1)
                if reads_before:
                    reads(g - 2, p)
                writes(g - 1)
                memory_rows(g, p)

            def mix_gates(g, second=5):
                pe.wait_ge(S["o_lo_ready"], 2 * g + 2)
                if not (isinstance(g, int) and g == 0):
                    pe.wait_ge(S["h2_ready"], g)
                for b, lo, hi in ((4, 0, P), (second, P, C)):
                    mm5(bank[b][0:hi - lo, :], [(mixg_h[:, lo:hi], o_hi[:, :]), (mixg_l[:, lo:hi], o_hi[:, :]),
                                                (mixg_h[:, lo:hi], o_lo[:, :]), (mixg2_h[:, lo:hi], o_2[:, :]),
                                                (mixg2_l[:, lo:hi], o_2[:, :])]).then_inc(S["mixg_mm"], 1)

            def mix(g, second=5):
                pe.wait_ge(S["q_lo_ready"], 2 * g + 2)
                for j in range(NJ):
                    cut = slice(j * P, (j + 1) * P)
                    i = mm5(bank_jc((4, second)[j // 2])[:, j % 2, :],
                            [(q_hi[:, cut], mix_h[:, :]), (q_hi[:, cut], mix_l[:, :]), (q_lo[:, cut], mix_h[:, :]),
                             (q_2[:, cut], mix2_h[:, :]), (q_2[:, cut], mix2_l[:, :])])
                    if j % 2:
                        i.then_inc(S["mix_mm"], 1)

            def ffn_in(g, c, p):
                if c == 0:
                    pe.wait_ge(S["n_split"], NG + g + 1)
                if not (isinstance(g, int) and g == 0 and c < 2):
                    pe.wait_ge(S["gelu_done"], NC * g + c - 1)
                cut = slice(c * P, (c + 1) * P)
                mm5(bank[2 + c % 2][:, :], [(fin_h[:, cut], n_hi[:, p, :]), (fin_l[:, cut], n_hi[:, p, :]),
                                            (fin_h[:, cut], n_lo[:, p, :]), (fin2_h[:, cut], n_2[:, p, :]),
                                            (fin2_l[:, cut], n_2[:, p, :])]).then_inc(S["in_mm"], 1)

            def ffn_out(g, c):
                if c == 0 and not (isinstance(g, int) and g == 0):
                    pe.wait_ge(S["out_ready"], g)
                pe.wait_ge(S["hid_lo_ready"], NC * g + c + 1)
                for j in range(NJ):
                    cut = slice(j * P, (j + 1) * P)
                    dst = bank_jc(6 + j // 2)[:, j % 2, :]
                    for n, (a, w) in enumerate(((hid_hi, fout_h), (hid_hi, fout_l), (hid_lo, fout_h))):
                        i = nc.tensor.matmul(dst, a[:, c % 3, cut], w[:, c, :], start=c == 0 and n == 0 and j % 2 == 0,
                                             stop=c == NC - 1 and n == 2, skip_group_check=True)
                i.then_inc(S["out_mm"], 1)

            def second_pass(g, p, ahead=2):
                ffn_in(g, 1, p)
                ffn_in(g, 2, p)
                ffn_out(g, 0)
                ffn_in(g, 3, p)
                ffn_out(g, 1)
                if ahead:
                    mix(g + 1)
                ffn_in(g, 4, p)
                ffn_out(g, 2)
                ffn_in(g, 5, p)
                ffn_out(g, 3)
                if ahead:
                    transposes(NG + g + 1)
                ffn_out(g, 4)
                if ahead == 2:
                    mix_gates(g + 2)
                if ahead:
                    ffn_in(g + 1, 0, 1 - p)
                ffn_out(g, 5)

            pe.wait_ge(S["mem_w_ready"], 3)
            transposes(0)
            pe.wait_ge(S["gate_ready"], 2)
            pe.wait_ge(S["pos_ready"], 4)
            gates(0, 0, first=True, reads_before=False)
            transposes(1)
            pe.wait_ge(S["ld_membg"], 16)
            memory_rows(0, 0, first=True)
            first_pass(1, 1, reads_before=False)
            first_pass(2, 0)
            first_pass(3, 1)
            with pe.Fori(2, NG // 2 - 1) as i:
                for k in range(2):
                    first_pass(2 * i + k, k)
            first_pass(NG - 2, 0)
            first_pass(NG - 1, 1, last=True)
            pe.wait_ge(S["step_done"], 8 * (NG - 1))
            writes(NG - 1)
            pe.wait_ge(S["weights_ready"], len(SECOND_WEIGHTS))
            pe.wait_ge(S["x_ready"], 2 * NG)
            mix_gates(0, second=2)
            reads_can_start(NG - 2)
            reads(NG - 2, 0)
            mix(0, second=2)
            reads_can_start(NG - 1)
            reads(NG - 1, 1)
            pe.wait_ge(S["step_done"], 8 * NG)
            mix_gates(1)
            transposes(NG)
            ffn_in(0, 0, 0)
            second_pass(0, 0)
            second_pass(1, 1)
            with pe.Fori(1, NG // 2 - 1) as i:
                for k in range(2):
                    second_pass(2 * i + k, k)
            second_pass(NG - 2, 0, ahead=1)
            second_pass(NG - 1, 1, ahead=0)


PARTS = [[(half, t, stage, k) for t in range(NT) for stage in range(3) for k in range(1, TAPS)] for half in range(2)]
FIRST_GROUPS, FIRST_SLOTS = B - 2, 4
TURN = (1, 4, 2, 1, 1)
SECOND_SLOTS, SECOND_ALL = NC, 35


def is_last(half, t, stage, k):
    return k == TAPS - 1


def spread(parts, slots, slot):
    return [part for n, part in enumerate(parts) if n * slots // len(parts) == slot]


def parts_in(g, slot):
    if g < NG:
        return spread(PARTS[0], FIRST_GROUPS * FIRST_SLOTS, FIRST_SLOTS * (g - B) + slot)
    return spread(PARTS[1][sum(TURN):], SECOND_ALL, SECOND_SLOTS * (g - NG) + slot)


def turn_parts(slot):
    at = sum(TURN[:slot])
    return PARTS[1][at:at + TURN[slot]]


def parts_of(g):
    if not B <= g < NG + B:
        return []
    slots = range(FIRST_SLOTS if g < NG else SECOND_SLOTS)
    turn = [part for slot in range(len(TURN)) for part in turn_parts(slot)] if g == NG else []
    return turn + [part for slot in slots for part in parts_in(g, slot)]


def finished_in(g):
    return [part[:2] for part in parts_of(g - 1 if g < NG else g) if part[2] == 2 and is_last(*part)]


_IN_ORDER = ["x", "tok", "posT", "pos_tab", "carryT", "conv", "memq", "memk", "memv", "memo", "memg", "membg", "gateT",
             "router_b", "mixgT", "mixg_b", "mixT", "mix_b", "finT", "fin_b", "fout", "digits", "ident", "mask"]


def _layout(i):
    import numpy as np

    def order(a, axis):
        parts = np.split(a, NH, axis=axis)
        return np.concatenate([parts[h] for h in ORDER], axis=axis)

    gate = np.asarray(i["L0_attn_gate_w"])
    xg, gt = order(gate[0:C], 0), order(gate[C:2 * C], 0)
    router = np.asarray(i["L0_attn_router_w"])[ORDER]
    mixg = order(order(np.asarray(i["L0_attn_mixg_w"]), 0), 1)
    conv_w = np.asarray(i["L0_attn_conv_w"])[ORDER].transpose(2, 0, 1, 3).reshape(HD, -1)
    conv_b = np.asarray(i["L0_attn_conv_b"])[ORDER].transpose(2, 0, 1).reshape(HD, -1)
    wq, wk, wv, wo = (np.asarray(i[f"L0_attn_mem_W{n}"]) for n in ("q", "k", "v", "out"))
    u = T - 1 - np.arange(T)
    digits = np.zeros((DIGIT_ROWS, T), np.float32)
    for d in range(3):
        digits[DIGIT_AT * d:DIGIT_AT * d + HD] = np.arange(HD)[:, None] == (u // HD ** d % HD)[None, :]
    pos_tab = np.zeros((DIGIT_ROWS, C), np.float32)
    pos_tab[0:HD] = np.asarray(i["L0_tok_pos_table"])
    lane = np.arange(C2) // HD
    return {
        "x": np.asarray(i["x"]),
        "tok": np.asarray(i["L0_tok_tok_table"]),
        "posT": np.asarray(i["L0_tok_pos_table"]).T,
        "pos_tab": pos_tab,
        "carryT": np.asarray(i["L0_tok_carry_W"]).T,
        "conv": np.concatenate([conv_w, conv_b], axis=1),
        "memq": wq.transpose(1, 0, 2).reshape(HD, C2),
        "memk": wk.transpose(1, 0, 2).reshape(HD, C2),
        "memv": wv.transpose(1, 0, 2).reshape(P, C2),
        "memo": wo.transpose(2, 0, 1).reshape(P, C2),
        "memg": np.asarray(i["L0_attn_mem_Wg_w"]).reshape(C2, 1),
        "membg": np.repeat(np.asarray(i["L0_attn_mem_Wg_b"]).reshape(1, NM), HD, axis=1),
        "gateT": np.concatenate([xg[0:P], gt[0:P], xg[P:C], gt[P:C], router], axis=0).T,
        "router_b": np.asarray(i["L0_attn_router_b"])[ORDER].reshape(NH, 1),
        "mixgT": mixg.T,
        "mixg_b": order(np.asarray(i["L0_attn_mixg_b"]), 0).reshape(C, 1),
        "mixT": order(np.asarray(i["L0_attn_mix_w"]), 1).T,
        "mix_b": np.asarray(i["L0_attn_mix_b"]),
        "finT": np.asarray(i["L0_ffn_in_weight"]).T,
        "fin_b": np.asarray(i["L0_ffn_in_bias"]).reshape(NC, P).T,
        "fout": np.asarray(i["L0_ffn_out_weight"]),
        "digits": digits,
        "ident": np.eye(P, dtype=np.float32),
        "mask": (lane[:, None] == lane[None, :]).astype(np.float32),
    }


def kernel(**inputs):
    import numpy as np
    import concourse.bacc as bacc
    from concourse.bass_utils import run_bass_kernel_spmd as run

    nc = bacc.Bacc("TRN2", target_bir_lowering=False, num_devices=1)
    operands = _layout(inputs)
    arrays, args = {}, []
    for name in _IN_ORDER:
        a = np.ascontiguousarray(operands[name])
        arrays[f"in_{name}"] = a
        args.append(nc.dram_tensor(f"in_{name}", a.shape, mybir.dt.from_np(a.dtype), kind="ExternalInput").ap())
    args.append(nc.dram_tensor("out_h", (B, T, C), F32, kind="ExternalOutput").ap())
    lm_tower(nc, *args)
    r = run(nc, [arrays], core_ids=[0])
    return r.results[0]["out_h"]
```
